# Optimizing a Trainium2 kernel written in Bass

```python
import numpy as np
import jax
import jax.numpy as jnp

def _softmax(x, axis=-1):
    return jax.nn.softmax(x, axis=axis)

def _gelu(x):
    return jax.nn.gelu(x, approximate=True)

def _silu(x):
    return jax.nn.silu(x)

def _sigmoid(x):
    return jax.nn.sigmoid(x)

def _layernorm(x, axis=-1, eps=1e-05):
    m = jnp.mean(x, axis=axis, keepdims=True)
    v = jnp.var(x, axis=axis, keepdims=True)
    return (x - m) / jnp.sqrt(v + eps)

def _scatter_add(tgt, idx, src, axis=0):
    return tgt.at[idx].add(src)

def _segment_sum(src, seg, n):
    return jax.ops.segment_sum(src, seg, n)
kernel_name = 'mk_vit_tower_d2_tok_img1024_r4_edd121'

def setup_inputs(seed: int=0):
    np.random.seed(seed)
    _w = jnp.asarray

    def _rec_inputs():
        import jax
        import jax.numpy as jnp
        _rk = jax.random.key(seed)
        x = -4.65018e-05 + 0.999886 * jax.random.normal(jax.random.fold_in(_rk, 1), (16, 3, 112, 112), jnp.float32)
        return x
    x = _rec_inputs()

    def _L0_tok_setup():
        import jax, jax.numpy as jnp
        import numpy as np
        P = 16
        key = jax.random.key(seed)
        k1, k2, k3 = jax.random.split(key, 3)
        B, C, H, W_ = (64, 3, 128, 128)
        D = 256
        x = jax.random.normal(k1, (B, C, H, W_), dtype=jnp.float32)
        W = jax.random.normal(k2, (C * P * P, D), dtype=jnp.float32) * (1.0 / np.sqrt(C * P * P))
        b = jax.random.normal(k3, (D,), dtype=jnp.float32) * 0.01
        return {'x': x, 'W': W, 'b': b}
    _L0_tok_all = _L0_tok_setup()
    _L0_tok_in = {k: v for k, v in _L0_tok_all.items() if k in ('W', 'b')}
    del _L0_tok_all

    def _L0_attn_setup():
        import math
        import jax, jax.numpy as jnp
        import numpy as np
        D_MODEL = 256
        N_HEADS = 16
        D_K = D_MODEL // N_HEADS
        THETA = 10000.0

        def _rope(t, cos, sin):
            B, H, S, d = t.shape
            tp = t.reshape(B, H, S, d // 2, 2)
            even, odd = (tp[..., 0], tp[..., 1])
            r_even = even * cos - odd * sin
            r_odd = even * sin + odd * cos
            return jnp.stack([r_even, r_odd], axis=-1).reshape(B, H, S, d)
        key = jax.random.key(seed)
        k1, k2, k3 = jax.random.split(key, 3)
        B, S = (2, 512)
        x = jax.random.normal(k1, (B, S, D_MODEL), dtype=jnp.float32)
        std_qkv = math.sqrt(2.0 / (D_MODEL + 3 * D_MODEL))
        std_out = math.sqrt(2.0 / (D_MODEL + D_MODEL))
        w_qkv = jnp.clip(jax.random.normal(k2, (3 * D_MODEL, D_MODEL), dtype=jnp.float32) * std_qkv, -3 * std_qkv, 3 * std_qkv)
        b_qkv = jnp.zeros((3 * D_MODEL,), dtype=jnp.float32)
        w_out = jnp.clip(jax.random.normal(k3, (D_MODEL, D_MODEL), dtype=jnp.float32) * std_out, -3 * std_out, 3 * std_out)
        b_out = jnp.zeros((D_MODEL,), dtype=jnp.float32)
        return {'x': x, 'w_qkv': w_qkv, 'b_qkv': b_qkv, 'w_out': w_out, 'b_out': b_out}
    _L0_attn_all = _L0_attn_setup()
    _L0_attn_in = {k: v for k, v in _L0_attn_all.items() if k in ('w_qkv', 'b_qkv', 'w_out', 'b_out')}
    del _L0_attn_all

    def _L0_ffn_setup():
        import jax, jax.numpy as jnp
        import numpy as np
        TOP_K = 8
        NUM_EXPERTS = 32
        CAPACITY = 256
        key = jax.random.key(seed)
        k1, k2, k3, k4 = jax.random.split(key, 4)
        B, S, H, E, F = (2, 256, 256, NUM_EXPERTS, 192)
        return {'hidden_states': jax.random.normal(k1, (B, S, H), dtype=jnp.float32), 'gate_weight': jax.random.normal(k2, (E, H), dtype=jnp.float32) * 0.02, 'gate_up_proj': jax.random.normal(k3, (E, 2 * F, H), dtype=jnp.float32) * 0.02, 'down_proj': jax.random.normal(k4, (E, H, F), dtype=jnp.float32) * 0.02}
    _L0_ffn_all = _L0_ffn_setup()
    _L0_ffn_in = {k: v for k, v in _L0_ffn_all.items() if k in ('gate_weight', 'gate_up_proj', 'down_proj')}
    del _L0_ffn_all

    def _L1_attn_setup():
        import jax, jax.numpy as jnp
        import numpy as np
        LN_EPS = 1e-05
        NUM_HEAD = 16
        key = jax.random.key(seed)
        ks = jax.random.split(key, 10)
        B, S, E = (2, 512, 256)
        sc = 0.02
        return {'x': jax.random.normal(ks[0], (B, S, E), jnp.float32), 'wq': jax.random.normal(ks[1], (E, E), jnp.float32) * sc, 'bq': jax.random.normal(ks[2], (E,), jnp.float32) * sc, 'wk': jax.random.normal(ks[3], (E, E), jnp.float32) * sc, 'bk': jax.random.normal(ks[4], (E,), jnp.float32) * sc, 'wv': jax.random.normal(ks[5], (E, E), jnp.float32) * sc, 'bv': jax.random.normal(ks[6], (E,), jnp.float32) * sc, 'wo': jax.random.normal(ks[7], (E, E), jnp.float32) * sc, 'bo': jax.random.normal(ks[8], (E,), jnp.float32) * sc, 'gamma': jnp.ones((E,), jnp.float32), 'beta': jnp.zeros((E,), jnp.float32)}
    _L1_attn_all = _L1_attn_setup()
    _L1_attn_in = {k: v for k, v in _L1_attn_all.items() if k in ('wq', 'bq', 'wk', 'bk', 'wv', 'bv', 'wo', 'bo', 'gamma', 'beta')}
    del _L1_attn_all

    def _L1_ffn_setup():
        import jax, jax.numpy as jnp
        import numpy as np
        B, S, H = (2, 1024, 256)
        I = 128
        E = 8
        TOPK = 2
        NGROUP = 2
        TOPK_GROUP = 1
        ROUTED_SCALE = 1.0

        def _silu(x):
            return x * jax.nn.sigmoid(x)
        key = jax.random.key(seed)
        ks = jax.random.split(key, 9)

        def w(k, shape, s=0.05):
            return jax.random.normal(k, shape, dtype=jnp.float32) * s
        return {'hidden_states': jax.random.normal(ks[0], (B, S, H), dtype=jnp.float32), 'router_weight': w(ks[1], (E, H)), 'correction_bias': w(ks[2], (E,)), 'w_gate': w(ks[3], (E, H, I)), 'w_up': w(ks[4], (E, H, I)), 'w_down': w(ks[5], (E, I, H)), 'sw_gate': w(ks[6], (H, I)), 'sw_up': w(ks[7], (H, I)), 'sw_down': w(ks[8], (I, H))}
    _L1_ffn_all = _L1_ffn_setup()
    _L1_ffn_in = {k: v for k, v in _L1_ffn_all.items() if k in ('router_weight', 'correction_bias', 'w_gate', 'w_up', 'w_down', 'sw_gate', 'sw_up', 'sw_down')}
    del _L1_ffn_all
    return {'x': x, 'L0_tok_W': _L0_tok_in['W'], 'L0_tok_b': _L0_tok_in['b'], 'L0_attn_w_qkv': _L0_attn_in['w_qkv'], 'L0_attn_b_qkv': _L0_attn_in['b_qkv'], 'L0_attn_w_out': _L0_attn_in['w_out'], 'L0_attn_b_out': _L0_attn_in['b_out'], 'L0_ffn_gate_weight': _L0_ffn_in['gate_weight'], 'L0_ffn_gate_up_proj': _L0_ffn_in['gate_up_proj'], 'L0_ffn_down_proj': _L0_ffn_in['down_proj'], 'L1_attn_wq': _L1_attn_in['wq'], 'L1_attn_bq': _L1_attn_in['bq'], 'L1_attn_wk': _L1_attn_in['wk'], 'L1_attn_bk': _L1_attn_in['bk'], 'L1_attn_wv': _L1_attn_in['wv'], 'L1_attn_bv': _L1_attn_in['bv'], 'L1_attn_wo': _L1_attn_in['wo'], 'L1_attn_bo': _L1_attn_in['bo'], 'L1_attn_gamma': _L1_attn_in['gamma'], 'L1_attn_beta': _L1_attn_in['beta'], 'L1_ffn_router_weight': _L1_ffn_in['router_weight'], 'L1_ffn_correction_bias': _L1_ffn_in['correction_bias'], 'L1_ffn_w_gate': _L1_ffn_in['w_gate'], 'L1_ffn_w_up': _L1_ffn_in['w_up'], 'L1_ffn_w_down': _L1_ffn_in['w_down'], 'L1_ffn_sw_gate': _L1_ffn_in['sw_gate'], 'L1_ffn_sw_up': _L1_ffn_in['sw_up'], 'L1_ffn_sw_down': _L1_ffn_in['sw_down']}

def reference(x, L0_tok_W, L0_tok_b, L0_attn_w_qkv, L0_attn_b_qkv, L0_attn_w_out, L0_attn_b_out, L0_ffn_gate_weight, L0_ffn_gate_up_proj, L0_ffn_down_proj, L1_attn_wq, L1_attn_bq, L1_attn_wk, L1_attn_bk, L1_attn_wv, L1_attn_bv, L1_attn_wo, L1_attn_bo, L1_attn_gamma, L1_attn_beta, L1_ffn_router_weight, L1_ffn_correction_bias, L1_ffn_w_gate, L1_ffn_w_up, L1_ffn_w_down, L1_ffn_sw_gate, L1_ffn_sw_up, L1_ffn_sw_down):
    import jax
    import jax.numpy as jnp

    def _L0_tok_ref(x, W, b):
        import jax, jax.numpy as jnp
        import numpy as np
        P = 16
        B, C, H, W_ = x.shape
        nh, nw = (H // P, W_ // P)
        patches = x.reshape(B, C, nh, P, nw, P)
        patches = patches.transpose(0, 2, 4, 1, 3, 5)
        patches = patches.reshape(B, nh * nw, C * P * P)
        return jnp.einsum('bnk,kd->bnd', patches, W) + b

    def _L0_attn_ref(x, w_qkv, b_qkv, w_out, b_out):
        import math
        import jax, jax.numpy as jnp
        import numpy as np
        D_MODEL = 256
        N_HEADS = 16
        D_K = D_MODEL // N_HEADS
        THETA = 10000.0

        def _rope(t, cos, sin):
            B, H, S, d = t.shape
            tp = t.reshape(B, H, S, d // 2, 2)
            even, odd = (tp[..., 0], tp[..., 1])
            r_even = even * cos - odd * sin
            r_odd = even * sin + odd * cos
            return jnp.stack([r_even, r_odd], axis=-1).reshape(B, H, S, d)
        B, S, _ = x.shape
        qkv = jnp.einsum('bsi,oi->bso', x, w_qkv) + b_qkv
        qkv = qkv.reshape(B, S, 3, N_HEADS, D_K).transpose(2, 0, 3, 1, 4)
        q, k, v = (qkv[0], qkv[1], qkv[2])
        inv_freq = THETA ** (-jnp.arange(0, D_K, 2, dtype=jnp.float32) / D_K)
        ang = jnp.arange(S, dtype=jnp.float32)[:, None] * inv_freq[None, :]
        cos, sin = (jnp.cos(ang), jnp.sin(ang))
        q = _rope(q, cos, sin)
        k = _rope(k, cos, sin)
        scale = 1.0 / math.sqrt(D_K)
        scores = jnp.einsum('bhqd,bhkd->bhqk', q.astype(jnp.float32), k.astype(jnp.float32)) * scale
        causal = jnp.tril(jnp.ones((S, S), dtype=bool))
        scores = jnp.where(causal, scores, jnp.finfo(jnp.float32).min)
        ex = jnp.exp(scores - jnp.max(scores, axis=-1, keepdims=True))
        attn = ex / (jnp.sum(ex, axis=-1, keepdims=True) + 1e-08)
        attn = attn.astype(v.dtype)
        o = jnp.einsum('bhqk,bhkd->bhqd', attn, v)
        o = o.transpose(0, 2, 1, 3).reshape(B, S, D_MODEL)
        out = jnp.einsum('bsi,oi->bso', o, w_out) + b_out
        return out

    def _L0_ffn_ref(hidden_states, gate_weight, gate_up_proj, down_proj):
        import jax, jax.numpy as jnp
        import numpy as np
        TOP_K = 8
        NUM_EXPERTS = 32
        CAPACITY = 256
        B, S, H = hidden_states.shape
        E = gate_weight.shape[0]
        N = B * S
        x = hidden_states.reshape(N, H)
        logits = x @ gate_weight.T
        probs = jax.nn.softmax(logits.astype(jnp.float32), axis=-1)
        topw, topi = jax.lax.top_k(probs, TOP_K)
        topw = topw / topw.sum(-1, keepdims=True)
        topw = topw.astype(x.dtype)
        flat_e = topi.reshape(-1)
        flat_w = topw.reshape(-1)
        flat_x = jnp.repeat(x, TOP_K, axis=0)
        oh = jax.nn.one_hot(flat_e, E, dtype=jnp.int32)
        pos = (jnp.cumsum(oh, axis=0) * oh).sum(-1) - 1
        buf = jnp.zeros((E, CAPACITY, H), x.dtype).at[flat_e, pos].set(flat_x, mode='drop')
        gu = jnp.einsum('ech,efh->ecf', buf, gate_up_proj)
        gate, up = jnp.split(gu, 2, axis=-1)
        h = jax.nn.silu(gate) * up
        eo = jnp.einsum('ecf,ehf->ech', h, down_proj)
        tok_out = eo.at[flat_e, pos].get(mode='fill', fill_value=0)
        out = (tok_out * flat_w[:, None]).reshape(N, TOP_K, H).sum(1)
        return out.reshape(B, S, H)

    def _L1_attn_ref(x, wq, bq, wk, bk, wv, bv, wo, bo, gamma, beta):
        import jax, jax.numpy as jnp
        import numpy as np
        LN_EPS = 1e-05
        NUM_HEAD = 16
        B, S, E = x.shape
        H = NUM_HEAD
        D = E // H
        Q = x @ wq + bq
        K = x @ wk + bk
        V = x @ wv + bv
        Q = Q.reshape(B * H, S, D)
        K = K.reshape(B * H, S, D)
        V = V.reshape(B * H, S, D)
        scores = jnp.einsum('bqd,bkd->bqk', Q, K) / jnp.sqrt(jnp.float32(D))
        attn = jax.nn.softmax(scores, axis=-1)
        ctx = jnp.einsum('bqk,bkd->bqd', attn, V)
        ctx = ctx.reshape(B, S, E)
        out = ctx @ wo + bo
        out = out + x
        mu = jnp.mean(out, axis=-1, keepdims=True)
        var = jnp.var(out, axis=-1, keepdims=True)
        out = (out - mu) * jax.lax.rsqrt(var + LN_EPS) * gamma + beta
        return out

    def _L1_ffn_ref(hidden_states, router_weight, correction_bias, w_gate, w_up, w_down, sw_gate, sw_up, sw_down):
        import jax, jax.numpy as jnp
        import numpy as np
        B, S, H = (2, 1024, 256)
        I = 128
        E = 8
        TOPK = 2
        NGROUP = 2
        TOPK_GROUP = 1
        ROUTED_SCALE = 1.0

        def _silu(x):
            return x * jax.nn.sigmoid(x)
        b, s, h = hidden_states.shape
        x = hidden_states.reshape(-1, h)
        logits = x @ router_weight.T
        scores = jax.nn.sigmoid(logits)
        scores_for_choice = scores + correction_bias[None, :]
        e_per_g = E // NGROUP
        group_scores = jax.lax.top_k(scores_for_choice.reshape(-1, NGROUP, e_per_g), 2)[0].sum(-1)
        group_idx = jax.lax.top_k(group_scores, TOPK_GROUP)[1]
        group_mask = jax.nn.one_hot(group_idx, NGROUP, dtype=scores.dtype).sum(1)
        score_mask = jnp.repeat(group_mask, e_per_g, axis=1)
        masked = jnp.where(score_mask > 0, scores_for_choice, 0.0)
        topk_idx = jax.lax.top_k(masked, TOPK)[1]
        topk_w = jnp.take_along_axis(scores, topk_idx, axis=1)
        topk_w = topk_w / (topk_w.sum(-1, keepdims=True) + 1e-20)
        topk_w = topk_w * ROUTED_SCALE
        comb = (jax.nn.one_hot(topk_idx, E, dtype=x.dtype) * topk_w[..., None]).sum(1)
        g = jnp.einsum('th,ehi->tei', x, w_gate)
        u = jnp.einsum('th,ehi->tei', x, w_up)
        y = jnp.einsum('tei,eih->teh', _silu(g) * u, w_down)
        routed = jnp.einsum('teh,te->th', y, comb).reshape(b, s, h)
        shared = _silu(hidden_states @ sw_gate) * (hidden_states @ sw_up) @ sw_down
        return routed + shared
    h = _L0_tok_ref(x, L0_tok_W, L0_tok_b)
    h = h + _L0_attn_ref(_layernorm(h, axis=-1), L0_attn_w_qkv, L0_attn_b_qkv, L0_attn_w_out, L0_attn_b_out)
    h = h + _L0_ffn_ref(_layernorm(h, axis=-1), L0_ffn_gate_weight, L0_ffn_gate_up_proj, L0_ffn_down_proj)
    h = h + _L1_attn_ref(_layernorm(h, axis=-1), L1_attn_wq, L1_attn_bq, L1_attn_wk, L1_attn_bk, L1_attn_wv, L1_attn_bv, L1_attn_wo, L1_attn_bo, L1_attn_gamma, L1_attn_beta)
    h = h + _L1_ffn_ref(_layernorm(h, axis=-1), L1_ffn_router_weight, L1_ffn_correction_bias, L1_ffn_w_gate, L1_ffn_w_up, L1_ffn_w_down, L1_ffn_sw_gate, L1_ffn_sw_up, L1_ffn_sw_down)
    return h

_drawn_inputs = setup_inputs


def setup_inputs(seed=0):
    import zlib

    import numpy as np

    out = dict(_drawn_inputs(seed))
    spreads = {'L0_attn_b_qkv': (0.0, 0.1),
     'L0_attn_b_out': (0.0, 0.1),
     'L1_attn_gamma': (1.0, 0.547),
     'L1_attn_beta': (0.0, 0.526)}
    factors = {'L0_tok_b': 4.203,
     'L0_ffn_gate_weight': 8.0,
     'L0_ffn_gate_up_proj': 8.0,
     'L0_ffn_down_proj': 8.0,
     'L1_attn_wq': 8.0,
     'L1_attn_bq': 8.0,
     'L1_attn_wk': 8.0,
     'L1_attn_bk': 22.69,
     'L1_attn_wv': 6.115,
     'L1_attn_bv': 35.485,
     'L1_attn_wo': 6.253,
     'L1_attn_bo': 38.008,
     'L1_ffn_router_weight': 3.031,
     'L1_ffn_correction_bias': 5.947,
     'L1_ffn_w_gate': 2.752}
    for name, (base, spread) in spreads.items():
        noise = np.random.default_rng([zlib.crc32(name.encode()), seed]).standard_normal(out[name].shape)
        drawn = base * np.exp(spread * noise) if base else spread * noise
        out[name] = jnp.asarray(drawn.astype(out[name].dtype))
    for name, factor in factors.items():
        out[name] = (out[name] * factor).astype(out[name].dtype)
    return out
```

```python
from contextlib import ExitStack

import numpy as np

import concourse.bass as bass
from concourse import mybir

F32 = mybir.dt.float32
BF16 = mybir.dt.bfloat16
I32 = mybir.dt.int32
U32 = mybir.dt.uint32
ALU = mybir.AluOpType
ACT = mybir.ActivationFunctionType
AX = mybir.AxisListType

P = 128
IMAGES, S, D = 16, 49, 256
TOKENS = IMAGES * S
TILES = IMAGES // 2
PAIR = 2 * S
SLOT = 64
PATCH = 768
KP = PATCH // P
KD = D // P
HEADS, HD = 16, 16
HG = HEADS // KD
SCALE = HD ** -0.5
HP = HEADS // 2
VW = 2 * (HD + 1)
EPS = 1e-5

E0, TOP0, CAP, F0 = 32, 8, 256, 192
CT = CAP // P
F0B = F0 - P
ROW = D + 1 + E0
FAR = float(1 << 20)
ACC_ROWS = TOKENS + 1 + P

E1, TOP1, I1 = 8, 2, 128
HALF = TOKENS // 2
HT = TILES // 2

LOOP0_STEPS = 60
LOOP1_STEPS = 34

_AT = {}
_WIDTH = 0
for _name, _w in (("ident", P), ("head_mask", HG), ("causal", S), ("cos", S), ("sin", S), ("earlier", P),
                  ("valid", P), ("pad_far", 1), ("slot_base", E0), ("iota", E0), ("token", 1),
                  ("empty_row", 1), ("eps", 1)):
    _AT[_name] = (_WIDTH, _WIDTH + _w)
    _WIDTH += _w


def constants():
    c = np.zeros((P, _WIDTH), np.float32)

    def put(name, a):
        lo, hi = _AT[name]
        c[:, lo:hi] = a

    p = np.arange(P)
    pos, valid = p % SLOT, (p % SLOT) < S
    put("ident", np.eye(P))
    put("head_mask", (p[:, None] // HD) == np.arange(HG)[None, :])
    put("causal", np.where(np.arange(S)[None, :] <= pos[:, None], 0.0, -1e30))
    freq = (np.float32(10000.0) ** (-np.arange(0, HD, 2, dtype=np.float32) / np.float32(HD))).astype(np.float32)
    ang = np.arange(S, dtype=np.float32)[None, :] * freq[(p % HD) // 2][:, None]
    put("cos", np.cos(ang))
    put("sin", np.sin(ang) * np.where(p % 2 == 0, -1.0, 1.0)[:, None])
    put("earlier", valid[:, None] & (p[:, None] < p[None, :]))
    put("valid", np.repeat(valid[:, None], P, axis=1))
    put("pad_far", np.where(valid, 0.0, FAR)[:, None])
    put("slot_base", CAP * np.arange(E0)[None, :])
    put("iota", np.arange(E0)[None, :])
    put("token", (pos + S * (p // SLOT) + 1)[:, None])
    put("empty_row", (TOKENS + 1 + p)[:, None])
    put("eps", EPS)
    return c


class Steps:

    def __init__(self, eng, sem):
        self.eng, self.sem, self.total = eng, sem, 0
        self.base, self.n = 0, 0

    def begin(self, i, per_pass):
        self.total += self.n
        self.base, self.n, self.per_pass = self.total + i * per_pass, 0, per_pass

    def end(self, passes):
        assert self.n == self.per_pass, f"{self.n} steps in a pass"
        self.total += passes * self.n
        self.base, self.n = self.total, 0

    def do(self, instruction):
        self.mark(instruction)
        self.wait()

    def mark(self, instruction):
        instruction.then_inc(self.sem, 1)
        self.n += 1

    def wait(self):
        self.eng.wait_ge(self.sem, self.base + self.n)


def vit_tower(nc, dram, out):
    ctx = ExitStack()
    with ctx:
        def sb(name, shape, dt=F32):
            return ctx.enter_context(nc.sbuf_tensor(name, shape, dt))

        def two(name, shape, dt=F32):
            return [sb(f"{name}{u}", shape, dt) for u in range(2)]

        def sem(name):
            return ctx.enter_context(nc.semaphore(name))

        def sem2(name):
            return [sem(f"{name}{u}") for u in range(2)]

        def cols(name):
            lo, hi = _AT[name]
            return const[:, lo:hi]

        def spread(ap, n):
            return ap.unsqueeze(1).to_broadcast([ap.shape[0], n] + list(ap.shape[1:]))

        def repeat(ap, n):
            return ap.unsqueeze(len(ap.shape)).to_broadcast(list(ap.shape) + [n])

        table = nc.dram_tensor("expert_rows", [E0 * CAP, ROW], F32, kind="Internal").ap()
        acc = [nc.dram_tensor(f"expert_sums{c}", [ACC_ROWS, D], F32, kind="Internal").ap() for c in range(CT)]
        qkv_flat = nc.dram_tensor("qkv_flat", [3, TOKENS, D], F32, kind="Internal").ap()
        ctx_flat = nc.dram_tensor("ctx_flat", [TOKENS, D], F32, kind="Internal").ap()
        comb_flat = nc.dram_tensor("comb_flat", [E1 * TILES, 2, S], F32, kind="Internal").ap()

        const = sb("const", [P, _WIDTH])
        count_earlier = sb("count_earlier", [P, P], BF16)
        count_valid = sb("count_valid", [P, P], BF16)
        zeros = sb("zeros", [P, 2 * ROW])
        tok_w = sb("tok_w", [P, KP, D])
        tok_b = sb("tok_b", [P, D])
        wqk = sb("wqk", [P, KD, 4 * D])
        rope_b = sb("rope_b", [P, 8])
        rope_bias = sb("rope_bias", [P, 4, S])
        wv = sb("wv", [P, KD, D])
        bv = sb("bv", [P, D])
        wo = sb("wo", [P, KD, D])
        bo = sb("bo", [P, D])
        gate_w = sb("gate_w", [P, KD, E0])
        wqkv1 = sb("wqkv1", [P, KD, 3 * D])
        bqkv1 = sb("bqkv1", [P, 3 * D])
        wo1 = sb("wo1", [P, KD, D])
        bo1 = sb("bo1", [P, D])
        gamma = sb("gamma", [P, D])
        beta = sb("beta", [P, D])
        router_w = sb("router_w", [P, KD, E1])
        corr = sb("corr", [P, E1])
        H = sb("H", [P, TILES, D])
        taken = sb("taken", [P, E0], BF16)
        patches = two("patches", [P, KP * PAIR + 16])
        stats = two("stats", [P, 6])
        moments = two("moments", [P, 2])
        dev = two("dev", [P, 1])
        rstd = two("rstd", [P, 1])
        N = two("N", [P, D])
        NT = two("NT", [P, KD, P])
        room = sb("room", [P, E1 * TOKENS])
        room_used = 0

        def in_room(pattern, *dims, **sizes):
            nonlocal room_used
            lo, n = room_used, int(np.prod(dims))
            room_used += n
            return room[:, lo:lo + n].rearrange(pattern, **sizes)

        rope_a = [in_room("p (m x) -> p m x", 4, 2 * S, m=4) for _ in range(2)]
        rope_s = [in_room("p (m x) -> p m x", 4, 2 * S, m=4) for _ in range(2)]
        KB = [in_room("p (m h k) -> p m h k", 4, HG, S, m=4, h=HG) for _ in range(2)]
        SM = [in_room("p (h k) -> p h k", HEADS, S, h=HEADS) for _ in range(2)]
        comb_b = room
        QK = two("QK", [P, 4, 2, SLOT])
        VB = two("VB", [P, 2, HP, VW])
        top = two("top", [P, HEADS])
        PR = two("PR", [P, HEADS, SLOT])
        PRT = two("PRT", [P, HP, P])
        den = two("den", [P, HEADS])
        rden = two("rden", [P, HEADS])
        CX = two("CX", [P, HEADS, HD])
        CXT = two("CXT", [P, KD, P])
        row = two("row", [P, ROW])
        r_neg = two("r_neg", [P, 1])
        r_top = two("r_top", [P, TOP0])
        r_exp = two("r_exp", [P, E0])
        r_sum = two("r_sum", [P, 1])
        r_inv = two("r_inv", [P, 1])
        r_prob = two("r_prob", [P, E0])
        r_left = two("r_left", [P, E0])
        r_index = two("r_index", [P, TOP0], U32)
        r_expert = two("r_expert", [P, TOP0])
        r_mask = two("r_mask", [P, E0], BF16)
        r_over = two("r_over", [P, E0])
        r_slots = two("r_slots", [P, E0])
        r_pick = two("r_pick", [P, TOP0, E0])
        r_slot = two("r_slot", [P, TOP0])
        slot = two("slot", [P, TOP0], I32)
        xrows = two("xrows", [P, CT, ROW])
        gu_w = two("gu_w", [P, KD, 2 * F0])
        dn_w = two("dn_w", [P, 2, D])
        xT = two("xT", [P, KD, CAP])
        silu_a = two("silu_a", [P, CAP])
        silu_b = two("silu_b", [P, CAP])
        hid_a = two("hid_a", [P, CAP])
        hid_b = two("hid_b", [P, CAP])
        y_rows = two("y_rows", [P, CT, D])
        dest_f = two("dest_f", [P, CT])
        dest = two("dest", [P, CT], I32)
        sums = two("sums", [P, CT, D])
        QKV = two("QKV", [P, 3, D])
        headQ = two("headQ", [P, 2, D])
        rows1 = two("rows1", [P, D])
        Z = two("Z", [P, D])
        N3T = sb("N3T", [P, KD, TOKENS])
        logits1 = sb("logits1", [P, TILES, E1])
        wgu1 = two("wgu1", [P, KD, 2 * I1])
        wd1 = two("wd1", [P, D])
        comb_T = sb("comb_T", [E1 * TILES, P])
        sig1 = sb("sig1", [P, TILES, E1])
        choice = sb("choice", [P, TILES, E1])
        pair_hi = sb("pair_hi", [P, 2 * TILES, 2])
        pair_lo = sb("pair_lo", [P, 2 * TILES, 2])
        best = sb("best", [P, 2 * TILES, 1])
        second_a = sb("second_a", [P, 2 * TILES, 1])
        second_b = sb("second_b", [P, 2 * TILES, 1])
        group_sel = sb("group_sel", [P, TILES, 2])
        sorted1 = sb("sorted1", [P, TILES, E1])
        index1 = sb("index1", [P, TILES, E1], U32)
        index1f = sb("index1f", [P, TILES, TOP1])
        picks1 = sb("picks1", [P, TILES, TOP1, E1])
        picked1 = sb("picked1", [P, TILES, TOP1, E1])
        weight1 = sb("weight1", [P, TILES, TOP1])
        total1 = sb("total1", [P, TILES])
        comb1 = sb("comb1", [P, E1, TILES])
        silu1 = two("silu1", [P, HALF])
        hid1 = two("hid1", [P, HT, 2, SLOT])

        psum = ctx.enter_context(nc.psum_tensor("psum", [P, 8, 512], F32))

        def bank(u, b):
            return psum[:, 4 * u + b, :]

        def scores(u):
            return psum[:, 4 * u + 2:4 * u + 4, :]

        small_loaded = sem("small_loaded")
        late_loaded = sem("late_loaded")
        vec_setup = sem("vector_setup")
        pool_setup = sem("pool_setup")
        patches_loaded = sem2("patches_loaded")
        vec = sem("vector_steps")
        act_step = sem("scalar_steps")
        pool_step = sem("pool_steps")
        passed = sem("passed_wait")
        embedded = sem("embedded")
        var_ready = sem("var_ready")
        dev_ready = sem("dev_ready")
        normed = sem("normed")
        transposed = sem("transposed")
        NT_ready = sem("NT_ready")
        bias_added = sem("bias_added")
        qk_ready = sem("qk_ready")
        v_ready = sem("v_ready")
        kb_ready = sem("kb_ready")
        vb_ready = sem("vb_ready")
        scored = sem("scored")
        shifted = sem("shifted")
        exped = sem("exped")
        prt_psum = sem("probs_transposed")
        prt_ready = sem("prt_ready")
        attended = sem("attended")
        cx_ready = sem("cx_ready")
        cx_transposed = sem("cx_transposed")
        cxt_ready = sem("cxt_ready")
        projected = sem("projected")
        var2_ready = sem("var2_ready")
        dev2_ready = sem("dev2_ready")
        normed2 = sem("normed2")
        transposed2 = sem("transposed2")
        NT2_ready = sem("NT2_ready")
        routed = sem("router_logits")
        neg_ready = sem("neg_ready")
        rexp_ready = sem("rexp_ready")
        mask_ready = sem("mask_ready")
        taken_ready = sem("taken_ready")
        counted = sem("counted")
        slots_ready = sem("slots_ready")
        scattered = sem2("scattered")
        rows_loaded = sem2("rows_loaded")
        ew_loaded = sem2("expert_weights_loaded")
        rows_transposed = sem("rows_transposed")
        xT_ready = sem("xT_ready")
        gu_ready = sem("gate_up_ready")
        silu_ready = sem("silu_ready")
        hid_ready = sem("hidden_ready")
        down_ready = sem("down_ready")
        y_ready = sem("y_ready")
        added = sem2("sums_added")
        sums_loaded = sem2("sums_loaded")
        qkv_ready = sem("qkv_ready")
        qkv_stored = sem2("qkv_stored")
        heads_loaded = sem2("heads_loaded")
        h_transposed = sem("heads_transposed")
        h_ready = sem("heads_ready")
        ctx_stored = sem2("ctx_stored")
        ctx_loaded = sem2("ctx_loaded")
        var3_ready = sem("var3_ready")
        dev3_ready = sem("dev3_ready")
        compacted = sem("compacted")
        logits_ready = sem("logits_ready")
        logits_copied = sem("logits_copied")
        sig_ready = sem("sigmoid_ready")
        comb_ready = sem("comb_ready")
        comb_turned = sem("comb_turned")
        comb_copied = sem("comb_copied")
        comb_stored = sem("comb_stored")
        comb_loaded = sem("comb_loaded")
        w1_loaded = sem2("w1_loaded")
        gu1_ready = sem("gate_up1_ready")
        silu1_ready = sem("silu1_ready")
        hid1_ready = sem("hidden1_ready")
        down1_done = sem("down1_done")
        final_ready = sem("final_ready")
        out_stored = sem("out_stored")

        early = [(const[:], dram["const"]), (tok_w[:], dram["tok_w"]),
                 (tok_b[:], dram["tok_b"].partition_broadcast(P)),
                 (rope_b[:], dram["rope_b"]), (wqk[:], dram["wqk"]), (wv[:], dram["wv"]),
                 (bv[:], dram["bv"].partition_broadcast(P)), (wo[:], dram["wo"]),
                 (bo[:], dram["bo"].partition_broadcast(P)), (gate_w[:], dram["gate_w"])]
        late = [(wqkv1[:], dram["wqkv1"]), (bqkv1[:], dram["bqkv1"].partition_broadcast(P)),
                (wo1[:], dram["wo1"]), (bo1[:], dram["bo1"].partition_broadcast(P)),
                (gamma[:], dram["gamma"].partition_broadcast(P)),
                (beta[:], dram["beta"].partition_broadcast(P)),
                (router_w[:], dram["router_w"]), (corr[:], dram["corr"].partition_broadcast(P))]
    
        def images(ap):
            return [ap[SLOT * i:SLOT * i + S] for i in range(2)]

        def heads_of(which, t, i):
            flat = (ctx_flat if which is None else qkv_flat[which]).rearrange("t (c d) -> (t c) d", d=HD)
            return flat[bass.ds((t * 2 + i) * S * HEADS, S * HEADS), :].rearrange("(j q) d -> q j d", q=S)

        block = ctx.enter_context(nc.Block())

        @block.sync
        def _(sp):
            def load_patches(t, u):
                sp.dma_start(patches[u][:, 0:KP * PAIR],
                             dram["patches"][bass.ds(t, 1), :, :].rearrange("o p x -> (o p) x")
                             ).then_inc(patches_loaded[u], 16)

            for dst, src in early[:3]:
                sp.dma_start(dst, src).then_inc(small_loaded, 16)
            for u in range(2):
                load_patches(u, u)
            for dst, src in early[3:]:
                sp.dma_start(dst, src).then_inc(small_loaded, 16)

            def load_expert(e, u):
                sp.dma_start(gu_w[u][:], dram["gu_w"][bass.ds(e, 1), :, :, :].rearrange("o p k n -> (o p) k n")
                             ).then_inc(ew_loaded[u], 16)
                sp.dma_start(dn_w[u][:, 0, :], dram["dn_w"][bass.ds(e, 1), 0:P, :].rearrange("o p n -> (o p) n")
                             ).then_inc(ew_loaded[u], 16)
                sp.dma_start(dn_w[u][P - F0B:P, 1, :],
                             dram["dn_w"][bass.ds(e, 1), P:F0, :].rearrange("o p n -> (o p) n")
                             ).then_inc(ew_loaded[u], 16)

            def load_rows(e, u):
                sp.dma_start(xrows[u][:], table[bass.ds(e * CAP, CAP), :].rearrange("(c p) x -> p c x", p=P)
                             ).then_inc(rows_loaded[u], 16)

            with sp.Fori(0, TILES // 2 - 1) as i:
                for u in range(2):
                    sp.wait_ge(embedded, i * 2 + u + 1)
                    load_patches(i * 2 + u + 2, u)
            for dst, src in late:
                sp.dma_start(dst, src).then_inc(late_loaded, 16)
            for u in range(2):
                load_expert(u, u)
            for u in range(2):
                sp.wait_ge(scattered[u], 16 + 16 * TOP0 * (TILES // 2))
            for u in range(2):
                load_rows(u, u)
            with sp.Fori(0, E0 // 2 - 1) as i:
                for u in range(2):
                    sp.wait_ge(down_ready, i * 2 + u + 1)
                    load_expert(i * 2 + u + 2, u)
                for u in range(2):
                    sp.wait_ge(y_ready, i * 2 + u + 3)
                    load_rows(i * 2 + u + 2, u)

            def load_w1(e, u):
                sp.dma_start(wgu1[u][:], dram["wgu1"][bass.ds(e, 1), :, :, :].rearrange("o p k n -> (o p) k n")
                             ).then_inc(w1_loaded[u], 16)
                sp.dma_start(wd1[u][:], dram["wd1"][bass.ds(e, 1), :, :].rearrange("o p n -> (o p) n")
                             ).then_inc(w1_loaded[u], 16)

            for u in range(2):
                load_w1(u, u)

            def load_sums(t, u):
                for c in range(CT):
                    for im, half in enumerate(images(sums[u])):
                        sp.dma_start(half[:, c, :], acc[c][bass.ds(t * PAIR + S * im + 1, S), :]
                                     ).then_inc(sums_loaded[u], 16)

            sp.wait_ge(pool_setup, 1)
            for c in range(CT):
                sp.wait_ge(added[c], 32 + 16 * E0)
            for u in range(2):
                load_sums(u, u)

            def second(i, last):
                for u in range(2):
                    t = i * 2 + u
                    sp.wait_ge(qkv_ready, t + 1)
                    for im, half in enumerate(images(QKV[u])):
                        sp.dma_start(qkv_flat[:, bass.ds(t * PAIR + S * im, S), :].rearrange("w t f -> t w f"),
                                     half).then_inc(qkv_stored[u], 16)
                    if not last:
                        load_sums(t + 2, u)
                for u in range(2):
                    t = i * 2 + u
                    sp.wait_ge(qkv_stored[u], i * 32 + 32)
                    for w in range(2):
                        for im in range(2):
                            sp.dma_start(images(headQ[u])[im][:, w, :].rearrange("q (j d) -> q j d", d=HD),
                                         heads_of(w, t, im)).then_inc(heads_loaded[u], 16)
                    for im in range(2):
                        both = heads_of(2, t, im).rearrange("q (h o) d -> q o h d", o=2)
                        for o in range(2):
                            sp.dma_start(VB[u][SLOT * o:SLOT * o + S, im, :, (HD + 1) * o:(HD + 1) * o + HD],
                                         both[:, o]).then_inc(heads_loaded[u], 16)
                for u in range(2):
                    t = i * 2 + u
                    sp.wait_ge(cx_ready, TILES + t + 1)
                    for im, half in enumerate(images(CX[u])):
                        sp.dma_start(heads_of(None, t, im), half).then_inc(ctx_stored[u], 16)
                for u in range(2):
                    t = i * 2 + u
                    sp.wait_ge(ctx_stored[u], i * 32 + 32)
                    for im, half in enumerate(images(rows1[u])):
                        sp.dma_start(half, ctx_flat[bass.ds(t * PAIR + S * im, S), :]
                                     ).then_inc(ctx_loaded[u], 16)

            with sp.Fori(0, TILES // 2 - 1) as i:
                second(i, False)
            second(TILES // 2 - 1, True)

            sp.wait_ge(comb_copied, 1)
            for im in range(2):
                sp.dma_start(comb_flat[:, im, :], comb_T[0:E1 * TILES, SLOT * im:SLOT * im + S]
                             ).then_inc(comb_stored, 16)
            sp.wait_ge(comb_stored, 32)
            sp.dma_start(comb_b[:], comb_flat.rearrange("a i q -> (a i q)").partition_broadcast(P)
                         ).then_inc(comb_loaded, 16)
            with sp.Fori(0, (E1 - 2) // 2) as i:
                for u in range(2):
                    sp.wait_ge(down1_done, i * 4 + 2 * u + 2)
                    load_w1(i * 2 + u + 2, u)
            sp.wait_ge(down1_done, 2 * (E1 - 1))
            load_w1(E1, 0)
            sp.wait_ge(final_ready, TILES // 2)
            for im in range(2):
                sp.dma_start(out.rearrange("(t i) q f -> i q t f", i=2)[im],
                             H[SLOT * im:SLOT * im + S, :, :]).then_inc(out_stored, 16)
            sp.wait_ge(out_stored, 32)

        def softmax_vector(ve, steps, k, eps, mask):
            for u in range(2):
                ve.wait_ge(scored, k + u)
                sc = scores(u)[:, :, 0:HG * S].rearrange("p g (h k) -> p g h k", k=S)
                sm = SM[u][:].rearrange("p (g h) k -> p g h k", g=KD)
                mx = top[u][:].rearrange("p (g h) -> p g h", g=KD)
                if mask:
                    causal = cols("causal").unsqueeze(1).unsqueeze(1).to_broadcast([P, KD, HG, S])
                    steps.do(nc.vector.tensor_tensor(sm, sc, causal, ALU.add))
                    sc = sm
                steps.do(nc.vector.tensor_reduce(mx, sc, AX.X, ALU.max))
                nc.vector.tensor_tensor(sm, sc, repeat(mx, S), ALU.subtract).then_inc(shifted, 1)
            for u in range(2):
                ve.wait_ge(attended, k + u)
                o = bank(u, 1)[:, 0:HP * VW].rearrange("p (h x) -> p h x", x=HD + 1)
                total = o[:, :, HD:HD + 1].rearrange("p h x -> p (h x)")
                if eps:
                    steps.do(nc.vector.tensor_scalar(den[u][:], total, 1e-8, None, ALU.add))
                    total = den[u][:]
                steps.do(nc.vector.reciprocal(rden[u][:], total))
                nc.vector.tensor_tensor(CX[u][:], o[:, :, 0:HD], repeat(rden[u][:], HD),
                                        ALU.mult).then_inc(cx_ready, 1)

        def key_blocks(steps, u):
            keys = QK[u][:, 2:4, :, 0:S].rearrange("p g i q -> p (g i) q").unsqueeze(2).to_broadcast([P, 4, HG, S])
            mask = repeat(spread(cols("head_mask"), 4), S)
            return nc.vector.tensor_tensor(KB[u][:], keys, mask, ALU.mult)

        def statistics(steps, src, u, ready):
            steps.eng.sem_inc(passed, 1)
            steps.do(nc.vector.bn_stats(stats[u][:], src))
            steps.eng.sem_inc(passed, 1)
            nc.vector.bn_aggr(moments[u][:], stats[u][:]).then_inc(ready, 1)

        def normalise(ve, steps, dst, src, u, ready, k):
            ve.wait_ge(ready, k + u)
            steps.do(nc.vector.reciprocal(rstd[u][:], dev[u][:]))
            return nc.vector.tensor_scalar(dst, src, moments[u][:, 0:1], rstd[u][:], ALU.subtract, ALU.mult)

        def tile_of(t):
            return H[:, bass.ds(t, 1), :].rearrange("p o f -> p (o f)")

        @block.vector
        def _(ve):
            steps = Steps(ve, vec)
            nc.vector.memset(taken[:], 0.0).then_inc(taken_ready, 1)
            for u in range(2):
                nc.vector.memset(patches[u][:, KP * PAIR:], 0.0)
                nc.vector.memset(QK[u][:], 0.0)
                nc.vector.memset(PR[u][:], 0.0)
                steps.mark(nc.vector.memset(VB[u][:], 0.0))
            steps.wait()
            for u in range(2):
                nc.vector.memset(VB[u][0:SLOT, :, :, HD:HD + 1], 1.0)
                nc.vector.memset(VB[u][SLOT:P, :, :, VW - 1:VW], 1.0)
            ve.wait_ge(small_loaded, 16 * len(early))
            nc.vector.tensor_copy(count_earlier[:], cols("earlier"))
            nc.vector.tensor_copy(count_valid[:], cols("valid"))
            for u in range(2):
                nc.vector.tensor_scalar(row[u][:, D:D + 1], cols("token"), float(PAIR * (u - 2)), None, ALU.add)
            for m in range(4):
                steps.mark(nc.vector.tensor_scalar(rope_bias[:, m, :], cols("cos"), rope_b[:, m:m + 1], None, ALU.mult))
            steps.wait()
            for m in range(4):
                steps.mark(nc.vector.scalar_tensor_tensor(rope_bias[:, m, :], cols("sin"), rope_b[:, 4 + m:5 + m],
                                                          rope_bias[:, m, :], ALU.mult, ALU.add))
            steps.wait()
            ve.sem_inc(y_ready, 2)
            nc.vector.memset(r_left[0][:], 0.0).then_inc(vec_setup, 1)

            with ve.Fori(0, TILES // 2) as i:
                steps.begin(i, LOOP0_STEPS)
                k = i * 2 + 1
                for u in range(2):
                    t = i * 2 + u
                    ve.wait_ge(embedded, k + u)
                    steps.do(nc.vector.tensor_tensor(tile_of(t), bank(u, 0)[:, 0:D], tok_b[:], ALU.add))
                    statistics(steps, tile_of(t), u, var_ready)
                for u in range(2):
                    normalise(ve, steps, N[u][:], tile_of(i * 2 + u), u, dev_ready, k).then_inc(normed, 1)
                for u in range(2):
                    ve.wait_ge(qk_ready, k + u)
                    shape = [P, 8, S]
                    cos, sin = (cols(c).unsqueeze(1).to_broadcast(shape) for c in ("cos", "sin"))
                    flat = [x[u][:].rearrange("p m (i q) -> p (m i) q", i=2) for x in (rope_a, rope_s)]
                    src = [bank(u, b)[:, 0:8 * S].rearrange("p (m q) -> p m q", q=S) for b in (2, 3)]
                    steps.mark(nc.vector.tensor_tensor(flat[0], src[0], cos, ALU.mult))
                    steps.mark(nc.vector.tensor_tensor(flat[1], src[1], sin, ALU.mult))
                    steps.wait()
                    a, r = (x[u][:].rearrange("p m (i q) -> p m i q", i=2) for x in (rope_a, rope_s))
                    bias = rope_bias[:].unsqueeze(2).to_broadcast([P, 4, 2, S])
                    steps.do(nc.vector.tensor_tensor(a, a, bias, ALU.add))
                    steps.do(nc.vector.tensor_tensor(QK[u][:, :, :, 0:S], a, r, ALU.add))
                    key_blocks(steps, u).then_inc(kb_ready, 1)
                    ve.wait_ge(v_ready, k + u)
                    v = bank(u, 0).rearrange("p (i h o d) -> p i h o d", i=2, h=HP, o=2)
                    b = bv[:].rearrange("p (h o d) -> p h o d", h=HP, o=2)
                    for o in range(2):
                        lo, hi = SLOT * o, SLOT * o + SLOT
                        ins = nc.vector.tensor_tensor(VB[u][lo:hi, :, :, (HD + 1) * o:(HD + 1) * o + HD],
                                                      v[lo:hi, :, :, o, :], spread(b[lo:hi, :, o, :], 2), ALU.add)
                    ins.then_inc(vb_ready, 1)
                softmax_vector(ve, steps, k, True, True)
                for u in range(2):
                    t = i * 2 + u
                    ve.wait_ge(projected, k + u)
                    ve.wait_ge(bias_added, k + u)
                    steps.do(nc.vector.tensor_tensor(tile_of(t), bank(u, 1)[:, 0:D], tile_of(t), ALU.add))
                    statistics(steps, tile_of(t), u, var2_ready)
                for u in range(2):
                    ve.wait_ge(scattered[u], i * (16 * TOP0) + 16)
                    nc.vector.tensor_scalar(row[u][:, D:D + 1], row[u][:, D:D + 1], float(2 * PAIR), None, ALU.add)
                    normalise(ve, steps, row[u][:, 0:D], tile_of(i * 2 + u), u, dev2_ready, k).then_inc(normed2, 1)
                for u in range(2):
                    ve.wait_ge(routed, k + u)
                    ve.sem_inc(passed, 1)
                    steps.do(nc.vector.max(r_top[u][:], bank(u, 1)[:, 0:E0]))
                    nc.vector.tensor_scalar(r_neg[u][:], r_top[u][:, 0:1], -1.0, None, ALU.mult).then_inc(neg_ready, 1)
                for u in range(2):
                    ve.wait_ge(rexp_ready, k + u)
                    steps.do(nc.vector.reciprocal(r_inv[u][:], r_sum[u][:]))
                    steps.do(nc.vector.tensor_scalar(r_prob[u][:], r_exp[u][:], r_inv[u][:], None, ALU.mult))
                    ve.sem_inc(passed, 1)
                    steps.do(nc.vector.max(r_top[u][:], r_prob[u][:]))
                    ve.sem_inc(passed, 1)
                    steps.mark(nc.vector.match_replace(r_left[u][:], r_top[u][:], r_prob[u][:], -1.0))
                    steps.mark(nc.vector.max_index(r_index[u][:], r_top[u][:], r_prob[u][:]))
                    steps.do(nc.vector.tensor_reduce(r_sum[u][:], r_top[u][:], AX.X, ALU.add))
                    nc.vector.tensor_scalar(r_mask[u][:], r_left[u][:], 0.0, None, ALU.is_lt).then_inc(mask_ready, 1)
                    steps.mark(nc.vector.tensor_copy(r_expert[u][:], r_index[u][:]))
                    steps.do(nc.vector.reciprocal(r_inv[u][:], r_sum[u][:]))
                    ve.wait_ge(mask_ready, k + u)
                    steps.do(nc.vector.scalar_tensor_tensor(row[u][:, D + 1:ROW], r_mask[u][:], r_inv[u][:],
                                                            r_prob[u][:], ALU.mult, ALU.mult))
                for u in range(2):
                    ve.wait_ge(counted, k + u)
                    nc.vector.tensor_tensor(taken[:], taken[:], r_mask[u][:], ALU.add).then_inc(taken_ready, 1)
                    cnt = bank(u, 2)[:, 0:E0]
                    steps.mark(nc.vector.tensor_scalar(r_over[u][:], cnt, cols("pad_far"), float(CAP), ALU.add, ALU.is_ge))
                    steps.mark(nc.vector.tensor_tensor(r_slots[u][:], cnt, cols("slot_base"), ALU.add))
                    steps.do(nc.vector.tensor_tensor(r_pick[u][:], spread(cols("iota"), TOP0), repeat(r_expert[u][:], E0),
                                                     ALU.is_equal))
                    steps.do(nc.vector.scalar_tensor_tensor(r_slots[u][:], r_over[u][:], FAR, r_slots[u][:],
                                                            ALU.mult, ALU.add))
                    steps.do(nc.vector.tensor_tensor(r_pick[u][:], r_pick[u][:], spread(r_slots[u][:], TOP0), ALU.mult))
                    steps.do(nc.vector.tensor_reduce(r_slot[u][:], r_pick[u][:], AX.X, ALU.add))
                    nc.vector.tensor_copy(slot[u][:], r_slot[u][:]).then_inc(slots_ready, 1)
            steps.end(TILES // 2)

            with ve.Fori(0, E0 // 2) as i:
                steps.begin(i, 2)
                k = i * 2 + 1
                for u in range(2):
                    ve.wait_ge(rows_loaded[u], i * 16 + 16)
                    ids = xrows[u][:, :, D:D + 1].rearrange("p c o -> p (c o)")
                    steps.do(nc.vector.tensor_scalar(dest_f[u][:], ids, 0.0, cols("empty_row"), ALU.is_equal, ALU.mult))
                    ve.wait_ge(added[0], i * 32 + 16 * u + 16)
                    ve.wait_ge(added[1], i * 32 + 16 * u + 16)
                    nc.vector.tensor_tensor(dest[u][:], dest_f[u][:], ids, ALU.add)
                for u in range(2):
                    ve.wait_ge(silu_ready, k + u)
                    nc.vector.tensor_tensor(hid_a[u][:], silu_a[u][:], bank(u, 1)[:, CAP:2 * CAP], ALU.mult)
                    nc.vector.tensor_tensor(hid_b[u][P - F0B:P, :], silu_b[u][P - F0B:P, :],
                                            bank(u, 2)[P - F0B:P, 0:CAP], ALU.mult).then_inc(hid_ready, 1)
                for u in range(2):
                    ve.wait_ge(down_ready, k + u)
                    for c in range(CT):
                        w = xrows[u][:, c, bass.ds(i * 2 + (u + D + 1), 1)]
                        ins = nc.vector.tensor_scalar(y_rows[u][:, c, :], bank(u, 3)[:, c * D:(c + 1) * D], w, None,
                                                      ALU.mult)
                    ins.then_inc(y_ready, 1)
            steps.end(E0 // 2)

            with ve.Fori(0, TILES // 2) as i:
                steps.begin(i, LOOP1_STEPS)
                k = i * 2 + (TILES + 1)
                for u in range(2):
                    t = i * 2 + u
                    ve.wait_ge(sums_loaded[u], i * (32 * CT) + 32 * CT)
                    for c in range(CT):
                        steps.do(nc.vector.tensor_tensor(tile_of(t), tile_of(t), sums[u][:, c, :], ALU.add))
                    statistics(steps, tile_of(t), u, var_ready)
                for u in range(2):
                    normalise(ve, steps, N[u][:], tile_of(i * 2 + u), u, dev_ready, k).then_inc(normed, 1)
                for u in range(2):
                    ve.wait_ge(qk_ready, k + u)
                    nc.vector.tensor_tensor(QKV[u][:, 0:2, :].rearrange("p w f -> p (w f)"), bank(u, 2),
                                            bqkv1[:, 0:2 * D], ALU.add)
                    nc.vector.tensor_tensor(QKV[u][:, 2, :], bank(u, 3)[:, 0:D], bqkv1[:, 2 * D:3 * D],
                                            ALU.add).then_inc(qkv_ready, 1)
                for u in range(2):
                    ve.wait_ge(h_ready, i * 2 + u + 1)
                    key_blocks(steps, u).then_inc(kb_ready, 1)
                softmax_vector(ve, steps, k, False, False)
                for u in range(2):
                    ve.wait_ge(projected, k + u)
                    steps.do(nc.vector.tensor_tensor(Z[u][:], bank(u, 1)[:, 0:D], bo1[:], ALU.add))
                    steps.do(nc.vector.tensor_tensor(Z[u][:], Z[u][:], N[u][:], ALU.add))
                    statistics(steps, Z[u][:], u, var3_ready)
                for u in range(2):
                    t = i * 2 + u
                    steps.do(normalise(ve, steps, Z[u][:], Z[u][:], u, dev3_ready, i * 2 + 1))
                    steps.do(nc.vector.tensor_tensor(Z[u][:], Z[u][:], gamma[:], ALU.mult))
                    steps.do(nc.vector.tensor_tensor(Z[u][:], Z[u][:], beta[:], ALU.add))
                    steps.do(nc.vector.tensor_tensor(tile_of(t), tile_of(t), Z[u][:], ALU.add))
                    statistics(steps, tile_of(t), u, var2_ready)
                for u in range(2):
                    normalise(ve, steps, N[u][:], tile_of(i * 2 + u), u, dev2_ready, k).then_inc(normed2, 1)
                for u in range(2):
                    ve.wait_ge(logits_ready, i * 2 + u + 1)
                    steps.do(nc.vector.tensor_copy(logits1[:, bass.ds(i * 2 + u, 1), :].rearrange("p o e -> p (o e)"),
                                                   bank(u, 1)[:, 0:E1]))
            steps.end(TILES // 2)
            nc.vector.memset(psum[:, 4:8, :], 0.0).then_inc(logits_copied, 1)

            ve.wait_ge(sig_ready, 1)
            steps.do(nc.vector.tensor_tensor(choice[:], sig1[:], spread(corr[:], TILES), ALU.add))
            quads = choice[:].rearrange("p t (g a b) -> p (t g) a b", g=2, a=2)
            a, b = quads[:, :, :, 0], quads[:, :, :, 1]
            steps.mark(nc.vector.tensor_tensor(pair_hi[:], a, b, ALU.max))
            steps.mark(nc.vector.tensor_tensor(pair_lo[:], a, b, ALU.min))
            steps.wait()
            steps.mark(nc.vector.tensor_tensor(best[:], pair_hi[:, :, 0:1], pair_hi[:, :, 1:2], ALU.max))
            steps.mark(nc.vector.tensor_tensor(second_a[:], pair_hi[:, :, 0:1], pair_hi[:, :, 1:2], ALU.min))
            steps.mark(nc.vector.tensor_tensor(second_b[:], pair_lo[:, :, 0:1], pair_lo[:, :, 1:2], ALU.max))
            steps.wait()
            steps.do(nc.vector.tensor_tensor(second_a[:], second_a[:], second_b[:], ALU.max))
            steps.do(nc.vector.tensor_tensor(best[:], best[:], second_a[:], ALU.add))
            g = best[:].rearrange("p (t g) o -> p t (g o)", g=2)
            steps.mark(nc.vector.tensor_tensor(group_sel[:, :, 0:1], g[:, :, 0:1], g[:, :, 1:2], ALU.is_ge))
            steps.mark(nc.vector.tensor_tensor(group_sel[:, :, 1:2], g[:, :, 0:1], g[:, :, 1:2], ALU.is_lt))
            steps.wait()
            groups = choice[:].rearrange("p t (g a) -> p (t g) a", g=2)
            steps.do(nc.vector.tensor_tensor(groups, groups, repeat(group_sel[:].rearrange("p t g -> p (t g)"), 4),
                                             ALU.mult))
            steps.do(nc.vector.tensor_scalar(choice[:], choice[:], 0.0, None, ALU.add))
            for t in range(TILES):
                steps.mark(nc.vector.max(sorted1[:, t, :], choice[:, t, :]))
            steps.wait()
            for t in range(TILES):
                steps.mark(nc.vector.max_index(index1[:, t, :], sorted1[:, t, :], choice[:, t, :]))
            steps.wait()
            steps.do(nc.vector.tensor_copy(index1f[:], index1[:, :, 0:TOP1]))
            full = [P, TILES * TOP1, E1]
            flat = picks1[:].rearrange("p t k e -> p (t k) e")
            chosen = index1f[:].rearrange("p t k -> p (t k)")
            steps.do(nc.vector.tensor_tensor(flat, cols("iota")[:, 0:E1].unsqueeze(1).to_broadcast(full),
                                             repeat(chosen, E1), ALU.is_equal))
            steps.do(nc.vector.tensor_tensor(picked1[:], picks1[:], sig1[:].unsqueeze(2).to_broadcast([P, TILES, TOP1, E1]),
                                             ALU.mult))
            steps.do(nc.vector.tensor_reduce(weight1[:], picked1[:], AX.X, ALU.add))
            steps.do(nc.vector.tensor_reduce(total1[:], weight1[:], AX.X, ALU.add))
            steps.do(nc.vector.tensor_scalar(total1[:], total1[:], 1e-20, None, ALU.add))
            steps.do(nc.vector.reciprocal(total1[:], total1[:]))
            steps.do(nc.vector.tensor_tensor(weight1[:], weight1[:], repeat(total1[:], TOP1), ALU.mult))
            steps.do(nc.vector.tensor_tensor(flat, flat, repeat(weight1[:].rearrange("p t k -> p (t k)"), E1), ALU.mult))
            nc.vector.tensor_tensor(comb1[:].rearrange("p e t -> p t e"), picks1[:, :, 0, :], picks1[:, :, 1, :],
                                    ALU.add).then_inc(comb_ready, 1)
            ve.wait_ge(comb_turned, 1)
            nc.vector.tensor_copy(comb_T[:], psum[0:E1 * TILES, 0, 0:P]).then_inc(comb_copied, 1)

            for h in range(2):
                ve.wait_ge(silu1_ready, h + 1)
                nc.vector.tensor_tensor(hid1[h][:].rearrange("p t i q -> p (t i) q")[:, :, 0:S],
                                        silu1[h][:].rearrange("p (m q) -> p m q", q=S),
                                        psum[:, 2 * h + 1, 0:HALF].rearrange("p (m q) -> p m q", q=S),
                                        ALU.mult).then_inc(hid1_ready, 1)
            ve.wait_ge(comb_loaded, 16)
            with ve.Fori(0, E1 // 2) as i:
                steps.begin(i, 4)
                for j in range(2):
                    for h in range(2):
                        n = i * 4 + (2 + 2 * j + h)
                        ve.wait_ge(silu1_ready, n + 1)
                        w = comb_b[:, bass.ds(i * (2 * TOKENS) + (j * TOKENS + h * HALF), HALF)]
                        steps.do(nc.vector.tensor_tensor(silu1[h][:], silu1[h][:], w, ALU.mult))
                        ve.wait_ge(down1_done, n - 1)
                        nc.vector.tensor_tensor(hid1[h][:].rearrange("p t i q -> p (t i) q")[:, :, 0:S],
                                                silu1[h][:].rearrange("p (m q) -> p m q", q=S),
                                                psum[:, 2 * h + 1, 0:HALF].rearrange("p (m q) -> p m q", q=S),
                                                ALU.mult).then_inc(hid1_ready, 1)
            steps.end(E1 // 2)
            ve.wait_ge(down1_done, 2 * (E1 + 1))
            for b in range(TILES // 2):
                pair = H[:, 2 * b:2 * b + 2, :].rearrange("p t f -> p (t f)")
                nc.vector.tensor_tensor(pair, psum[:, 4 + b, :], pair, ALU.add).then_inc(final_ready, 1)

        def softmax_scalar(act, k):
            for u in range(2):
                act.wait_ge(shifted, k + u)
                nc.scalar.activation(PR[u][:, :, 0:S], SM[u][:], ACT.Exp, scale=SCALE).then_inc(exped, 1)
            for u in range(2):
                act.wait_ge(prt_psum, k + u)
                nc.scalar.copy(PRT[u][:].rearrange("p (b h) q -> p b (h q)", b=2), scores(u)).then_inc(prt_ready, 1)

        def deviation(act, k, var, ready):
            for u in range(2):
                act.wait_ge(var, k + u)
                nc.scalar.activation(dev[u][:], moments[u][:, 1:2], ACT.Sqrt, bias=cols("eps")).then_inc(ready, 1)

        def evacuate(act, k, dst, b, width, psum_ready, ready):
            for u in range(2):
                act.wait_ge(psum_ready, k + u)
                nc.scalar.copy(dst[u], bank(u, b)[:, 0:width]).then_inc(ready, 1)

        @block.scalar
        def _(act):
            nt = [x[:].rearrange("p k q -> p (k q)") for x in NT]
            cxt = [x[:].rearrange("p k q -> p (k q)") for x in CXT]
            act.wait_ge(vec_setup, 1)
            with act.Fori(0, TILES // 2) as i:
                k = i * 2 + 1
                deviation(act, k, var_ready, dev_ready)
                evacuate(act, k, nt, 1, D, transposed, NT_ready)
                softmax_scalar(act, k)
                evacuate(act, k, cxt, 0, D, cx_transposed, cxt_ready)
                deviation(act, k, var2_ready, dev2_ready)
                evacuate(act, k, nt, 0, D, transposed2, NT2_ready)
                for u in range(2):
                    act.wait_ge(neg_ready, k + u)
                    nc.scalar.activation(r_exp[u][:], bank(u, 1)[:, 0:E0], ACT.Exp, bias=r_neg[u][:],
                                         accum_out=r_sum[u][:]).then_inc(rexp_ready, 1)
            with act.Fori(0, E0 // 2) as i:
                k = i * 2 + 1
                for u in range(2):
                    act.wait_ge(rows_transposed, k + u)
                    nc.scalar.copy(xT[u][:].rearrange("p k c -> p (k c)"), bank(u, 0)).then_inc(xT_ready, 1)
                for u in range(2):
                    act.wait_ge(gu_ready, k + u)
                    nc.scalar.activation(silu_a[u][:], bank(u, 1)[:, 0:CAP], ACT.Silu)
                    nc.scalar.activation(silu_b[u][P - F0B:P, :], bank(u, 2)[0:F0B, 0:CAP],
                                         ACT.Silu).then_inc(silu_ready, 1)
            with act.Fori(0, TILES // 2) as i:
                k = i * 2 + (TILES + 1)
                deviation(act, k, var_ready, dev_ready)
                evacuate(act, k, nt, 1, D, transposed, NT_ready)
                evacuate(act, i * 2 + 1, [x[:].rearrange("p m i q -> p (m i q)") for x in QK], 0, 4 * P,
                         h_transposed, h_ready)
                softmax_scalar(act, k)
                evacuate(act, k, cxt, 0, D, cx_transposed, cxt_ready)
                deviation(act, i * 2 + 1, var3_ready, dev3_ready)
                deviation(act, k, var2_ready, dev2_ready)
                for u in range(2):
                    act.wait_ge(transposed2, k + u)
                    both = bank(u, 0)[:, 0:D].rearrange("p (k i q) -> p k i q", k=KD, i=2)
                    for f in range(KD):
                        nc.scalar.copy(N3T[:, f, bass.ds(i * (2 * PAIR) + PAIR * u, PAIR)].rearrange(
                            "p (i q) -> p i q", i=2), both[:, f, :, 0:S])
                    nc.scalar.copy(nt[u], bank(u, 0)[:, 0:D]).then_inc(NT2_ready, 1)
            act.wait_ge(logits_copied, 1)
            nc.scalar.activation(sig1[:], logits1[:], ACT.Sigmoid).then_inc(sig_ready, 1)
            for h in range(2):
                act.wait_ge(gu1_ready, h + 1)
                nc.scalar.activation(silu1[h][:], psum[:, 2 * h, 0:HALF], ACT.Silu).then_inc(silu1_ready, 1)
            with act.Fori(0, E1 // 2) as i:
                for j in range(2):
                    for h in range(2):
                        act.wait_ge(gu1_ready, i * 4 + (3 + 2 * j + h))
                        nc.scalar.activation(silu1[h][:], psum[:, 2 * h, 0:HALF], ACT.Silu).then_inc(silu1_ready, 1)

        @block.gpsimd
        def _(pool):
            nc.gpsimd.memset(zeros[:], 0.0).then_inc(pool_step, 1)
            for u in range(2):
                nc.gpsimd.memset(headQ[u][:], 0.0)
                nc.gpsimd.memset(rows1[u][:], 0.0)
                nc.gpsimd.memset(hid1[u][:], 0.0)
                ins = nc.gpsimd.memset(sums[u][:], 0.0)
            ins.then_inc(pool_setup, 1)
            pool.wait_ge(pool_step, 1)
            span = zeros.shape[1]
            half = E0 * CAP // 2
            reps = half * ROW // P // span
            for u in range(2):
                dst = table[half * u:half * (u + 1), :].rearrange("(p r) x -> p (r x)", p=P)
                pool.dma_start(dst.rearrange("p (a b) -> p a b", b=span), spread(zeros[:], reps)).then_inc(scattered[u], 16)
            for c in range(CT):
                top_rows = ACC_ROWS // P * P
                pool.dma_start(acc[c][0:top_rows, :].rearrange("(p r) f -> p r f", p=P),
                               spread(zeros[:, 0:D], top_rows // P)).then_inc(added[c], 16)
                pool.dma_start(acc[c][top_rows:ACC_ROWS, :], zeros[0:ACC_ROWS - top_rows, 0:D]).then_inc(added[c], 16)
            for u in range(2):
                pool.wait_ge(scattered[u], 16)
            pool.wait_ge(small_loaded, 16 * len(early))
            with pool.Fori(0, TILES // 2) as i:
                k = i * 2 + 1
                for u in range(2):
                    t = i * 2 + u
                    pool.wait_ge(normed, k + u)
                    nc.gpsimd.tensor_tensor(tile_of(t), tile_of(t), bo[:], ALU.add).then_inc(bias_added, 1)
                for u in range(2):
                    pool.wait_ge(slots_ready, k + u)
                    pool.sem_inc(passed, 1)
                    for j in range(TOP0):
                        pool.indirect_dma_start(table, bass.IndirectOffsetOnAxis(ap=slot[u][:, j:j + 1], axis=0),
                                                row[u][:], None, bounds_check=E0 * CAP - 1,
                                                oob_is_err=False).then_inc(scattered[u], 16)
            with pool.Fori(0, E0 // 2) as i:
                for u in range(2):
                    pool.wait_ge(y_ready, i * 2 + u + 3)
                    for c in range(CT):
                        pool.wait_ge(added[c], i * 32 + (16 * u + 32))
                        pool.sem_inc(passed, 1)
                        pool.indirect_dma_start(acc[c], bass.IndirectOffsetOnAxis(ap=dest[u][:, c:c + 1], axis=0),
                                                y_rows[u][:, c, :], None, bounds_check=ACC_ROWS - 1,
                                                compute_op=ALU.add, oob_is_err=True).then_inc(added[c], 16)

        def product(dst, terms):
            for n, (a, b) in enumerate(terms):
                mm = nc.tensor.matmul(dst, a, b, start=(n == 0), stop=(n == len(terms) - 1))
            return mm

        def turn(pe, k, src, b, ready, done):
            for u in range(2):
                pe.wait_ge(ready, k + u)
                for g in range(src[u].shape[1] // P):
                    mm = nc.tensor.transpose(bank(u, b)[:, g * P:(g + 1) * P], src[u][:, g * P:(g + 1) * P], cols("ident"))
                mm.then_inc(done, 1)

        def attention_tensor(pe, k, values_ready):
            for u in range(2):
                pe.wait_ge(kb_ready, k + u)
                for g in range(KD):
                    for im in range(2):
                        mm = product(scores(u)[SLOT * im:SLOT * im + SLOT, g, 0:HG * S],
                                     [(QK[u][:, g, im, :], KB[u][:, 2 * g + im, :, :].rearrange("p h q -> p (h q)"))])
                mm.then_inc(scored, 1)
            for u in range(2):
                pe.wait_ge(exped, k + u)
                for hp in range(HP):
                    mm = nc.tensor.transpose(scores(u)[:, hp // 4, (hp % 4) * P:(hp % 4 + 1) * P],
                                             PR[u][:, 2 * hp:2 * hp + 2, :].rearrange("p h q -> p (h q)"), cols("ident"))
                mm.then_inc(prt_psum, 1)
            for u in range(2):
                pe.wait_ge(prt_ready, k + u)
                values_ready(u)
                for hp in range(HP):
                    for im in range(2):
                        mm = product(bank(u, 1)[SLOT * im:SLOT * im + SLOT, hp * VW:(hp + 1) * VW],
                                     [(PRT[u][:, hp, SLOT * im:SLOT * im + SLOT], VB[u][:, im, hp, :])])
                mm.then_inc(attended, 1)

        def project(pe, k, w):
            for u in range(2):
                pe.wait_ge(cxt_ready, k + u)
                product(bank(u, 1)[:, 0:D], [(CXT[u][:, g, :], w[:, g, :]) for g in range(KD)]).then_inc(projected, 1)

        @block.tensor
        def _(pe):
            pe.wait_ge(small_loaded, 16 * len(early))
            pe.wait_ge(vec_setup, 1)
            pe.wait_ge(pool_setup, 1)
            with pe.Fori(0, TILES // 2) as i:
                k = i * 2 + 1
                for u in range(2):
                    pe.wait_ge(patches_loaded[u], i * 16 + 16)
                    for im in range(2):
                        mm = product(bank(u, 0)[SLOT * im:SLOT * im + SLOT, 0:D],
                                     [(patches[u][:, kp * PAIR + S * im:kp * PAIR + S * im + SLOT], tok_w[:, kp, :])
                                      for kp in range(KP)])
                    mm.then_inc(embedded, 1)
                turn(pe, k, [x[:] for x in N], 1, normed, transposed)
                for u in range(2):
                    pe.wait_ge(NT_ready, k + u)
                    tokens = [NT[u][:, f, :].rearrange("p (i q) -> p i q", i=2)[:, :, 0:S] for f in range(KD)]
                    for half in range(2):
                        for m in range(4):
                            c = (4 * half + m) * P
                            mm = product(bank(u, 2 + half)[:, m * PAIR:(m + 1) * PAIR].rearrange("p (i q) -> p i q", i=2),
                                         [(wqk[:, f, c:c + P], tokens[f]) for f in range(KD)])
                    mm.then_inc(qk_ready, 1)
                    for im in range(2):
                        for o in range(2):
                            mm = product(bank(u, 0)[SLOT * o:SLOT * o + SLOT, im * D:(im + 1) * D],
                                         [(NT[u][:, f, SLOT * im:SLOT * im + SLOT], wv[:, f, :]) for f in range(KD)])
                    mm.then_inc(v_ready, 1)
                attention_tensor(pe, k, lambda u: pe.wait_ge(vb_ready, k + u))
                turn(pe, k, [x[:].rearrange("p h d -> p (h d)") for x in CX], 0, cx_ready, cx_transposed)
                project(pe, k, wo)
                turn(pe, k, [x[:, 0:D] for x in row], 0, normed2, transposed2)
                for u in range(2):
                    pe.wait_ge(NT2_ready, k + u)
                    product(bank(u, 1)[:, 0:E0], [(NT[u][:, f, :], gate_w[:, f, :]) for f in range(KD)]).then_inc(routed, 1)
                for u in range(2):
                    pe.wait_ge(mask_ready, k + u)
                    pe.wait_ge(taken_ready, k + u)
                    product(bank(u, 2)[:, 0:E0], [(count_earlier[:], r_mask[u][:]), (count_valid[:], taken[:])]
                            ).then_inc(counted, 1)
            with pe.Fori(0, E0 // 2) as i:
                k = i * 2 + 1
                for u in range(2):
                    pe.wait_ge(rows_loaded[u], i * 16 + 16)
                    for f in range(KD):
                        for c in range(CT):
                            mm = nc.tensor.transpose(bank(u, 0)[:, f * CAP + c * P:f * CAP + (c + 1) * P],
                                                     xrows[u][:, c, f * P:(f + 1) * P], cols("ident"))
                    mm.then_inc(rows_transposed, 1)
                for u in range(2):
                    pe.wait_ge(xT_ready, k + u)
                    pe.wait_ge(ew_loaded[u], i * 48 + 48)
                    for b, c, m in ((1, 0, 0), (1, CAP, 2 * P), (2, 0, P)):
                        mm = product(bank(u, b)[:, c:c + CAP],
                                     [(gu_w[u][:, f, m:m + P], xT[u][:, f, :]) for f in range(KD)])
                    mm.then_inc(gu_ready, 1)
                for u in range(2):
                    pe.wait_ge(hid_ready, k + u)
                    pe.wait_ge(y_ready, k + u)
                    for c in range(CT):
                        mm = product(bank(u, 3)[:, c * D:(c + 1) * D],
                                     [(hid_a[u][:, c * P:(c + 1) * P], dn_w[u][:, 0, :]),
                                      (hid_b[u][P - F0B:P, c * P:(c + 1) * P], dn_w[u][P - F0B:P, 1, :])])
                    mm.then_inc(down_ready, 1)
            pe.wait_ge(late_loaded, 16 * len(late))
            with pe.Fori(0, TILES // 2) as i:
                k = i * 2 + (TILES + 1)
                turn(pe, k, [x[:] for x in N], 1, normed, transposed)
                for u in range(2):
                    pe.wait_ge(NT_ready, k + u)
                    product(bank(u, 2), [(NT[u][:, f, :], wqkv1[:, f, 0:2 * D]) for f in range(KD)])
                    product(bank(u, 3)[:, 0:D], [(NT[u][:, f, :], wqkv1[:, f, 2 * D:3 * D]) for f in range(KD)]
                            ).then_inc(qk_ready, 1)
                for u in range(2):
                    pe.wait_ge(heads_loaded[u], i * 128 + 128)
                    for m in range(4):
                        mm = nc.tensor.transpose(bank(u, 0)[:, m * P:(m + 1) * P],
                                                 headQ[u][:, m // 2, (m % 2) * P:(m % 2 + 1) * P], cols("ident"))
                    mm.then_inc(h_transposed, 1)
                attention_tensor(pe, k, lambda u: None)
                for u in range(2):
                    pe.wait_ge(ctx_loaded[u], i * 32 + 32)
                    for g in range(KD):
                        mm = nc.tensor.transpose(bank(u, 0)[:, g * P:(g + 1) * P], rows1[u][:, g * P:(g + 1) * P],
                                                 cols("ident"))
                    mm.then_inc(cx_transposed, 1)
                project(pe, k, wo1)
                turn(pe, k, [x[:] for x in N], 0, normed2, transposed2)
                for u in range(2):
                    pe.wait_ge(NT2_ready, k + u)
                    product(bank(u, 1)[:, 0:E1], [(NT[u][:, f, :], router_w[:, f, :]) for f in range(KD)]
                            ).then_inc(logits_ready, 1)
            pe.wait_ge(comb_ready, 1)
            nc.tensor.transpose(psum[0:E1 * TILES, 0, 0:P], comb1[:].rearrange("p e t -> p (e t)"), cols("ident")
                                ).then_inc(comb_turned, 1)
            pe.wait_ge(comb_copied, 1)

            def gate_up(buf, h):
                for m in range(2):
                    mm = product(psum[:, 2 * h + m, 0:HALF],
                                 [(wgu1[buf][:, f, m * I1:(m + 1) * I1], N3T[:, f, h * HALF:(h + 1) * HALF])
                                  for f in range(KD)])
                mm.then_inc(gu1_ready, 1)

            def down(buf, h):
                for t in range(HT):
                    at = h * HT + t
                    mm = nc.tensor.matmul(psum[:, 4 + at // 2, (at % 2) * D:(at % 2 + 1) * D],
                                          hid1[h][:, t, :, :].rearrange("p i q -> p (i q)"), wd1[buf][:],
                                          start=False, stop=True, skip_group_check=True)
                mm.then_inc(down1_done, 1)

            pe.wait_ge(w1_loaded[0], 32)
            gate_up(0, 0)
            gate_up(0, 1)
            pe.wait_ge(hid1_ready, 1)
            down(0, 0)
            with pe.Fori(0, E1 // 2) as i:
                for j, buf in ((0, 1), (1, 0)):
                    n = i * 4 + (2 + 2 * j)
                    pe.wait_ge(w1_loaded[buf], i * 32 + (32 if buf else 64))
                    gate_up(buf, 0)
                    pe.wait_ge(hid1_ready, n)
                    down(1 - buf, 1)
                    gate_up(buf, 1)
                    pe.wait_ge(hid1_ready, n + 1)
                    down(buf, 0)
            pe.wait_ge(hid1_ready, 2 * (E1 + 1))
            down(0, 1)


_OUT = (IMAGES, S, D)


def _layout(a):
    def k_rows(w):
        return np.ascontiguousarray(w.reshape(w.shape[0] // P, P, -1).transpose(1, 0, 2))

    x = a["x"].reshape(TILES, 2, 3, 7, 16, 7, 16).transpose(0, 2, 4, 6, 1, 3, 5).reshape(TILES, KP, P, PAIR)
    wqkv, bqkv = a["L0_attn_w_qkv"], a["L0_attn_b_qkv"]
    swap = np.arange(2 * D) ^ 1
    wqk = np.concatenate([wqkv[:2 * D], wqkv[:2 * D][swap]], axis=0).T
    rope_b = np.concatenate([bqkv[:2 * D], bqkv[:2 * D][swap]]).reshape(8, P).T
    order = np.concatenate([np.arange(P), np.arange(P, F0), np.arange(F0 + P, 2 * F0), np.arange(F0, F0 + P)])
    gu = a["L0_ffn_gate_up_proj"][:, order, :].transpose(0, 2, 1).reshape(E0, KD, P, 2 * F0).transpose(0, 2, 1, 3)
    gate = np.concatenate([a["L1_ffn_sw_gate"][None], a["L1_ffn_w_gate"]])
    up = np.concatenate([a["L1_ffn_sw_up"][None], a["L1_ffn_w_up"]])
    gu1 = np.concatenate([gate, up], axis=2).reshape(E1 + 1, KD, P, 2 * I1).transpose(0, 2, 1, 3)
    return {
        "const": constants(),
        "patches": x.transpose(0, 2, 1, 3).reshape(TILES, P, KP * PAIR),
        "tok_w": k_rows(a["L0_tok_W"]), "tok_b": a["L0_tok_b"],
        "wqk": k_rows(wqk), "rope_b": rope_b,
        "wv": k_rows(wqkv[2 * D:].T), "bv": bqkv[2 * D:],
        "wo": k_rows(a["L0_attn_w_out"].T), "bo": a["L0_attn_b_out"],
        "gate_w": k_rows(a["L0_ffn_gate_weight"].T),
        "gu_w": gu, "dn_w": a["L0_ffn_down_proj"].transpose(0, 2, 1),
        "wqkv1": k_rows(np.concatenate([a["L1_attn_wq"], a["L1_attn_wk"], a["L1_attn_wv"]], axis=1)),
        "bqkv1": np.concatenate([a["L1_attn_bq"], a["L1_attn_bk"], a["L1_attn_bv"]]),
        "wo1": k_rows(a["L1_attn_wo"]), "bo1": a["L1_attn_bo"],
        "gamma": a["L1_attn_gamma"], "beta": a["L1_attn_beta"],
        "router_w": k_rows(a["L1_ffn_router_weight"].T), "corr": a["L1_ffn_correction_bias"],
        "wgu1": gu1, "wd1": np.concatenate([a["L1_ffn_sw_down"][None], a["L1_ffn_w_down"]]),
    }


def kernel(**inputs):
    import concourse.bacc as bacc
    from concourse.bass_utils import run_bass_kernel_spmd

    nc = bacc.Bacc("TRN2", target_bir_lowering=False, num_devices=1)
    laid = {n: np.ascontiguousarray(v) for n, v in _layout({n: np.asarray(v) for n, v in inputs.items()}).items()}
    arrays = {f"in_{n}": v for n, v in laid.items()}
    dram = {n: nc.dram_tensor(f"in_{n}", list(v.shape), F32, kind="ExternalInput").ap() for n, v in laid.items()}
    out = nc.dram_tensor("out_0", list(_OUT), F32, kind="ExternalOutput").ap()
    vit_tower(nc, dram, out)
    r = run_bass_kernel_spmd(nc, [arrays], core_ids=[0])
    return r.results[0]["out_0"]
```

```python
from contextlib import ExitStack

import numpy as np

import concourse.bass as bass
from concourse import mybir

F32 = mybir.dt.float32
BF16 = mybir.dt.bfloat16
I32 = mybir.dt.int32
U32 = mybir.dt.uint32
ALU = mybir.AluOpType
ACT = mybir.ActivationFunctionType
AX = mybir.AxisListType

P = 128
IMAGES, S, D = 16, 49, 256
TOKENS = IMAGES * S
TILES = IMAGES // 2
PAIR = 2 * S
SLOT = 64
PATCH = 768
KP = PATCH // P
KD = D // P
HEADS, HD = 16, 16
HG = HEADS // KD
SCALE = HD ** -0.5
HP = HEADS // 2
VW = 2 * (HD + 1)
EPS = 1e-5

E0, TOP0, CAP, F0 = 32, 8, 256, 192
CT = CAP // P
F0B = F0 - P
ROW = D + 1 + E0
FAR = float(1 << 20)
ACC_ROWS = TOKENS + 1 + P

E1, TOP1, I1 = 8, 2, 128
CH = D // HD
QKV_ROWS = SLOT + HD
LONG = PAIR * CH
CG = CH // 4
HALF = TOKENS // 2
HT = TILES // 2

LOOP0_STEPS = 60
LOOP1_STEPS = 26

_AT = {}
_WIDTH = 0
for _name, _w in (("ident", P), ("head_mask", HG), ("causal", S), ("cos", S), ("sin", S), ("earlier", P),
                  ("valid", P), ("pad_far", 1), ("slot_base", E0), ("iota", E0), ("token", 1),
                  ("empty_row", 1), ("eps", 1)):
    _AT[_name] = (_WIDTH, _WIDTH + _w)
    _WIDTH += _w


def constants():
    c = np.zeros((P, _WIDTH), np.float32)

    def put(name, a):
        lo, hi = _AT[name]
        c[:, lo:hi] = a

    p = np.arange(P)
    pos, valid = p % SLOT, (p % SLOT) < S
    put("ident", np.eye(P))
    put("head_mask", (p[:, None] // HD) == np.arange(HG)[None, :])
    put("causal", np.where(np.arange(S)[None, :] <= pos[:, None], 0.0, -1e30))
    freq = (np.float32(10000.0) ** (-np.arange(0, HD, 2, dtype=np.float32) / np.float32(HD))).astype(np.float32)
    ang = np.arange(S, dtype=np.float32)[None, :] * freq[(p % HD) // 2][:, None]
    put("cos", np.cos(ang))
    put("sin", np.sin(ang) * np.where(p % 2 == 0, -1.0, 1.0)[:, None])
    put("earlier", valid[:, None] & (p[:, None] < p[None, :]))
    put("valid", np.repeat(valid[:, None], P, axis=1))
    put("pad_far", np.where(valid, 0.0, FAR)[:, None])
    put("slot_base", CAP * np.arange(E0)[None, :])
    put("iota", np.arange(E0)[None, :])
    put("token", (pos + S * (p // SLOT) + 1)[:, None])
    put("empty_row", (TOKENS + 1 + p)[:, None])
    put("eps", EPS)
    return c


class Steps:

    def __init__(self, eng, sem):
        self.eng, self.sem, self.total = eng, sem, 0
        self.base, self.n = 0, 0

    def begin(self, i, per_pass):
        self.total += self.n
        self.base, self.n, self.per_pass = self.total + i * per_pass, 0, per_pass

    def end(self, passes):
        assert self.n == self.per_pass, f"{self.n} steps in a pass"
        self.total += passes * self.n
        self.base, self.n = self.total, 0

    def do(self, instruction):
        self.mark(instruction)
        self.wait()

    def mark(self, instruction):
        instruction.then_inc(self.sem, 1)
        self.n += 1

    def wait(self):
        self.eng.wait_ge(self.sem, self.base + self.n)


def vit_tower(nc, dram, out):
    ctx = ExitStack()
    with ctx:
        def sb(name, shape, dt=F32):
            return ctx.enter_context(nc.sbuf_tensor(name, shape, dt))

        def two(name, shape, dt=F32):
            return [sb(f"{name}{u}", shape, dt) for u in range(2)]

        def sem(name):
            return ctx.enter_context(nc.semaphore(name))

        def sem2(name):
            return [sem(f"{name}{u}") for u in range(2)]

        def cols(name):
            lo, hi = _AT[name]
            return const[:, lo:hi]

        def spread(ap, n):
            return ap.unsqueeze(1).to_broadcast([ap.shape[0], n] + list(ap.shape[1:]))

        def repeat(ap, n):
            return ap.unsqueeze(len(ap.shape)).to_broadcast(list(ap.shape) + [n])

        table = nc.dram_tensor("expert_rows", [E0 * CAP, ROW], F32, kind="Internal").ap()
        acc = [nc.dram_tensor(f"expert_sums{c}", [ACC_ROWS, D], F32, kind="Internal").ap() for c in range(CT)]
        comb_flat = nc.dram_tensor("comb_flat", [E1 * TILES, 2, S], F32, kind="Internal").ap()

        const = sb("const", [P, _WIDTH])
        count_earlier = sb("count_earlier", [P, P], BF16)
        count_valid = sb("count_valid", [P, P], BF16)
        zeros = sb("zeros", [P, 2 * ROW])
        tok_w = sb("tok_w", [P, KP, D])
        tok_b = sb("tok_b", [P, D])
        wqk = sb("wqk", [P, KD, 4 * D])
        rope_b = sb("rope_b", [P, 8])
        rope_bias = sb("rope_bias", [P, 4, S])
        wv = sb("wv", [P, KD, D])
        bv = sb("bv", [P, D])
        wo = sb("wo", [P, KD, D])
        bo = sb("bo", [P, D])
        gate_w = sb("gate_w", [P, KD, E0])
        wqkv1 = sb("wqkv1", [P, KD, CH, QKV_ROWS])
        bqkv1 = sb("bqkv1", [QKV_ROWS, CH])
        wo1 = sb("wo1", [P, CG, D])
        bo1 = sb("bo1", [P, D])
        gamma = sb("gamma", [P, D])
        beta = sb("beta", [P, D])
        router_w = sb("router_w", [P, KD, E1])
        corr = sb("corr", [P, E1])
        H = sb("H", [P, TILES, D])
        taken = sb("taken", [P, E0], BF16)
        patches = two("patches", [P, KP * PAIR + 16])
        stats = two("stats", [P, 6])
        moments = two("moments", [P, 2])
        dev = two("dev", [P, 1])
        rstd = two("rstd", [P, 1])
        N = two("N", [P, D])
        NT = two("NT", [P, KD, P])
        room = sb("room", [P, E1 * TOKENS])
        room_used = 0

        def in_room(pattern, *dims, **sizes):
            nonlocal room_used
            lo, n = room_used, int(np.prod(dims))
            room_used += n
            return room[:, lo:lo + n].rearrange(pattern, **sizes)

        rope_a = [in_room("p (m x) -> p m x", 4, 2 * S, m=4) for _ in range(2)]
        rope_s = [in_room("p (m x) -> p m x", 4, 2 * S, m=4) for _ in range(2)]
        KB = [in_room("p (m h k) -> p m h k", 4, HG, S, m=4, h=HG) for _ in range(2)]
        SM = [in_room("p (h k) -> p h k", HEADS, S, h=HEADS) for _ in range(2)]
        comb_b = room
        QK = two("QK", [P, 4, 2, SLOT])
        VB = two("VB", [P, 2, HP, VW])
        top = two("top", [P, HEADS])
        PR = two("PR", [P, HEADS, SLOT])
        PRT = two("PRT", [P, HP, P])
        den = two("den", [P, HEADS])
        rden = two("rden", [P, HEADS])
        CX = two("CX", [P, HEADS, HD])
        CXT = two("CXT", [P, KD, P])
        row = two("row", [P, ROW])
        r_neg = two("r_neg", [P, 1])
        r_top = two("r_top", [P, TOP0])
        r_exp = two("r_exp", [P, E0])
        r_sum = two("r_sum", [P, 1])
        r_inv = two("r_inv", [P, 1])
        r_prob = two("r_prob", [P, E0])
        r_left = two("r_left", [P, E0])
        r_index = two("r_index", [P, TOP0], U32)
        r_expert = two("r_expert", [P, TOP0])
        r_mask = two("r_mask", [P, E0], BF16)
        r_over = two("r_over", [P, E0])
        r_slots = two("r_slots", [P, E0])
        r_pick = two("r_pick", [P, TOP0, E0])
        r_slot = two("r_slot", [P, TOP0])
        slot = two("slot", [P, TOP0], I32)
        xrows = two("xrows", [P, CT, ROW])
        gu_w = two("gu_w", [P, KD, 2 * F0])
        dn_w = two("dn_w", [P, 2, D])
        work = two("work", [P, LONG + SLOT - S + 1])
        xT = [x[:, 0:KD * CAP].rearrange("p (k c) -> p k c", k=KD) for x in work]
        silu_a, silu_b, hid_a, hid_b = ([x[:, n * CAP:(n + 1) * CAP] for x in work] for n in range(KD, KD + 4))
        positions = work
        y_rows = two("y_rows", [P, CT, D])
        row_id = two("row_id", [P, CT])
        row_w = two("row_w", [P, CT])
        dest_f = two("dest_f", [P, CT])
        dest = two("dest", [P, CT], I32)
        sums = two("sums", [P, CT, D])
        KP1 = [x.rearrange("p m h k -> p (m h k)") for x in KB]
        CT1 = [x[:].rearrange("p m i q -> p m (i q)") for x in QK]
        residual = two("residual", [P, D])
        Z = two("Z", [P, D])
        N3 = [x[:, 0:D] for x in row]
        N3T = sb("N3T", [P, KD, TOKENS])
        logits1 = sb("logits1", [P, TILES, E1])
        wgu1 = two("wgu1", [P, KD, 2 * I1])
        wd1 = two("wd1", [P, D])
        comb_T = sb("comb_T", [E1 * TILES, P])
        sig1 = sb("sig1", [P, TILES, E1])
        choice = sb("choice", [P, TILES, E1])
        pair_hi = sb("pair_hi", [P, 2 * TILES, 2])
        pair_lo = sb("pair_lo", [P, 2 * TILES, 2])
        best = sb("best", [P, 2 * TILES, 1])
        second_a = sb("second_a", [P, 2 * TILES, 1])
        second_b = sb("second_b", [P, 2 * TILES, 1])
        group_sel = sb("group_sel", [P, TILES, 2])
        sorted1 = sb("sorted1", [P, TILES, E1])
        index1 = sb("index1", [P, TILES, E1], U32)
        index1f = sb("index1f", [P, TILES, TOP1])
        picks1 = sb("picks1", [P, TILES, TOP1, E1])
        picked1 = sb("picked1", [P, TILES, TOP1, E1])
        weight1 = sb("weight1", [P, TILES, TOP1])
        total1 = sb("total1", [P, TILES])
        comb1 = sb("comb1", [P, E1, TILES])
        silu1 = two("silu1", [P, HALF])
        hid1 = two("hid1", [P, HT, 2, SLOT])

        psum = ctx.enter_context(nc.psum_tensor("psum", [P, 8, 512], F32))

        def bank(u, b):
            return psum[:, 4 * u + b, :]

        def scores(u):
            return psum[:, 4 * u + 2:4 * u + 4, :]

        small_loaded = sem("small_loaded")
        late_loaded = sem("late_loaded")
        vec_setup = sem("vector_setup")
        pool_setup = sem("pool_setup")
        patches_loaded = sem2("patches_loaded")
        vec = sem("vector_steps")
        act_step = sem("scalar_steps")
        pool_step = sem("pool_steps")
        passed = sem("passed_wait")
        embedded = sem("embedded")
        var_ready = sem("var_ready")
        dev_ready = sem("dev_ready")
        normed = sem("normed")
        transposed = sem("transposed")
        NT_ready = sem("NT_ready")
        bias_added = sem("bias_added")
        qk_ready = sem("qk_ready")
        v_ready = sem("v_ready")
        kb_ready = sem("kb_ready")
        vb_ready = sem("vb_ready")
        scored = sem("scored")
        shifted = sem("shifted")
        exped = sem("exped")
        prt_psum = sem("probs_transposed")
        prt_ready = sem("prt_ready")
        attended = sem("attended")
        cx_ready = sem("cx_ready")
        cx_transposed = sem("cx_transposed")
        cxt_ready = sem("cxt_ready")
        projected = sem("projected")
        var2_ready = sem("var2_ready")
        dev2_ready = sem("dev2_ready")
        normed2 = sem("normed2")
        transposed2 = sem("transposed2")
        NT2_ready = sem("NT2_ready")
        routed = sem("router_logits")
        neg_ready = sem("neg_ready")
        rexp_ready = sem("rexp_ready")
        mask_ready = sem("mask_ready")
        taken_ready = sem("taken_ready")
        counted = sem("counted")
        slots_ready = sem("slots_ready")
        scattered = sem2("scattered")
        rows_loaded = sem2("rows_loaded")
        gu_loaded = sem2("gate_up_loaded")
        dn_loaded = sem2("down_loaded")
        meta_ready = sem("slot_tokens_ready")
        rows_transposed = sem("rows_transposed")
        xT_ready = sem("xT_ready")
        gu_ready = sem("gate_up_ready")
        silu_ready = sem("silu_ready")
        hid_ready = sem("hidden_ready")
        down_ready = sem("down_ready")
        y_ready = sem("y_ready")
        added = sem2("sums_added")
        sums_loaded = sem2("sums_loaded")
        qkv_ready = sem("qkv_ready")
        keys_ready = sem("keys_ready")
        values_turned = sem("values_turned")
        values_ready = sem("values_ready")
        summed = sem("experts_summed")
        residual_ready = sem("residual_ready")
        exped1 = sem("exped1")
        probs_ready = sem("probs_ready")
        attended1 = sem("attended1")
        low_ready = sem("low_results_ready")
        high_ready = sem("high_results_ready")
        var3_ready = sem("var3_ready")
        dev3_ready = sem("dev3_ready")
        compacted = sem("compacted")
        logits_ready = sem("logits_ready")
        logits_copied = sem("logits_copied")
        sig_ready = sem("sigmoid_ready")
        comb_ready = sem("comb_ready")
        comb_turned = sem("comb_turned")
        comb_copied = sem("comb_copied")
        comb_stored = sem("comb_stored")
        comb_loaded = sem("comb_loaded")
        w1_loaded = sem2("w1_loaded")
        gu1_ready = sem("gate_up1_ready")
        silu1_ready = sem("silu1_ready")
        hid1_ready = sem("hidden1_ready")
        down1_done = sem("down1_done")
        final_ready = sem("final_ready")
        out_stored = sem("out_stored")

        early = [(const[:], dram["const"]), (tok_w[:], dram["tok_w"]),
                 (tok_b[:], dram["tok_b"].partition_broadcast(P)),
                 (rope_b[:], dram["rope_b"]), (wqk[:], dram["wqk"]), (wv[:], dram["wv"]),
                 (bv[:], dram["bv"].partition_broadcast(P)), (wo[:], dram["wo"]),
                 (bo[:], dram["bo"].partition_broadcast(P)), (gate_w[:], dram["gate_w"])]
        late = [(wqkv1[:], dram["wqkv1"]), (bqkv1[:], dram["bqkv1"]),
                (wo1[:], dram["wo1"]), (bo1[:], dram["bo1"].partition_broadcast(P)),
                (gamma[:], dram["gamma"].partition_broadcast(P)),
                (beta[:], dram["beta"].partition_broadcast(P)),
                (router_w[:], dram["router_w"]), (corr[:], dram["corr"].partition_broadcast(P))]
    
        def images(ap):
            return [ap[SLOT * i:SLOT * i + S] for i in range(2)]

        FIRST = 0

        def following(j, u):
            return ((j, 1), (j + 1, 0)) if u == 0 else ((j + 1, 0), (j + 1, 1))

        block = ctx.enter_context(nc.Block())

        @block.sync
        def _(sp):
            def load_patches(t, u):
                sp.dma_start(patches[u][:, 0:KP * PAIR],
                             dram["patches"][bass.ds(t, 1), :, :].rearrange("o p x -> (o p) x")
                             ).then_inc(patches_loaded[u], 16)

            for dst, src in early[:3]:
                sp.dma_start(dst, src).then_inc(small_loaded, 16)
            for u in range(2):
                load_patches(u, u)
            for dst, src in early[3:]:
                sp.dma_start(dst, src).then_inc(small_loaded, 16)

            def load_gate_up(e, u):
                sp.dma_start(gu_w[u][:], dram["gu_w"][bass.ds(e, 1), :, :, :].rearrange("o p k n -> (o p) k n")
                             ).then_inc(gu_loaded[u], 16)

            def load_down(e, u):
                sp.dma_start(dn_w[u][:, 0, :], dram["dn_w"][bass.ds(e, 1), 0:P, :].rearrange("o p n -> (o p) n")
                             ).then_inc(dn_loaded[u], 16)
                sp.dma_start(dn_w[u][P - F0B:P, 1, :],
                             dram["dn_w"][bass.ds(e, 1), P:F0, :].rearrange("o p n -> (o p) n")
                             ).then_inc(dn_loaded[u], 16)

            def load_rows(e, u):
                sp.dma_start(xrows[u][:], table[bass.ds(e * CAP, CAP), :].rearrange("(c p) x -> p c x", p=P)
                             ).then_inc(rows_loaded[u], 16)

            with sp.Fori(0, TILES // 2 - 1) as i:
                for u in range(2):
                    sp.wait_ge(embedded, i * 2 + u + 1)
                    load_patches(i * 2 + u + 2, u)
            for dst, src in late:
                sp.dma_start(dst, src).then_inc(late_loaded, 16)
            for u in range(2):
                load_gate_up(u, u)
                load_down(u, u)
            for u in range(2):
                sp.wait_ge(scattered[u], 16 + 16 * TOP0 * (TILES // 2))
            for u in range(2):
                load_rows(u, u)
            def next_rows(e, u):
                sp.wait_ge(rows_transposed, e - 1)
                sp.wait_ge(meta_ready, e - 1)
                load_rows(e, u)
                sp.wait_ge(gu_ready, e - 1)
                load_gate_up(e, u)

            def next_down(e, u):
                sp.wait_ge(down_ready, e - 1)
                load_down(e, u)

            next_rows(2, 0)
            with sp.Fori(0, E0 // 2 - 2) as i:
                for e, u in ((i * 2 + 3, 1), (i * 2 + 4, 0)):
                    next_rows(e, u)
                    next_down(e - 1, 1 - u)
            next_rows(E0 - 1, 1)
            next_down(E0 - 2, 0)
            next_down(E0 - 1, 1)

            def load_w1(e, u):
                sp.dma_start(wgu1[u][:], dram["wgu1"][bass.ds(e, 1), :, :, :].rearrange("o p k n -> (o p) k n")
                             ).then_inc(w1_loaded[u], 16)
                sp.dma_start(wd1[u][:], dram["wd1"][bass.ds(e, 1), :, :].rearrange("o p n -> (o p) n")
                             ).then_inc(w1_loaded[u], 16)

            for u in range(2):
                load_w1(u, u)

            def load_sums(t, u):
                for c in range(CT):
                    for im, half in enumerate(images(sums[u])):
                        sp.dma_start(half[:, c, :], acc[c][bass.ds(t * PAIR + S * im + 1, S), :]
                                     ).then_inc(sums_loaded[u], 16)

            sp.wait_ge(pool_setup, 1)
            for c in range(CT):
                sp.wait_ge(added[c], 32 + 16 * E0)
            for u in range(2):
                load_sums(u, u)

            with sp.Fori(0, TILES // 2 - 1) as i:
                for u in range(2):
                    sp.wait_ge(summed, i * 2 + u + 1)
                    load_sums(i * 2 + u + 2, u)

            sp.wait_ge(comb_copied, 1)
            for im in range(2):
                sp.dma_start(comb_flat[:, im, :], comb_T[0:E1 * TILES, SLOT * im:SLOT * im + S]
                             ).then_inc(comb_stored, 16)
            sp.wait_ge(comb_stored, 32)
            sp.dma_start(comb_b[:], comb_flat.rearrange("a i q -> (a i q)").partition_broadcast(P)
                         ).then_inc(comb_loaded, 16)
            with sp.Fori(0, (E1 - 2) // 2) as i:
                for u in range(2):
                    sp.wait_ge(down1_done, i * 4 + 2 * u + 2)
                    load_w1(i * 2 + u + 2, u)
            sp.wait_ge(down1_done, 2 * (E1 - 1))
            load_w1(E1, 0)
            sp.wait_ge(final_ready, TILES // 2)
            for im in range(2):
                sp.dma_start(out.rearrange("(t i) q f -> i q t f", i=2)[im],
                             H[SLOT * im:SLOT * im + S, :, :]).then_inc(out_stored, 16)
            sp.wait_ge(out_stored, 32)

        def results_by_chunks(copy, u, g):
            first = HG * S * g
            for j in range(4):
                tokens = [t for t in range(S) if first <= t * CH + CG * j < first + HG * S]
                lo, n = tokens[0], len(tokens)
                at = lo * CH + CG * j - first
                src = psum[0:HD, 4 * u + 2 * g:4 * u + 2 * g + 2, at:at + n * CH]
                dst = CT1[u][32 * j:32 * j + HD, :, :].rearrange("p c (i q) -> p i q c", i=2)[:, :, lo:lo + n, :]
                ins = copy(dst, src.rearrange("p i (q c) -> p i q c", c=CH)[:, :, :, 0:CG])
            return ins

        def shifted_scores(ve, steps, k, mask):
            for u in range(2):
                shift_tile(ve, steps, k + u, u, mask)

        def shift_tile(ve, steps, n, u, mask):
            ve.wait_ge(scored, n)
            sc = scores(u)[:, :, 0:HG * S].rearrange("p g (h k) -> p g h k", k=S)
            sm = SM[u][:].rearrange("p (g h) k -> p g h k", g=KD)
            mx = top[u][:].rearrange("p (g h) -> p g h", g=KD)
            if mask:
                causal = cols("causal").unsqueeze(1).unsqueeze(1).to_broadcast([P, KD, HG, S])
                steps.do(nc.vector.tensor_tensor(sm, sc, causal, ALU.add))
                sc = sm
            steps.do(nc.vector.tensor_reduce(mx, sc, AX.X, ALU.max))
            nc.vector.tensor_tensor(sm, sc, repeat(mx, S), ALU.subtract).then_inc(shifted, 1)

        def head_results(ve, steps, k):
            for u in range(2):
                ve.wait_ge(attended, k + u)
                o = bank(u, 1)[:, 0:HP * VW].rearrange("p (h x) -> p h x", x=HD + 1)
                total = o[:, :, HD:HD + 1].rearrange("p h x -> p (h x)")
                steps.do(nc.vector.tensor_scalar(den[u][:], total, 1e-8, None, ALU.add))
                steps.do(nc.vector.reciprocal(rden[u][:], den[u][:]))
                nc.vector.tensor_tensor(CX[u][:], o[:, :, 0:HD], repeat(rden[u][:], HD),
                                        ALU.mult).then_inc(cx_ready, 1)

        def key_blocks(steps, u):
            keys = QK[u][:, 2:4, :, 0:S].rearrange("p g i q -> p (g i) q").unsqueeze(2).to_broadcast([P, 4, HG, S])
            mask = repeat(spread(cols("head_mask"), 4), S)
            return nc.vector.tensor_tensor(KB[u][:], keys, mask, ALU.mult)

        def statistics(steps, src, u, ready):
            steps.eng.sem_inc(passed, 1)
            steps.do(nc.vector.bn_stats(stats[u][:], src))
            steps.eng.sem_inc(passed, 1)
            nc.vector.bn_aggr(moments[u][:], stats[u][:]).then_inc(ready, 1)

        def normalise(ve, steps, dst, src, u, ready, k):
            ve.wait_ge(ready, k + u)
            steps.do(nc.vector.reciprocal(rstd[u][:], dev[u][:]))
            return nc.vector.tensor_scalar(dst, src, moments[u][:, 0:1], rstd[u][:], ALU.subtract, ALU.mult)

        def tile_of(t):
            return H[:, bass.ds(t, 1), :].rearrange("p o f -> p (o f)")

        @block.vector
        def _(ve):
            steps = Steps(ve, vec)
            nc.vector.memset(taken[:], 0.0).then_inc(taken_ready, 1)
            for u in range(2):
                nc.vector.memset(patches[u][:, KP * PAIR:], 0.0)
                nc.vector.memset(QK[u][:], 0.0)
                nc.vector.memset(PR[u][:], 0.0)
                nc.vector.memset(positions[u][0:QKV_ROWS, LONG:], 0.0)
                steps.mark(nc.vector.memset(VB[u][:], 0.0))
            steps.wait()
            for u in range(2):
                nc.vector.memset(VB[u][0:SLOT, :, :, HD:HD + 1], 1.0)
                nc.vector.memset(VB[u][SLOT:P, :, :, VW - 1:VW], 1.0)
            ve.wait_ge(small_loaded, 16 * len(early))
            nc.vector.tensor_copy(count_earlier[:], cols("earlier"))
            nc.vector.tensor_copy(count_valid[:], cols("valid"))
            for u in range(2):
                nc.vector.tensor_scalar(row[u][:, D:D + 1], cols("token"), float(PAIR * (u - 2)), None, ALU.add)
            for m in range(4):
                steps.mark(nc.vector.tensor_scalar(rope_bias[:, m, :], cols("cos"), rope_b[:, m:m + 1], None, ALU.mult))
            steps.wait()
            for m in range(4):
                steps.mark(nc.vector.scalar_tensor_tensor(rope_bias[:, m, :], cols("sin"), rope_b[:, 4 + m:5 + m],
                                                          rope_bias[:, m, :], ALU.mult, ALU.add))
            steps.wait()
            ve.sem_inc(y_ready, 2)
            nc.vector.memset(r_left[0][:], 0.0).then_inc(vec_setup, 1)

            with ve.Fori(0, TILES // 2) as i:
                steps.begin(i, LOOP0_STEPS)
                k = i * 2 + 1
                for u in range(2):
                    t = i * 2 + u
                    ve.wait_ge(embedded, k + u)
                    steps.do(nc.vector.tensor_tensor(tile_of(t), bank(u, 0)[:, 0:D], tok_b[:], ALU.add))
                    statistics(steps, tile_of(t), u, var_ready)
                for u in range(2):
                    normalise(ve, steps, N[u][:], tile_of(i * 2 + u), u, dev_ready, k).then_inc(normed, 1)
                for u in range(2):
                    ve.wait_ge(qk_ready, k + u)
                    shape = [P, 8, S]
                    cos, sin = (cols(c).unsqueeze(1).to_broadcast(shape) for c in ("cos", "sin"))
                    flat = [x[u][:].rearrange("p m (i q) -> p (m i) q", i=2) for x in (rope_a, rope_s)]
                    src = [bank(u, b)[:, 0:8 * S].rearrange("p (m q) -> p m q", q=S) for b in (2, 3)]
                    steps.mark(nc.vector.tensor_tensor(flat[0], src[0], cos, ALU.mult))
                    steps.mark(nc.vector.tensor_tensor(flat[1], src[1], sin, ALU.mult))
                    steps.wait()
                    a, r = (x[u][:].rearrange("p m (i q) -> p m i q", i=2) for x in (rope_a, rope_s))
                    bias = rope_bias[:].unsqueeze(2).to_broadcast([P, 4, 2, S])
                    steps.do(nc.vector.tensor_tensor(a, a, bias, ALU.add))
                    steps.do(nc.vector.tensor_tensor(QK[u][:, :, :, 0:S], a, r, ALU.add))
                    key_blocks(steps, u).then_inc(kb_ready, 1)
                    ve.wait_ge(v_ready, k + u)
                    v = bank(u, 0).rearrange("p (i h o d) -> p i h o d", i=2, h=HP, o=2)
                    b = bv[:].rearrange("p (h o d) -> p h o d", h=HP, o=2)
                    for o in range(2):
                        lo, hi = SLOT * o, SLOT * o + SLOT
                        ins = nc.vector.tensor_tensor(VB[u][lo:hi, :, :, (HD + 1) * o:(HD + 1) * o + HD],
                                                      v[lo:hi, :, :, o, :], spread(b[lo:hi, :, o, :], 2), ALU.add)
                    ins.then_inc(vb_ready, 1)
                shifted_scores(ve, steps, k, True)
                head_results(ve, steps, k)
                for u in range(2):
                    t = i * 2 + u
                    ve.wait_ge(projected, k + u)
                    ve.wait_ge(bias_added, k + u)
                    steps.do(nc.vector.tensor_tensor(tile_of(t), bank(u, 1)[:, 0:D], tile_of(t), ALU.add))
                    statistics(steps, tile_of(t), u, var2_ready)
                for u in range(2):
                    ve.wait_ge(scattered[u], i * (16 * TOP0) + 16)
                    nc.vector.tensor_scalar(row[u][:, D:D + 1], row[u][:, D:D + 1], float(2 * PAIR), None, ALU.add)
                    normalise(ve, steps, row[u][:, 0:D], tile_of(i * 2 + u), u, dev2_ready, k).then_inc(normed2, 1)
                for u in range(2):
                    ve.wait_ge(routed, k + u)
                    ve.sem_inc(passed, 1)
                    steps.do(nc.vector.max(r_top[u][:], bank(u, 1)[:, 0:E0]))
                    nc.vector.tensor_scalar(r_neg[u][:], r_top[u][:, 0:1], -1.0, None, ALU.mult).then_inc(neg_ready, 1)
                for u in range(2):
                    ve.wait_ge(rexp_ready, k + u)
                    steps.do(nc.vector.reciprocal(r_inv[u][:], r_sum[u][:]))
                    steps.do(nc.vector.tensor_scalar(r_prob[u][:], r_exp[u][:], r_inv[u][:], None, ALU.mult))
                    ve.sem_inc(passed, 1)
                    steps.do(nc.vector.max(r_top[u][:], r_prob[u][:]))
                    ve.sem_inc(passed, 1)
                    steps.mark(nc.vector.match_replace(r_left[u][:], r_top[u][:], r_prob[u][:], -1.0))
                    steps.mark(nc.vector.max_index(r_index[u][:], r_top[u][:], r_prob[u][:]))
                    steps.do(nc.vector.tensor_reduce(r_sum[u][:], r_top[u][:], AX.X, ALU.add))
                    nc.vector.tensor_scalar(r_mask[u][:], r_left[u][:], 0.0, None, ALU.is_lt).then_inc(mask_ready, 1)
                    steps.mark(nc.vector.tensor_copy(r_expert[u][:], r_index[u][:]))
                    steps.do(nc.vector.reciprocal(r_inv[u][:], r_sum[u][:]))
                    ve.wait_ge(mask_ready, k + u)
                    steps.do(nc.vector.scalar_tensor_tensor(row[u][:, D + 1:ROW], r_mask[u][:], r_inv[u][:],
                                                            r_prob[u][:], ALU.mult, ALU.mult))
                for u in range(2):
                    ve.wait_ge(counted, k + u)
                    nc.vector.tensor_tensor(taken[:], taken[:], r_mask[u][:], ALU.add).then_inc(taken_ready, 1)
                    cnt = bank(u, 2)[:, 0:E0]
                    steps.mark(nc.vector.tensor_scalar(r_over[u][:], cnt, cols("pad_far"), float(CAP), ALU.add, ALU.is_ge))
                    steps.mark(nc.vector.tensor_tensor(r_slots[u][:], cnt, cols("slot_base"), ALU.add))
                    steps.do(nc.vector.tensor_tensor(r_pick[u][:], spread(cols("iota"), TOP0), repeat(r_expert[u][:], E0),
                                                     ALU.is_equal))
                    steps.do(nc.vector.scalar_tensor_tensor(r_slots[u][:], r_over[u][:], FAR, r_slots[u][:],
                                                            ALU.mult, ALU.add))
                    steps.do(nc.vector.tensor_tensor(r_pick[u][:], r_pick[u][:], spread(r_slots[u][:], TOP0), ALU.mult))
                    steps.do(nc.vector.tensor_reduce(r_slot[u][:], r_pick[u][:], AX.X, ALU.add))
                    nc.vector.tensor_copy(slot[u][:], r_slot[u][:]).then_inc(slots_ready, 1)
            steps.end(TILES // 2)

            def slot_tokens(e, i, u):
                ve.wait_ge(rows_loaded[u], i * 16 + 16)
                ve.wait_ge(y_ready, e + 1)
                nc.vector.tensor_copy(row_id[u][:], xrows[u][:, :, D:D + 1].rearrange("p c o -> p (c o)"))
                nc.vector.tensor_copy(row_w[u][:], xrows[u][:, :, bass.ds(e + (D + 1), 1)].rearrange("p c o -> p (c o)")
                                      ).then_inc(meta_ready, 1)

            def hidden(e, u):
                ve.wait_ge(silu_ready, e + 1)
                nc.vector.tensor_tensor(hid_a[u][:], silu_a[u][:], bank(u, 1)[:, CAP:2 * CAP], ALU.mult)
                nc.vector.tensor_tensor(hid_b[u][P - F0B:P, :], silu_b[u][P - F0B:P, :],
                                        bank(u, 2)[P - F0B:P, 0:CAP], ALU.mult).then_inc(hid_ready, 1)

            def weighted(e, i, u):
                ve.wait_ge(meta_ready, e + 1)
                steps.do(nc.vector.tensor_scalar(dest_f[u][:], row_id[u][:], 0.0, cols("empty_row"),
                                                 ALU.is_equal, ALU.mult))
                ve.wait_ge(added[0], i * 32 + 16 * u + 16)
                ve.wait_ge(added[1], i * 32 + 16 * u + 16)
                nc.vector.tensor_tensor(dest[u][:], dest_f[u][:], row_id[u][:], ALU.add)
                ve.wait_ge(down_ready, e + 1)
                for c in range(CT):
                    ins = nc.vector.tensor_scalar(y_rows[u][:, c, :], bank(u, 3)[:, c * D:(c + 1) * D],
                                                  row_w[u][:, c:c + 1], None, ALU.mult)
                ins.then_inc(y_ready, 1)

            slot_tokens(0, 0, 0)
            hidden(0, 0)
            slot_tokens(1, 0, 1)
            with ve.Fori(0, E0 // 2 - 1) as i:
                steps.begin(i, 2)
                for e, now, last in ((i * 2 + 1, 1, i), (i * 2 + 2, 0, i)):
                    hidden(e, now)
                    weighted(e - 1, last, 1 - now)
                    slot_tokens(e + 1, i + 1, 1 - now)
            steps.end(E0 // 2 - 1)
            hidden(E0 - 1, 1)
            weighted(E0 - 2, E0 // 2 - 1, 0)
            weighted(E0 - 1, E0 // 2 - 1, 1)

            def new_statistics(j, u):
                ve.wait_ge(summed, j * 2 + u + 1)
                statistics(steps, tile_of(j * 2 + u), u, var_ready)

            def new_rows(j, u):
                if j is not FIRST:
                    ve.wait_ge(residual_ready, j * 2 + (u - 1))
                normalise(ve, steps, N[u][:], tile_of(j * 2 + u), u, dev_ready, j * 2 + (TILES + 1)).then_inc(normed, 1)

            def add_qkv_bias(j, u):
                ve.wait_ge(qk_ready, j * 2 + (u + TILES + 1))
                src = psum[0:QKV_ROWS, 4 * u:4 * u + 4, 0:CG * PAIR].rearrange("p b (c x) -> p b c x", c=CG)
                dst = positions[u][0:QKV_ROWS, 0:LONG].rearrange("p (x b c) -> p b c x", b=4, c=CG)
                bias = repeat(bqkv1[:].rearrange("p (b c) -> p b c", b=4), PAIR)
                nc.vector.tensor_tensor(dst, src, bias, ALU.add).then_inc(qkv_ready, 1)

            def probabilities(j, u):
                ve.wait_ge(exped1, j * 2 + u + 1)
                pr = PR[u][:, :, 0:S]
                steps.do(nc.vector.tensor_reduce(den[u][:], pr, AX.X, ALU.add))
                steps.do(nc.vector.reciprocal(rden[u][:], den[u][:]))
                nc.vector.tensor_tensor(pr, pr, repeat(rden[u][:], S), ALU.mult).then_inc(probs_ready, 1)

            def finish_tile(j, u):
                n = j * 2 + u + 1
                ve.wait_ge(projected, n + TILES)
                ve.wait_ge(residual_ready, n)
                steps.do(nc.vector.tensor_tensor(Z[u][:], bank(u, 1)[:, 0:D], residual[u][:], ALU.add))
                statistics(steps, Z[u][:], u, var3_ready)
                steps.do(normalise(ve, steps, Z[u][:], Z[u][:], u, dev3_ready, j * 2 + 1))
                steps.do(nc.vector.tensor_tensor(Z[u][:], Z[u][:], gamma[:], ALU.mult))
                stream = tile_of(j * 2 + u)
                steps.do(nc.vector.tensor_tensor(stream, stream, Z[u][:], ALU.add))
                statistics(steps, stream, u, var2_ready)
                normalise(ve, steps, N3[u], stream, u, dev2_ready, j * 2 + (TILES + 1)).then_inc(normed2, 1)

            def attend_vector(j, u, more):
                (j1, u1), (j2, u2) = following(j, u)
                if more > 1:
                    new_statistics(j2, u2)
                probabilities(j, u)
                if more > 1:
                    new_rows(j2, u2)
                if more > 0:
                    add_qkv_bias(j1, u1)
                ve.wait_ge(attended1, j * 2 + u + 1)
                results_by_chunks(nc.vector.tensor_copy, u, 1).then_inc(high_ready, 1)
                finish_tile(j, u)
                if more > 0:
                    shift_tile(ve, steps, j1 * 2 + (u1 + TILES + 1), u1, False)
                ve.wait_ge(logits_ready, j * 2 + u + 1)
                nc.vector.tensor_copy(logits1[:, bass.ds(j * 2 + u, 1), :].rearrange("p o e -> p (o e)"),
                                      bank(u, 3)[:, 0:E1]).then_inc(logits_copied, 1)

            for u in range(2):
                new_statistics(FIRST, u)
            for u in range(2):
                new_rows(FIRST, u)
            add_qkv_bias(FIRST, 0)
            shift_tile(ve, steps, TILES + 1, 0, False)
            with ve.Fori(0, TILES // 2 - 1) as i:
                steps.begin(i, LOOP1_STEPS)
                for u in range(2):
                    attend_vector(i, u, 2)
            steps.end(TILES // 2 - 1)
            attend_vector(TILES // 2 - 1, 0, 1)
            attend_vector(TILES // 2 - 1, 1, 0)
            ve.wait_ge(logits_copied, TILES)
            nc.vector.memset(psum[:, 4:8, :], 0.0).then_inc(logits_copied, 1)

            ve.wait_ge(sig_ready, 1)
            steps.do(nc.vector.tensor_tensor(choice[:], sig1[:], spread(corr[:], TILES), ALU.add))
            quads = choice[:].rearrange("p t (g a b) -> p (t g) a b", g=2, a=2)
            a, b = quads[:, :, :, 0], quads[:, :, :, 1]
            steps.mark(nc.vector.tensor_tensor(pair_hi[:], a, b, ALU.max))
            steps.mark(nc.vector.tensor_tensor(pair_lo[:], a, b, ALU.min))
            steps.wait()
            steps.mark(nc.vector.tensor_tensor(best[:], pair_hi[:, :, 0:1], pair_hi[:, :, 1:2], ALU.max))
            steps.mark(nc.vector.tensor_tensor(second_a[:], pair_hi[:, :, 0:1], pair_hi[:, :, 1:2], ALU.min))
            steps.mark(nc.vector.tensor_tensor(second_b[:], pair_lo[:, :, 0:1], pair_lo[:, :, 1:2], ALU.max))
            steps.wait()
            steps.do(nc.vector.tensor_tensor(second_a[:], second_a[:], second_b[:], ALU.max))
            steps.do(nc.vector.tensor_tensor(best[:], best[:], second_a[:], ALU.add))
            g = best[:].rearrange("p (t g) o -> p t (g o)", g=2)
            steps.mark(nc.vector.tensor_tensor(group_sel[:, :, 0:1], g[:, :, 0:1], g[:, :, 1:2], ALU.is_ge))
            steps.mark(nc.vector.tensor_tensor(group_sel[:, :, 1:2], g[:, :, 0:1], g[:, :, 1:2], ALU.is_lt))
            steps.wait()
            groups = choice[:].rearrange("p t (g a) -> p (t g) a", g=2)
            steps.do(nc.vector.tensor_tensor(groups, groups, repeat(group_sel[:].rearrange("p t g -> p (t g)"), 4),
                                             ALU.mult))
            steps.do(nc.vector.tensor_scalar(choice[:], choice[:], 0.0, None, ALU.add))
            for t in range(TILES):
                steps.mark(nc.vector.max(sorted1[:, t, :], choice[:, t, :]))
            steps.wait()
            for t in range(TILES):
                steps.mark(nc.vector.max_index(index1[:, t, :], sorted1[:, t, :], choice[:, t, :]))
            steps.wait()
            steps.do(nc.vector.tensor_copy(index1f[:], index1[:, :, 0:TOP1]))
            full = [P, TILES * TOP1, E1]
            flat = picks1[:].rearrange("p t k e -> p (t k) e")
            chosen = index1f[:].rearrange("p t k -> p (t k)")
            steps.do(nc.vector.tensor_tensor(flat, cols("iota")[:, 0:E1].unsqueeze(1).to_broadcast(full),
                                             repeat(chosen, E1), ALU.is_equal))
            steps.do(nc.vector.tensor_tensor(picked1[:], picks1[:], sig1[:].unsqueeze(2).to_broadcast([P, TILES, TOP1, E1]),
                                             ALU.mult))
            steps.do(nc.vector.tensor_reduce(weight1[:], picked1[:], AX.X, ALU.add))
            steps.do(nc.vector.tensor_reduce(total1[:], weight1[:], AX.X, ALU.add))
            steps.do(nc.vector.tensor_scalar(total1[:], total1[:], 1e-20, None, ALU.add))
            steps.do(nc.vector.reciprocal(total1[:], total1[:]))
            steps.do(nc.vector.tensor_tensor(weight1[:], weight1[:], repeat(total1[:], TOP1), ALU.mult))
            steps.do(nc.vector.tensor_tensor(flat, flat, repeat(weight1[:].rearrange("p t k -> p (t k)"), E1), ALU.mult))
            nc.vector.tensor_tensor(comb1[:].rearrange("p e t -> p t e"), picks1[:, :, 0, :], picks1[:, :, 1, :],
                                    ALU.add).then_inc(comb_ready, 1)
            ve.wait_ge(comb_turned, 1)
            nc.vector.tensor_copy(comb_T[:], psum[0:E1 * TILES, 0, 0:P]).then_inc(comb_copied, 1)

            for h in range(2):
                ve.wait_ge(silu1_ready, h + 1)
                nc.vector.tensor_tensor(hid1[h][:].rearrange("p t i q -> p (t i) q")[:, :, 0:S],
                                        silu1[h][:].rearrange("p (m q) -> p m q", q=S),
                                        psum[:, 2 * h + 1, 0:HALF].rearrange("p (m q) -> p m q", q=S),
                                        ALU.mult).then_inc(hid1_ready, 1)
            ve.wait_ge(comb_loaded, 16)
            with ve.Fori(0, E1 // 2) as i:
                steps.begin(i, 4)
                for j in range(2):
                    for h in range(2):
                        n = i * 4 + (2 + 2 * j + h)
                        ve.wait_ge(silu1_ready, n + 1)
                        w = comb_b[:, bass.ds(i * (2 * TOKENS) + (j * TOKENS + h * HALF), HALF)]
                        steps.do(nc.vector.tensor_tensor(silu1[h][:], silu1[h][:], w, ALU.mult))
                        ve.wait_ge(down1_done, n - 1)
                        nc.vector.tensor_tensor(hid1[h][:].rearrange("p t i q -> p (t i) q")[:, :, 0:S],
                                                silu1[h][:].rearrange("p (m q) -> p m q", q=S),
                                                psum[:, 2 * h + 1, 0:HALF].rearrange("p (m q) -> p m q", q=S),
                                                ALU.mult).then_inc(hid1_ready, 1)
            steps.end(E1 // 2)
            ve.wait_ge(down1_done, 2 * (E1 + 1))
            for b in range(TILES // 2):
                pair = H[:, 2 * b:2 * b + 2, :].rearrange("p t f -> p (t f)")
                nc.vector.tensor_tensor(pair, psum[:, 4 + b, :], pair, ALU.add).then_inc(final_ready, 1)

        def softmax_scalar(act, k, ready):
            for u in range(2):
                act.wait_ge(shifted, k + u)
                nc.scalar.activation(PR[u][:, :, 0:S], SM[u][:], ACT.Exp, scale=SCALE).then_inc(ready, 1)
            for u in range(2):
                act.wait_ge(prt_psum, k + u)
                nc.scalar.copy(PRT[u][:].rearrange("p (b h) q -> p b (h q)", b=2), scores(u)).then_inc(prt_ready, 1)

        def deviation(act, k, var, ready):
            for u in range(2):
                act.wait_ge(var, k + u)
                nc.scalar.activation(dev[u][:], moments[u][:, 1:2], ACT.Sqrt, bias=cols("eps")).then_inc(ready, 1)

        def evacuate(act, k, dst, b, width, psum_ready, ready):
            for u in range(2):
                act.wait_ge(psum_ready, k + u)
                nc.scalar.copy(dst[u], bank(u, b)[:, 0:width]).then_inc(ready, 1)

        @block.scalar
        def _(act):
            nt = [x[:].rearrange("p k q -> p (k q)") for x in NT]
            cxt = [x[:].rearrange("p k q -> p (k q)") for x in CXT]
            act.wait_ge(vec_setup, 1)
            with act.Fori(0, TILES // 2) as i:
                k = i * 2 + 1
                deviation(act, k, var_ready, dev_ready)
                evacuate(act, k, nt, 1, D, transposed, NT_ready)
                softmax_scalar(act, k, exped)
                evacuate(act, k, cxt, 0, D, cx_transposed, cxt_ready)
                deviation(act, k, var2_ready, dev2_ready)
                evacuate(act, k, nt, 0, D, transposed2, NT2_ready)
                for u in range(2):
                    act.wait_ge(neg_ready, k + u)
                    nc.scalar.activation(r_exp[u][:], bank(u, 1)[:, 0:E0], ACT.Exp, bias=r_neg[u][:],
                                         accum_out=r_sum[u][:]).then_inc(rexp_ready, 1)
            nc.scalar.activation(dev[0][:], cols("eps"), ACT.Silu)
            with act.Fori(0, E0 // 2) as i:
                k = i * 2 + 1
                for u in range(2):
                    act.wait_ge(rows_transposed, k + u)
                    nc.scalar.copy(xT[u][:].rearrange("p k c -> p (k c)"), bank(u, 0)).then_inc(xT_ready, 1)
                    act.wait_ge(gu_ready, k + u)
                    nc.scalar.activation(silu_a[u][:], bank(u, 1)[:, 0:CAP], ACT.Silu)
                    nc.scalar.activation(silu_b[u][P - F0B:P, :], bank(u, 2)[0:F0B, 0:CAP],
                                         ACT.Silu).then_inc(silu_ready, 1)
            def root(n, u, var, ready):
                act.wait_ge(var, n)
                nc.scalar.activation(dev[u][:], moments[u][:, 1:2], ACT.Sqrt, bias=cols("eps")).then_inc(ready, 1)

            def copy_turned(n, dst, src, psum_ready, ready):
                act.wait_ge(psum_ready, n)
                nc.scalar.copy(dst, src[:, 0:D]).then_inc(ready, 1)

            def keys(j, u):
                act.wait_ge(qkv_ready, j * 2 + u + 1)
                nc.scalar.copy(KP1[u][0:HD, :], positions[u][32:32 + HD, 0:LONG]).then_inc(keys_ready, 1)

            def values(j, u):
                act.wait_ge(values_turned, j * 2 + u + 1)
                v = bank(u, 0)[:, 0:D].rearrange("p (i h d) -> p i h d", i=2, h=HP)
                for o in range(2):
                    lo, hi = SLOT * o, SLOT * o + SLOT
                    ins = nc.scalar.copy(VB[u][lo:hi, :, :, (HD + 1) * o:(HD + 1) * o + HD], v[lo:hi])
                ins.then_inc(values_ready, 1)

            def exponentials(j, u):
                act.wait_ge(shifted, j * 2 + (u + TILES + 1))
                nc.scalar.activation(PR[u][:, :, 0:S], SM[u][:], ACT.Exp, scale=SCALE).then_inc(exped1, 1)

            def attend_scalar(j, u, more):
                (j1, u1), (j2, u2) = following(j, u)
                n = j * 2 + u + 1
                if more > 1:
                    root(j2 * 2 + (u2 + TILES + 1), u2, var_ready, dev_ready)
                act.wait_ge(prt_psum, n + TILES)
                nc.scalar.copy(PRT[u][:].rearrange("p (b h) q -> p b (h q)", b=2), scores(u)).then_inc(prt_ready, 1)
                if more > 0:
                    keys(j1, u1)
                act.wait_ge(attended1, n)
                results_by_chunks(nc.scalar.copy, u, 0).then_inc(low_ready, 1)
                root(n, u, var3_ready, dev3_ready)
                if more > 0:
                    values(j1, u1)
                root(n + TILES, u, var2_ready, dev2_ready)
                copy_turned(n + TILES, cxt[u], bank(u, 0), transposed2, NT2_ready)
                if more > 1:
                    copy_turned(j2 * 2 + (u2 + TILES + 1), nt[u2], bank(u2, 1), transposed, NT_ready)
                rows = CXT[u][:].rearrange("p k (i q) -> p k i q", i=2)
                act.wait_ge(NT2_ready, n + TILES)
                for f in range(KD):
                    nc.scalar.copy(N3T[:, f, bass.ds(j * (2 * PAIR) + PAIR * u, PAIR)].rearrange(
                        "p (i q) -> p i q", i=2), rows[:, f, :, 0:S])
                if more > 0:
                    exponentials(j1, u1)

            for u in range(2):
                root(u + TILES + 1, u, var_ready, dev_ready)
            for u in range(2):
                copy_turned(u + TILES + 1, nt[u], bank(u, 1), transposed, NT_ready)
            keys(FIRST, 0)
            values(FIRST, 0)
            exponentials(FIRST, 0)
            with act.Fori(0, TILES // 2 - 1) as i:
                for u in range(2):
                    attend_scalar(i, u, 2)
            attend_scalar(TILES // 2 - 1, 0, 1)
            attend_scalar(TILES // 2 - 1, 1, 0)
            act.wait_ge(logits_copied, TILES + 1)
            nc.scalar.activation(sig1[:], logits1[:], ACT.Sigmoid).then_inc(sig_ready, 1)
            for h in range(2):
                act.wait_ge(gu1_ready, h + 1)
                nc.scalar.activation(silu1[h][:], psum[:, 2 * h, 0:HALF], ACT.Silu).then_inc(silu1_ready, 1)
            with act.Fori(0, E1 // 2) as i:
                for j in range(2):
                    for h in range(2):
                        act.wait_ge(gu1_ready, i * 4 + (3 + 2 * j + h))
                        nc.scalar.activation(silu1[h][:], psum[:, 2 * h, 0:HALF], ACT.Silu).then_inc(silu1_ready, 1)

        @block.gpsimd
        def _(pool):
            nc.gpsimd.memset(zeros[:], 0.0).then_inc(pool_step, 1)
            for u in range(2):
                nc.gpsimd.memset(hid1[u][:], 0.0)
                ins = nc.gpsimd.memset(sums[u][:], 0.0)
            ins.then_inc(pool_setup, 1)
            pool.wait_ge(pool_step, 1)
            span = zeros.shape[1]
            half = E0 * CAP // 2
            reps = half * ROW // P // span
            for u in range(2):
                dst = table[half * u:half * (u + 1), :].rearrange("(p r) x -> p (r x)", p=P)
                pool.dma_start(dst.rearrange("p (a b) -> p a b", b=span), spread(zeros[:], reps)).then_inc(scattered[u], 16)
            for c in range(CT):
                top_rows = ACC_ROWS // P * P
                pool.dma_start(acc[c][0:top_rows, :].rearrange("(p r) f -> p r f", p=P),
                               spread(zeros[:, 0:D], top_rows // P)).then_inc(added[c], 16)
                pool.dma_start(acc[c][top_rows:ACC_ROWS, :], zeros[0:ACC_ROWS - top_rows, 0:D]).then_inc(added[c], 16)
            for u in range(2):
                pool.wait_ge(scattered[u], 16)
            pool.wait_ge(small_loaded, 16 * len(early))
            with pool.Fori(0, TILES // 2) as i:
                k = i * 2 + 1
                for u in range(2):
                    t = i * 2 + u
                    pool.wait_ge(normed, k + u)
                    nc.gpsimd.tensor_tensor(tile_of(t), tile_of(t), bo[:], ALU.add).then_inc(bias_added, 1)
                for u in range(2):
                    pool.wait_ge(slots_ready, k + u)
                    pool.sem_inc(passed, 1)
                    for j in range(TOP0):
                        pool.indirect_dma_start(table, bass.IndirectOffsetOnAxis(ap=slot[u][:, j:j + 1], axis=0),
                                                row[u][:], None, bounds_check=E0 * CAP - 1,
                                                oob_is_err=False).then_inc(scattered[u], 16)
            with pool.Fori(0, E0 // 2) as i:
                for u in range(2):
                    pool.wait_ge(y_ready, i * 2 + u + 3)
                    for c in range(CT):
                        pool.wait_ge(added[c], i * 32 + (16 * u + 32))
                        pool.sem_inc(passed, 1)
                        pool.indirect_dma_start(acc[c], bass.IndirectOffsetOnAxis(ap=dest[u][:, c:c + 1], axis=0),
                                                y_rows[u][:, c, :], None, bounds_check=ACC_ROWS - 1,
                                                compute_op=ALU.add, oob_is_err=True).then_inc(added[c], 16)
            pool.wait_ge(late_loaded, 16 * len(late))

            def add_sums(j, u):
                pool.wait_ge(sums_loaded[u], j * (32 * CT) + 32 * CT)
                t = j * 2 + u
                nc.gpsimd.tensor_tensor(sums[u][:, 0, :], sums[u][:, 0, :], sums[u][:, 1, :], ALU.add
                                        ).then_inc(pool_step, 1)
                pool.wait_ge(pool_step, t + 2)
                nc.gpsimd.tensor_tensor(tile_of(t), tile_of(t), sums[u][:, 0, :], ALU.add).then_inc(summed, 1)

            def add_residual(j, u):
                t = j * 2 + u
                pool.wait_ge(normed, t + (TILES + 1))
                pool.wait_ge(normed2, t + (TILES - 1))
                nc.gpsimd.tensor_tensor(residual[u][:], N[u][:], bo1[:], ALU.add)
                nc.gpsimd.tensor_tensor(tile_of(t), tile_of(t), beta[:], ALU.add).then_inc(residual_ready, 1)

            for u in range(2):
                add_sums(FIRST, u)
            add_residual(FIRST, 0)
            with pool.Fori(0, TILES // 2 - 1) as i:
                for u in range(2):
                    (j1, u1), (j2, u2) = following(i, u)
                    add_sums(j2, u2)
                    add_residual(j1, u1)
            add_residual(TILES // 2 - 1, 1)

        def product(dst, terms):
            for n, (a, b) in enumerate(terms):
                mm = nc.tensor.matmul(dst, a, b, start=(n == 0), stop=(n == len(terms) - 1))
            return mm

        def turn(pe, k, src, b, ready, done):
            for u in range(2):
                pe.wait_ge(ready, k + u)
                for g in range(src[u].shape[1] // P):
                    mm = nc.tensor.transpose(bank(u, b)[:, g * P:(g + 1) * P], src[u][:, g * P:(g + 1) * P], cols("ident"))
                mm.then_inc(done, 1)

        def turn_probs(pe, k, ready):
            for u in range(2):
                turn_probs_tile(pe, k + u, u, ready)

        def turn_probs_tile(pe, n, u, ready):
            pe.wait_ge(ready, n)
            for hp in range(HP):
                mm = nc.tensor.transpose(scores(u)[:, hp // 4, (hp % 4) * P:(hp % 4 + 1) * P],
                                         PR[u][:, 2 * hp:2 * hp + 2, :].rearrange("p h q -> p (h q)"), cols("ident"))
            mm.then_inc(prt_psum, 1)

        def attention_tensor(pe, k):
            for u in range(2):
                pe.wait_ge(kb_ready, k + u)
                for g in range(KD):
                    for im in range(2):
                        mm = product(scores(u)[SLOT * im:SLOT * im + SLOT, g, 0:HG * S],
                                     [(QK[u][:, g, im, :], KB[u][:, 2 * g + im, :, :].rearrange("p h q -> p (h q)"))])
                mm.then_inc(scored, 1)
            turn_probs(pe, k, exped)
            for u in range(2):
                pe.wait_ge(prt_ready, k + u)
                pe.wait_ge(vb_ready, k + u)
                for hp in range(HP):
                    for im in range(2):
                        mm = product(bank(u, 1)[SLOT * im:SLOT * im + SLOT, hp * VW:(hp + 1) * VW],
                                     [(PRT[u][:, hp, SLOT * im:SLOT * im + SLOT], VB[u][:, im, hp, :])])
                mm.then_inc(attended, 1)

        def project(pe, k, w):
            for u in range(2):
                pe.wait_ge(cxt_ready, k + u)
                product(bank(u, 1)[:, 0:D], [(CXT[u][:, g, :], w[:, g, :]) for g in range(KD)]).then_inc(projected, 1)

        @block.tensor
        def _(pe):
            pe.wait_ge(small_loaded, 16 * len(early))
            pe.wait_ge(vec_setup, 1)
            pe.wait_ge(pool_setup, 1)
            with pe.Fori(0, TILES // 2) as i:
                k = i * 2 + 1
                for u in range(2):
                    pe.wait_ge(patches_loaded[u], i * 16 + 16)
                    for im in range(2):
                        mm = product(bank(u, 0)[SLOT * im:SLOT * im + SLOT, 0:D],
                                     [(patches[u][:, kp * PAIR + S * im:kp * PAIR + S * im + SLOT], tok_w[:, kp, :])
                                      for kp in range(KP)])
                    mm.then_inc(embedded, 1)
                turn(pe, k, [x[:] for x in N], 1, normed, transposed)
                for u in range(2):
                    pe.wait_ge(NT_ready, k + u)
                    tokens = [NT[u][:, f, :].rearrange("p (i q) -> p i q", i=2)[:, :, 0:S] for f in range(KD)]
                    for half in range(2):
                        for m in range(4):
                            c = (4 * half + m) * P
                            mm = product(bank(u, 2 + half)[:, m * PAIR:(m + 1) * PAIR].rearrange("p (i q) -> p i q", i=2),
                                         [(wqk[:, f, c:c + P], tokens[f]) for f in range(KD)])
                    mm.then_inc(qk_ready, 1)
                    for im in range(2):
                        for o in range(2):
                            mm = product(bank(u, 0)[SLOT * o:SLOT * o + SLOT, im * D:(im + 1) * D],
                                         [(NT[u][:, f, SLOT * im:SLOT * im + SLOT], wv[:, f, :]) for f in range(KD)])
                    mm.then_inc(v_ready, 1)
                attention_tensor(pe, k)
                turn(pe, k, [x[:].rearrange("p h d -> p (h d)") for x in CX], 0, cx_ready, cx_transposed)
                project(pe, k, wo)
                turn(pe, k, [x[:, 0:D] for x in row], 0, normed2, transposed2)
                for u in range(2):
                    pe.wait_ge(NT2_ready, k + u)
                    product(bank(u, 1)[:, 0:E0], [(NT[u][:, f, :], gate_w[:, f, :]) for f in range(KD)]).then_inc(routed, 1)
                for u in range(2):
                    pe.wait_ge(mask_ready, k + u)
                    pe.wait_ge(taken_ready, k + u)
                    product(bank(u, 2)[:, 0:E0], [(count_earlier[:], r_mask[u][:]), (count_valid[:], taken[:])]
                            ).then_inc(counted, 1)
            def turn_rows(i, u):
                pe.wait_ge(rows_loaded[u], i * 16 + 16)
                for f in range(KD):
                    for c in range(CT):
                        mm = nc.tensor.transpose(bank(u, 0)[:, f * CAP + c * P:f * CAP + (c + 1) * P],
                                                 xrows[u][:, c, f * P:(f + 1) * P], cols("ident"))
                mm.then_inc(rows_transposed, 1)

            def expert_gate_up(e, i, u):
                pe.wait_ge(gu_loaded[u], i * 16 + 16)
                pe.wait_ge(xT_ready, e + 1)
                for b, c, m in ((1, 0, 0), (1, CAP, 2 * P), (2, 0, P)):
                    mm = product(bank(u, b)[:, c:c + CAP],
                                 [(gu_w[u][:, f, m:m + P], xT[u][:, f, :]) for f in range(KD)])
                mm.then_inc(gu_ready, 1)

            def expert_down(e, i, u):
                pe.wait_ge(dn_loaded[u], i * 32 + 32)
                pe.wait_ge(hid_ready, e + 1)
                pe.wait_ge(y_ready, e + 1)
                for c in range(CT):
                    mm = product(bank(u, 3)[:, c * D:(c + 1) * D],
                                 [(hid_a[u][:, c * P:(c + 1) * P], dn_w[u][:, 0, :]),
                                  (hid_b[u][P - F0B:P, c * P:(c + 1) * P], dn_w[u][P - F0B:P, 1, :])])
                mm.then_inc(down_ready, 1)

            turn_rows(0, 0)
            expert_gate_up(0, 0, 0)
            turn_rows(0, 1)
            with pe.Fori(0, E0 // 2 - 1) as i:
                for e, now, at in ((i * 2 + 1, 1, i), (i * 2 + 2, 0, i + 1)):
                    expert_gate_up(e, at, now)
                    turn_rows(i + 1, 1 - now)
                    expert_down(e - 1, i, 1 - now)
            expert_gate_up(E0 - 1, E0 // 2 - 1, 1)
            expert_down(E0 - 2, E0 // 2 - 1, 0)
            expert_down(E0 - 1, E0 // 2 - 1, 1)
            pe.wait_ge(late_loaded, 16 * len(late))
            def turn_tile(n, u, src, b, ready, done):
                pe.wait_ge(ready, n)
                for g in range(KD):
                    mm = nc.tensor.transpose(bank(u, b)[:, g * P:(g + 1) * P], src[:, g * P:(g + 1) * P], cols("ident"))
                mm.then_inc(done, 1)

            def qkv_by_chunks(j, u):
                pe.wait_ge(NT_ready, j * 2 + (u + TILES + 1))
                tokens = [NT[u][:, f, :].rearrange("p (i q) -> p i q", i=2)[:, :, 0:S] for f in range(KD)]
                for c in range(CH):
                    if c == 3 * CG and j is not FIRST:
                        pe.wait_ge(logits_copied, j * 2 + (u - 1))
                    at = c % CG * PAIR
                    mm = product(bank(u, c // CG)[0:QKV_ROWS, at:at + PAIR].rearrange("p (i q) -> p i q", i=2),
                                 [(wqkv1[:, f, c, :], tokens[f]) for f in range(KD)])
                mm.then_inc(qk_ready, 1)

            def turn_values_and_score(j, u):
                pe.wait_ge(qkv_ready, j * 2 + u + 1)
                pe.sem_inc(passed, 1)
                for im in range(2):
                    for h in range(HEADS):
                        lo, at = SLOT * (h % 2), (im * HEADS + h) * S
                        mm = product(bank(u, 0)[lo:lo + SLOT, (im * HP + h // 2) * HD:(im * HP + h // 2 + 1) * HD],
                                     [(positions[u][SLOT:SLOT + HD, at:at + SLOT],
                                       cols("ident")[SLOT:SLOT + HD, SLOT:SLOT + HD])])
                mm.then_inc(values_turned, 1)
                pe.wait_ge(keys_ready, j * 2 + u + 1)
                pe.sem_inc(passed, 1)
                for im in range(2):
                    for h in range(HEADS):
                        at = (im * HEADS + h) * S
                        mm = product(scores(u)[SLOT * im:SLOT * im + SLOT, h // HG, h % HG * S:(h % HG + 1) * S],
                                     [(positions[u][0:HD, at:at + SLOT], KP1[u][0:HD, at:at + S])])
                mm.then_inc(scored, 1)

            def attend_tensor(j, u, more):
                (j1, u1), (j2, u2) = following(j, u)
                n = j * 2 + u + 1
                turn_probs_tile(pe, n, u, probs_ready)
                pe.wait_ge(prt_ready, n + TILES)
                pe.wait_ge(values_ready, n)
                pe.sem_inc(passed, 1)
                for im in range(2):
                    for h in range(HEADS):
                        mm = product(bank(u, 2 * (h // HG) + im)[0:HD, h % HG * S:(h % HG + 1) * S],
                                     [(VB[u][:, im, h // 2, (HD + 1) * (h % 2):(HD + 1) * (h % 2) + HD],
                                       PRT[u][:, h // 2, SLOT * im:SLOT * im + S])])
                mm.then_inc(attended1, 1)
                pe.wait_ge(low_ready, n)
                pe.wait_ge(high_ready, n)
                product(bank(u, 1)[:, 0:D], [(CT1[u][:, c, :], wo1[:, c, :]) for c in range(CG)]).then_inc(projected, 1)
                if more > 0:
                    turn_values_and_score(j1, u1)
                turn_tile(n + TILES, u, N3[u], 0, normed2, transposed2)
                if more > 1:
                    turn_tile(j2 * 2 + (u2 + TILES + 1), u2, N[u2], 1, normed, transposed)
                pe.wait_ge(NT2_ready, n + TILES)
                product(bank(u, 3)[:, 0:E1], [(CXT[u][:, f, :], router_w[:, f, :]) for f in range(KD)]
                        ).then_inc(logits_ready, 1)
                if more > 1:
                    qkv_by_chunks(j2, u2)

            for u in range(2):
                turn_tile(u + TILES + 1, u, N[u], 1, normed, transposed)
            qkv_by_chunks(FIRST, 0)
            turn_values_and_score(FIRST, 0)
            qkv_by_chunks(FIRST, 1)
            with pe.Fori(0, TILES // 2 - 1) as i:
                for u in range(2):
                    attend_tensor(i, u, 2)
            attend_tensor(TILES // 2 - 1, 0, 1)
            attend_tensor(TILES // 2 - 1, 1, 0)
            pe.wait_ge(comb_ready, 1)
            nc.tensor.transpose(psum[0:E1 * TILES, 0, 0:P], comb1[:].rearrange("p e t -> p (e t)"), cols("ident")
                                ).then_inc(comb_turned, 1)
            pe.wait_ge(comb_copied, 1)

            def gate_up(buf, h):
                for m in range(2):
                    mm = product(psum[:, 2 * h + m, 0:HALF],
                                 [(wgu1[buf][:, f, m * I1:(m + 1) * I1], N3T[:, f, h * HALF:(h + 1) * HALF])
                                  for f in range(KD)])
                mm.then_inc(gu1_ready, 1)

            def down(buf, h):
                for t in range(HT):
                    at = h * HT + t
                    mm = nc.tensor.matmul(psum[:, 4 + at // 2, (at % 2) * D:(at % 2 + 1) * D],
                                          hid1[h][:, t, :, :].rearrange("p i q -> p (i q)"), wd1[buf][:],
                                          start=False, stop=True, skip_group_check=True)
                mm.then_inc(down1_done, 1)

            pe.wait_ge(w1_loaded[0], 32)
            gate_up(0, 0)
            gate_up(0, 1)
            pe.wait_ge(hid1_ready, 1)
            down(0, 0)
            with pe.Fori(0, E1 // 2) as i:
                for j, buf in ((0, 1), (1, 0)):
                    n = i * 4 + (2 + 2 * j)
                    pe.wait_ge(w1_loaded[buf], i * 32 + (32 if buf else 64))
                    gate_up(buf, 0)
                    pe.wait_ge(hid1_ready, n)
                    down(1 - buf, 1)
                    gate_up(buf, 1)
                    pe.wait_ge(hid1_ready, n + 1)
                    down(buf, 0)
            pe.wait_ge(hid1_ready, 2 * (E1 + 1))
            down(0, 1)


_OUT = (IMAGES, S, D)


def _layout(a):
    def k_rows(w):
        return np.ascontiguousarray(w.reshape(w.shape[0] // P, P, -1).transpose(1, 0, 2))

    def by_chunks(q, k, v):
        w = np.zeros((q.shape[0], CH, QKV_ROWS), np.float32)
        for n, x in enumerate((q, k, v)):
            w[:, :, 32 * n:32 * n + HD] = x.reshape(-1, CH, HD)
        return w

    x = a["x"].reshape(TILES, 2, 3, 7, 16, 7, 16).transpose(0, 2, 4, 6, 1, 3, 5).reshape(TILES, KP, P, PAIR)
    wqkv, bqkv = a["L0_attn_w_qkv"], a["L0_attn_b_qkv"]
    swap = np.arange(2 * D) ^ 1
    wqk = np.concatenate([wqkv[:2 * D], wqkv[:2 * D][swap]], axis=0).T
    rope_b = np.concatenate([bqkv[:2 * D], bqkv[:2 * D][swap]]).reshape(8, P).T
    order = np.concatenate([np.arange(P), np.arange(P, F0), np.arange(F0 + P, 2 * F0), np.arange(F0, F0 + P)])
    gu = a["L0_ffn_gate_up_proj"][:, order, :].transpose(0, 2, 1).reshape(E0, KD, P, 2 * F0).transpose(0, 2, 1, 3)
    wo1 = np.zeros((4, 32, CG, D), np.float32)
    wo1[:, :HD] = a["L1_attn_wo"].reshape(4, CG, HD, D).transpose(0, 2, 1, 3)
    gate = np.concatenate([a["L1_ffn_sw_gate"][None], a["L1_ffn_w_gate"]])
    up = np.concatenate([a["L1_ffn_sw_up"][None], a["L1_ffn_w_up"]])
    gu1 = np.concatenate([gate, up], axis=2).reshape(E1 + 1, KD, P, 2 * I1).transpose(0, 2, 1, 3)
    return {
        "const": constants(),
        "patches": x.transpose(0, 2, 1, 3).reshape(TILES, P, KP * PAIR),
        "tok_w": k_rows(a["L0_tok_W"]), "tok_b": a["L0_tok_b"],
        "wqk": k_rows(wqk), "rope_b": rope_b,
        "wv": k_rows(wqkv[2 * D:].T), "bv": bqkv[2 * D:],
        "wo": k_rows(a["L0_attn_w_out"].T), "bo": a["L0_attn_b_out"],
        "gate_w": k_rows(a["L0_ffn_gate_weight"].T),
        "gu_w": gu, "dn_w": a["L0_ffn_down_proj"].transpose(0, 2, 1),
        "wqkv1": k_rows(by_chunks(a["L1_attn_wq"], a["L1_attn_wk"], a["L1_attn_wv"])).reshape(P, KD, CH, QKV_ROWS),
        "bqkv1": by_chunks(*(a[n][None] for n in ("L1_attn_bq", "L1_attn_bk", "L1_attn_bv")))[0].T,
        "wo1": wo1.reshape(P, CG, D), "bo1": a["L1_attn_bo"],
        "gamma": a["L1_attn_gamma"], "beta": a["L1_attn_beta"],
        "router_w": k_rows(a["L1_ffn_router_weight"].T), "corr": a["L1_ffn_correction_bias"],
        "wgu1": gu1, "wd1": np.concatenate([a["L1_ffn_sw_down"][None], a["L1_ffn_w_down"]]),
    }


def kernel(**inputs):
    import concourse.bacc as bacc
    from concourse.bass_utils import run_bass_kernel_spmd

    nc = bacc.Bacc("TRN2", target_bir_lowering=False, num_devices=1)
    laid = {n: np.ascontiguousarray(v) for n, v in _layout({n: np.asarray(v) for n, v in inputs.items()}).items()}
    arrays = {f"in_{n}": v for n, v in laid.items()}
    dram = {n: nc.dram_tensor(f"in_{n}", list(v.shape), F32, kind="ExternalInput").ap() for n, v in laid.items()}
    out = nc.dram_tensor("out_0", list(_OUT), F32, kind="ExternalOutput").ap()
    vit_tower(nc, dram, out)
    r = run_bass_kernel_spmd(nc, [arrays], core_ids=[0])
    return r.results[0]["out_0"]
```

```python
from contextlib import ExitStack

import numpy as np

import concourse.bass as bass
from concourse import mybir

F32 = mybir.dt.float32
F32R = mybir.dt.float32r
BF16 = mybir.dt.bfloat16
I32 = mybir.dt.int32
U32 = mybir.dt.uint32
ALU = mybir.AluOpType
ACT = mybir.ActivationFunctionType
AX = mybir.AxisListType

P = 128
IMAGES, S, D = 16, 49, 256
TOKENS = IMAGES * S
TILES = IMAGES // 2
PAIR = 2 * S
SLOT = 64
PATCH = 768
KP = PATCH // P
KD = D // P
HEADS, HD = 16, 16
HG = HEADS // KD
SCALE = HD ** -0.5
HP = HEADS // 2
VW = 2 * (HD + 1)
EPS = 1e-5

E0, TOP0, CAP, F0 = 32, 8, 256, 192
CT = CAP // P
F0B = F0 - P
ROW = D + 1 + E0
FAR = float(1 << 20)
ACC_ROWS = TOKENS + 1 + P

E1, TOP1, I1 = 8, 2, 128
CH = D // HD
QKV_ROWS = SLOT + HD
LONG = PAIR * CH
CG = CH // 4
HALF = TOKENS // 2
HT = TILES // 2

LOOP0_STEPS = 60
LOOP1_STEPS = 26

_AT = {}
_WIDTH = 0
for _name, _w in (("ident", P), ("head_mask", HG), ("causal", S), ("cos", S), ("sin", S), ("earlier", P),
                  ("valid", P), ("pad_far", 1), ("slot_base", E0), ("iota", E0), ("token", 1),
                  ("empty_row", 1), ("eps", 1)):
    _AT[_name] = (_WIDTH, _WIDTH + _w)
    _WIDTH += _w


def constants():
    c = np.zeros((P, _WIDTH), np.float32)

    def put(name, a):
        lo, hi = _AT[name]
        c[:, lo:hi] = a

    p = np.arange(P)
    pos, valid = p % SLOT, (p % SLOT) < S
    put("ident", np.eye(P))
    put("head_mask", (p[:, None] // HD) == np.arange(HG)[None, :])
    put("causal", np.where(np.arange(S)[None, :] <= pos[:, None], 0.0, -1e30))
    freq = (np.float32(10000.0) ** (-np.arange(0, HD, 2, dtype=np.float32) / np.float32(HD))).astype(np.float32)
    ang = np.arange(S, dtype=np.float32)[None, :] * freq[(p % HD) // 2][:, None]
    put("cos", np.cos(ang))
    put("sin", np.sin(ang) * np.where(p % 2 == 0, -1.0, 1.0)[:, None])
    put("earlier", valid[:, None] & (p[:, None] < p[None, :]))
    put("valid", np.repeat(valid[:, None], P, axis=1))
    put("pad_far", np.where(valid, 0.0, FAR)[:, None])
    put("slot_base", CAP * np.arange(E0)[None, :])
    put("iota", np.arange(E0)[None, :])
    put("token", (pos + S * (p // SLOT) + 1)[:, None])
    put("empty_row", (TOKENS + 1 + p)[:, None])
    put("eps", EPS)
    return c


class Steps:

    def __init__(self, eng, sem):
        self.eng, self.sem, self.total = eng, sem, 0
        self.base, self.n = 0, 0

    def begin(self, i, per_pass):
        self.total += self.n
        self.base, self.n, self.per_pass = self.total + i * per_pass, 0, per_pass

    def end(self, passes):
        assert self.n == self.per_pass, f"{self.n} steps in a pass"
        self.total += passes * self.n
        self.base, self.n = self.total, 0

    def do(self, instruction):
        self.mark(instruction)
        self.wait()

    def mark(self, instruction):
        instruction.then_inc(self.sem, 1)
        self.n += 1

    def wait(self):
        self.eng.wait_ge(self.sem, self.base + self.n)


def vit_tower(nc, dram, out):
    ctx = ExitStack()
    with ctx:
        def sb(name, shape, dt=F32):
            return ctx.enter_context(nc.sbuf_tensor(name, shape, dt))

        def two(name, shape, dt=F32):
            return [sb(f"{name}{u}", shape, dt) for u in range(2)]

        def sem(name):
            return ctx.enter_context(nc.semaphore(name))

        def sem2(name):
            return [sem(f"{name}{u}") for u in range(2)]

        def cols(name):
            lo, hi = _AT[name]
            return const[:, lo:hi]

        def spread(ap, n):
            return ap.unsqueeze(1).to_broadcast([ap.shape[0], n] + list(ap.shape[1:]))

        def repeat(ap, n):
            return ap.unsqueeze(len(ap.shape)).to_broadcast(list(ap.shape) + [n])

        table = nc.dram_tensor("expert_rows", [E0 * CAP, ROW], F32, kind="Internal").ap()
        acc = [nc.dram_tensor(f"expert_sums{c}", [ACC_ROWS, D], F32, kind="Internal").ap() for c in range(CT)]
        comb_flat = nc.dram_tensor("comb_flat", [E1 * TILES, 2, S], F32, kind="Internal").ap()

        const = sb("const", [P, _WIDTH])
        count_earlier = sb("count_earlier", [P, P], BF16)
        count_valid = sb("count_valid", [P, P], BF16)
        zeros = sb("zeros", [P, 2 * ROW])
        tok_w = sb("tok_w", [P, KP, D])
        tok_b = sb("tok_b", [P, D])
        wqk = sb("wqk", [P, KD, 4 * D])
        rope_b = sb("rope_b", [P, 8])
        rope_bias = sb("rope_bias", [P, 4, S])
        wv = sb("wv", [P, KD, D])
        bv = sb("bv", [P, D])
        wo = sb("wo", [P, KD, D])
        bo = sb("bo", [P, D])
        gate_w = sb("gate_w", [P, KD, E0])
        wqkv1 = sb("wqkv1", [P, KD, CH, QKV_ROWS])
        bqkv1 = sb("bqkv1", [QKV_ROWS, CH])
        wo1 = sb("wo1", [P, CG, D])
        bo1 = sb("bo1", [P, D])
        gamma = sb("gamma", [P, D])
        beta = sb("beta", [P, D])
        router_w = sb("router_w", [P, KD, E1])
        corr = sb("corr", [P, E1])
        H = sb("H", [P, TILES, D])
        taken = sb("taken", [P, E0], BF16)
        patches = two("patches", [P, KP, 2 * SLOT])
        stats = two("stats", [P, 6])
        moments = two("moments", [P, 2])
        dev = two("dev", [P, 1])
        rstd = two("rstd", [P, 1])
        table_of = sb("table_of", [P, 1])
        N = two("N", [P, D])
        NT = two("NT", [P, KD, P])
        room = sb("room", [P, E1 * TOKENS])
        room_used = 0

        def in_room(pattern, *dims, **sizes):
            nonlocal room_used
            lo, n = room_used, int(np.prod(dims))
            room_used += n
            return room[:, lo:lo + n].rearrange(pattern, **sizes)

        rope_a = [in_room("p (m x) -> p m x", 4, 2 * S, m=4) for _ in range(2)]
        rope_s = [in_room("p (m x) -> p m x", 4, 2 * S, m=4) for _ in range(2)]
        KB = [in_room("p (m h k) -> p m h k", 4, HG, S, m=4, h=HG) for _ in range(2)]
        SM = [in_room("p (h k) -> p h k", HEADS, S, h=HEADS) for _ in range(2)]
        comb_b = room
        QK = two("QK", [P, 4, 2, SLOT])
        VB = two("VB", [P, 2, HP, VW])
        top = two("top", [P, HEADS])
        PR = two("PR", [P, HEADS, SLOT])
        PRT = two("PRT", [P, HP, P])
        den = two("den", [P, HEADS])
        rden = two("rden", [P, HEADS])
        CX = two("CX", [P, HEADS, HD])
        CXT = two("CXT", [P, KD, P])
        row = two("row", [P, ROW])
        r_neg = two("r_neg", [P, 1])
        r_top = two("r_top", [P, TOP0])
        r_exp = two("r_exp", [P, E0])
        r_sum = two("r_sum", [P, 1])
        r_inv = two("r_inv", [P, 1])
        r_prob = two("r_prob", [P, E0])
        r_left = two("r_left", [P, E0])
        r_index = two("r_index", [P, TOP0], U32)
        r_expert = two("r_expert", [P, TOP0])
        r_mask = two("r_mask", [P, E0], BF16)
        r_over = two("r_over", [P, E0])
        r_slots = two("r_slots", [P, E0])
        r_pick = two("r_pick", [P, TOP0, E0])
        r_slot = two("r_slot", [P, TOP0])
        slot = two("slot", [P, TOP0], I32)
        xrows = two("xrows", [P, CT, ROW])
        gu_w = two("gu_w", [P, KD, 2 * F0])
        dn_w = two("dn_w", [P, 2, D])
        work = two("work", [P, LONG + SLOT - S + 1])
        silu_a, silu_b, hid_a, hid_b = ([x[:, n * CAP:(n + 1) * CAP] for x in work] for n in range(4))
        positions = work
        y_rows = two("y_rows", [P, CT, D])
        row_id = two("row_id", [P, CT])
        row_w = two("row_w", [P, CT])
        dest_f = two("dest_f", [P, CT])
        dest = two("dest", [P, CT], I32)
        sums = two("sums", [P, CT, D])
        KP1 = [x.rearrange("p m h k -> p (m h k)") for x in KB]
        CT1 = [x[:].rearrange("p m i q -> p m (i q)") for x in QK]
        residual = two("residual", [P, D])
        Z = two("Z", [P, D])
        N3 = [x[:, 0:D] for x in row]
        N3_high = sb("N3_high", [P, KD, TOKENS], F32R)
        N3_low = sb("N3_low", [P, KD, TOKENS], F32R)
        NW = KD * 2 * I1 + D
        w1 = [x[:].rearrange("p k n -> p (k n)") for x in gu_w]
        w1_high = two("w1_high", [P, NW], F32R)
        w1_low = two("w1_low", [P, NW], F32R)
        GU = KD * 2 * F0
        gu_high, gu_low = w1_high, w1_low
        xT_high, xT_low = ([x[:].rearrange("p k n -> p (k n)")[:, 2 * P * KD * u:2 * P * KD * (u + 1)] for u in range(2)]
                           for x in (N3_high, N3_low))
        logits1 = sb("logits1", [P, TILES, E1])
        comb_T = sb("comb_T", [E1 * TILES, P])
        sig1 = sb("sig1", [P, TILES, E1])
        choice = sb("choice", [P, TILES, E1])
        pair_hi = sb("pair_hi", [P, 2 * TILES, 2])
        pair_lo = sb("pair_lo", [P, 2 * TILES, 2])
        best = sb("best", [P, 2 * TILES, 1])
        second_a = sb("second_a", [P, 2 * TILES, 1])
        second_b = sb("second_b", [P, 2 * TILES, 1])
        group_sel = sb("group_sel", [P, TILES, 2])
        sorted1 = sb("sorted1", [P, TILES, E1])
        index1 = sb("index1", [P, TILES, E1], U32)
        index1f = sb("index1f", [P, TILES, TOP1])
        picks1 = sb("picks1", [P, TILES, TOP1, E1])
        picked1 = sb("picked1", [P, TILES, TOP1, E1])
        weight1 = sb("weight1", [P, TILES, TOP1])
        total1 = sb("total1", [P, TILES])
        comb1 = sb("comb1", [P, E1, TILES])
        silu1 = two("silu1", [P, HALF])
        hid1_high = two("hid1_high", [P, HT, 2, SLOT], F32R)
        hid1_low = two("hid1_low", [P, HT, 2, SLOT], F32R)

        psum = ctx.enter_context(nc.psum_tensor("psum", [P, 8, 512], F32))

        def bank(u, b):
            return psum[:, 4 * u + b, :]

        def scores(u):
            return psum[:, 4 * u + 2:4 * u + 4, :]

        first_loaded = sem("first_loaded")
        small_loaded = sem("small_loaded")
        late_loaded = sem("late_loaded")
        vec_setup = sem("vector_setup")
        pool_setup = sem("pool_setup")
        patches_loaded = sem2("patches_loaded")
        vec = sem("vector_steps")
        act_step = sem("scalar_steps")
        pool_step = sem("pool_steps")
        passed = sem("passed_wait")
        embedded = sem("embedded")
        var_ready = sem("var_ready")
        dev_ready = sem("dev_ready")
        normed = sem("normed")
        transposed = sem("transposed")
        NT_ready = sem("NT_ready")
        bias_added = sem("bias_added")
        qk_ready = sem("qk_ready")
        v_ready = sem("v_ready")
        kb_ready = sem("kb_ready")
        vb_ready = sem("vb_ready")
        scored = sem("scored")
        shifted = sem("shifted")
        exped = sem("exped")
        prt_psum = sem("probs_transposed")
        prt_ready = sem("prt_ready")
        attended = sem("attended")
        cx_ready = sem("cx_ready")
        cx_transposed = sem("cx_transposed")
        cxt_ready = sem("cxt_ready")
        projected = sem("projected")
        var2_ready = sem("var2_ready")
        dev2_ready = sem("dev2_ready")
        normed2 = sem("normed2")
        transposed2 = sem("transposed2")
        NT2_ready = sem("NT2_ready")
        routed = sem("router_logits")
        neg_ready = sem("neg_ready")
        rexp_ready = sem("rexp_ready")
        mask_ready = sem("mask_ready")
        taken_ready = sem("taken_ready")
        counted = sem("counted")
        slots_ready = sem("slots_ready")
        scattered = sem2("scattered")
        rows_loaded = sem2("rows_loaded")
        gu_loaded = sem2("gate_up_loaded")
        dn_loaded = sem2("down_loaded")
        meta_ready = sem("slot_tokens_ready")
        rows_transposed = sem("rows_transposed")
        xT_ready = sem("xT_ready")
        x_split = sem("x_split")
        gu_high_ready = sem("gate_up_high_ready")
        gu_low_vec = sem("gate_up_low_vector")
        gu_low_pool = sem("gate_up_low_pool")
        gu_ready = sem("gate_up_ready")
        silu_ready = sem("silu_ready")
        hid_ready = sem("hidden_ready")
        down_ready = sem("down_ready")
        y_ready = sem("y_ready")
        added = sem2("sums_added")
        sums_loaded = sem2("sums_loaded")
        qkv_ready = sem("qkv_ready")
        keys_ready = sem("keys_ready")
        values_turned = sem("values_turned")
        values_ready = sem("values_ready")
        summed = sem("experts_summed")
        residual_ready = sem("residual_ready")
        exped1 = sem("exped1")
        probs_ready = sem("probs_ready")
        attended1 = sem("attended1")
        low_ready = sem("low_results_ready")
        high_ready = sem("high_results_ready")
        var3_ready = sem("var3_ready")
        dev3_ready = sem("dev3_ready")
        compacted = sem("compacted")
        logits_ready = sem("logits_ready")
        logits_copied = sem("logits_copied")
        sums_cleared = sem("sums_cleared")
        sig_ready = sem("sigmoid_ready")
        comb_ready = sem("comb_ready")
        comb_turned = sem("comb_turned")
        comb_copied = sem("comb_copied")
        comb_stored = sem("comb_stored")
        comb_loaded = sem("comb_loaded")
        w1_loaded = sem2("w1_loaded")
        n3_split = sem("n3_split")
        high_step = sem("weights_high_step")
        gate1_split = sem("gate1_split")
        down1_split = sem("down1_split")
        product1_ready = sem("product1_ready")
        high1_ready = sem("high1_ready")
        gu1_ready = sem("gate_up1_ready")
        silu1_ready = sem("silu1_ready")
        hid1_ready = sem("hidden1_ready")
        down1_done = sem("down1_done")
        final_ready = sem("final_ready")
        out_stored = sem("out_stored")

        first = [(tok_w[:], dram["tok_w"]), (const[:], dram["const"]),
                 (tok_b[:], dram["tok_b"].partition_broadcast(P))]
        early = [(wqk[:], dram["wqk"]), (rope_b[:], dram["rope_b"]), (wv[:], dram["wv"]),
                 (bv[:], dram["bv"].partition_broadcast(P)), (wo[:], dram["wo"]),
                 (bo[:], dram["bo"].partition_broadcast(P)), (gate_w[:], dram["gate_w"])]
        late = [(wqkv1[:], dram["wqkv1"]), (bqkv1[:], dram["bqkv1"]),
                (wo1[:], dram["wo1"]), (bo1[:], dram["bo1"].partition_broadcast(P)),
                (gamma[:], dram["gamma"].partition_broadcast(P)),
                (beta[:], dram["beta"].partition_broadcast(P)),
                (router_w[:], dram["router_w"]), (corr[:], dram["corr"].partition_broadcast(P))]
    
        def images(ap):
            return [ap[SLOT * i:SLOT * i + S] for i in range(2)]

        FIRST = 0

        def following(j, u):
            return ((j, 1), (j + 1, 0)) if u == 0 else ((j + 1, 0), (j + 1, 1))

        block = ctx.enter_context(nc.Block())

        @block.sync
        def _(sp):
            def load_patches(t, u):
                sp.dma_start(patches[u][:], dram["patches"][bass.ds(t, 1), :, :, :].rearrange("o p k x -> (o p) k x")
                             ).then_inc(patches_loaded[u], 16)

            load_patches(0, 0)
            for dst, src in first:
                sp.dma_start(dst, src).then_inc(first_loaded, 16)
            load_patches(1, 1)
            for dst, src in early:
                sp.dma_start(dst, src).then_inc(small_loaded, 16)

            def load_gate_up(e, u):
                sp.dma_start(gu_w[u][:], dram["gu_w"][bass.ds(e, 1), :, :, :].rearrange("o p k n -> (o p) k n")
                             ).then_inc(gu_loaded[u], 16)

            def load_down(e, u):
                sp.dma_start(dn_w[u][:, 0, :], dram["dn_w"][bass.ds(e, 1), 0:P, :].rearrange("o p n -> (o p) n")
                             ).then_inc(dn_loaded[u], 16)
                sp.dma_start(dn_w[u][P - F0B:P, 1, :],
                             dram["dn_w"][bass.ds(e, 1), P:F0, :].rearrange("o p n -> (o p) n")
                             ).then_inc(dn_loaded[u], 16)

            def load_rows(e, u):
                sp.dma_start(xrows[u][:], table[bass.ds(e * CAP, CAP), :].rearrange("(c p) x -> p c x", p=P)
                             ).then_inc(rows_loaded[u], 16)

            with sp.Fori(0, TILES // 2 - 1) as i:
                for u in range(2):
                    sp.wait_ge(embedded, i * 2 + u + 1)
                    load_patches(i * 2 + u + 2, u)
            for dst, src in late:
                sp.dma_start(dst, src).then_inc(late_loaded, 16)
            for u in range(2):
                load_gate_up(u, u)
                load_down(u, u)
            for u in range(2):
                sp.wait_ge(scattered[u], 16 + 16 * TOP0 * (TILES // 2))
            for u in range(2):
                load_rows(u, u)
            def next_rows(e, u):
                sp.wait_ge(rows_transposed, e - 1)
                sp.wait_ge(meta_ready, e - 1)
                load_rows(e, u)

            def next_gate_up(e, u):
                sp.wait_ge(gu_low_vec, e - 1)
                sp.wait_ge(gu_low_pool, e - 1)
                load_gate_up(e, u)

            def next_down(e, u):
                sp.wait_ge(down_ready, e - 1)
                load_down(e, u)

            next_gate_up(2, 0)
            next_rows(2, 0)
            next_gate_up(3, 1)
            with sp.Fori(0, E0 // 2 - 2) as i:
                for e, u in ((i * 2 + 3, 1), (i * 2 + 4, 0)):
                    next_rows(e, u)
                    next_gate_up(e + 1, 1 - u)
                    next_down(e - 1, 1 - u)
            next_rows(E0 - 1, 1)
            next_down(E0 - 2, 0)
            next_down(E0 - 1, 1)

            def load_w1(e, u):
                sp.dma_start(w1[u], dram["w1"][bass.ds(e, 1), :, :].rearrange("o p n -> (o p) n")
                             ).then_inc(w1_loaded[u], 16)


            def load_sums(t, u):
                for c in range(CT):
                    for im, half in enumerate(images(sums[u])):
                        sp.dma_start(half[:, c, :], acc[c][bass.ds(t * PAIR + S * im + 1, S), :]
                                     ).then_inc(sums_loaded[u], 16)

            sp.wait_ge(pool_setup, 1)
            for c in range(CT):
                sp.wait_ge(added[c], 32 + 16 * E0)
            for u in range(2):
                load_sums(u, u)
            sp.wait_ge(down_ready, E0)
            for u in range(2):
                load_w1(u, u)

            with sp.Fori(0, TILES // 2 - 1) as i:
                for u in range(2):
                    sp.wait_ge(summed, i * 2 + u + 1)
                    load_sums(i * 2 + u + 2, u)

            def next_w1(e, u):
                sp.wait_ge(down1_split, e - 1)
                load_w1(e, u)

            for u in range(2):
                next_w1(u + 2, u)
            sp.wait_ge(comb_copied, 1)
            for im in range(2):
                sp.dma_start(comb_flat[:, im, :], comb_T[0:E1 * TILES, SLOT * im:SLOT * im + S]
                             ).then_inc(comb_stored, 16)
            sp.wait_ge(comb_stored, 32)

            def spread_weights(n):
                at = bass.ds(n * (2 * TOKENS), 2 * TOKENS)
                sp.dma_start(comb_b[:, at], comb_flat.rearrange("a i q -> (a i q)")[at].partition_broadcast(P)
                             ).then_inc(comb_loaded, 16)

            spread_weights(0)
            with sp.Fori(0, (E1 - 4) // 2) as i:
                sp.wait_ge(comb_loaded, i * 16 + 16)
                spread_weights(i + 1)
                for u in range(2):
                    next_w1(i * 2 + u + 4, u)
            sp.wait_ge(comb_loaded, 16 * (E1 // 2 - 1))
            spread_weights(E1 // 2 - 1)
            next_w1(E1, 0)
            sp.wait_ge(final_ready, TILES // 2)
            for im in range(2):
                sp.dma_start(out.rearrange("(t i) q f -> i q t f", i=2)[im],
                             H[SLOT * im:SLOT * im + S, :, :]).then_inc(out_stored, 16)
            sp.wait_ge(out_stored, 32)

        def results_by_chunks(copy, u, g):
            first = HG * S * g
            for j in range(4):
                tokens = [t for t in range(S) if first <= t * CH + CG * j < first + HG * S]
                lo, n = tokens[0], len(tokens)
                at = lo * CH + CG * j - first
                src = psum[0:HD, 4 * u + 2 * g:4 * u + 2 * g + 2, at:at + n * CH]
                dst = CT1[u][32 * j:32 * j + HD, :, :].rearrange("p c (i q) -> p i q c", i=2)[:, :, lo:lo + n, :]
                ins = copy(dst, src.rearrange("p i (q c) -> p i q c", c=CH)[:, :, :, 0:CG])
            return ins

        def shift_tile(ve, steps, n, u, mask):
            ve.wait_ge(scored, n)
            sc = scores(u)[:, :, 0:HG * S].rearrange("p g (h k) -> p g h k", k=S)
            sm = SM[u][:].rearrange("p (g h) k -> p g h k", g=KD)
            mx = top[u][:].rearrange("p (g h) -> p g h", g=KD)
            if mask:
                causal = cols("causal").unsqueeze(1).unsqueeze(1).to_broadcast([P, KD, HG, S])
                steps.do(nc.vector.tensor_tensor(sm, sc, causal, ALU.add))
                sc = sm
            steps.do(nc.vector.tensor_reduce(mx, sc, AX.X, ALU.max))
            nc.vector.tensor_tensor(sm, sc, repeat(mx, S), ALU.subtract).then_inc(shifted, 1)

        def head_results(ve, steps, n, u):
            ve.wait_ge(attended, n)
            o = bank(u, 1)[:, 0:HP * VW].rearrange("p (h x) -> p h x", x=HD + 1)
            total = o[:, :, HD:HD + 1].rearrange("p h x -> p (h x)")
            steps.do(nc.vector.tensor_scalar(den[u][:], total, 1e-8, None, ALU.add))
            steps.do(nc.vector.reciprocal(rden[u][:], den[u][:]))
            nc.vector.tensor_tensor(CX[u][:], o[:, :, 0:HD], repeat(rden[u][:], HD), ALU.mult).then_inc(cx_ready, 1)

        def key_blocks(steps, u):
            keys = QK[u][:, 2:4, :, 0:S].rearrange("p g i q -> p (g i) q").unsqueeze(2).to_broadcast([P, 4, HG, S])
            mask = repeat(spread(cols("head_mask"), 4), S)
            return nc.vector.tensor_tensor(KB[u][:], keys, mask, ALU.mult)

        def statistics(steps, src, u, ready):
            steps.eng.sem_inc(passed, 1)
            steps.do(nc.vector.bn_stats(stats[u][:], src))
            steps.eng.sem_inc(passed, 1)
            nc.vector.bn_aggr(moments[u][:], stats[u][:]).then_inc(ready, 1)

        def normalise(ve, steps, dst, src, u, ready, k):
            ve.wait_ge(ready, k + u)
            steps.do(nc.vector.reciprocal(rstd[u][:], dev[u][:]))
            return nc.vector.tensor_scalar(dst, src, moments[u][:, 0:1], rstd[u][:], ALU.subtract, ALU.mult)

        def tile_of(t):
            return H[:, bass.ds(t, 1), :].rearrange("p o f -> p (o f)")

        def split_half(eng, u, half):
            at = slice(half * GU // 2, (half + 1) * GU // 2)
            return eng.tensor_tensor(gu_low[u][:, at], gu_w[u][:].rearrange("p k n -> p (k n)")[:, at],
                                     gu_high[u][:, at].bitcast(F32), ALU.subtract)

        @block.vector
        def _(ve):
            steps = Steps(ve, vec)
            nc.vector.memset(taken[:], 0.0).then_inc(taken_ready, 1)
            for u in range(2):
                nc.vector.memset(QK[u][:], 0.0)
                nc.vector.memset(PR[u][:], 0.0)
                nc.vector.memset(positions[u][0:QKV_ROWS, LONG:], 0.0)
                steps.mark(nc.vector.memset(VB[u][:], 0.0))
            steps.wait()
            for u in range(2):
                nc.vector.memset(VB[u][0:SLOT, :, :, HD:HD + 1], 1.0)
                nc.vector.memset(VB[u][SLOT:P, :, :, VW - 1:VW], 1.0)
            ve.sem_inc(y_ready, 2)
            nc.vector.memset(r_left[0][:], 0.0).then_inc(vec_setup, 1)
            ve.wait_ge(first_loaded, 16 * len(first))

            def embed(j, u):
                n = j * 2 + u + 1
                ve.wait_ge(embedded, n)
                steps.do(nc.vector.tensor_tensor(tile_of(j * 2 + u), bank(u, 0)[:, 0:D], tok_b[:], ALU.add))
                statistics(steps, tile_of(j * 2 + u), u, var_ready)

            def embedded_rows(j, u):
                normalise(ve, steps, N[u][:], tile_of(j * 2 + u), u, dev_ready, j * 2 + 1).then_inc(normed, 1)

            def rotate(j, u):
                ve.wait_ge(qk_ready, j * 2 + u + 1)
                shape = [P, 8, S]
                cos, sin = (cols(c).unsqueeze(1).to_broadcast(shape) for c in ("cos", "sin"))
                flat = [x[u][:].rearrange("p m (i q) -> p (m i) q", i=2) for x in (rope_a, rope_s)]
                src = [bank(u, b)[:, 0:8 * S].rearrange("p (m q) -> p m q", q=S) for b in (2, 3)]
                steps.mark(nc.vector.tensor_tensor(flat[0], src[0], cos, ALU.mult))
                steps.mark(nc.vector.tensor_tensor(flat[1], src[1], sin, ALU.mult))
                steps.wait()
                a, r = (x[u][:].rearrange("p m (i q) -> p m i q", i=2) for x in (rope_a, rope_s))
                bias = rope_bias[:].unsqueeze(2).to_broadcast([P, 4, 2, S])
                steps.do(nc.vector.tensor_tensor(a, a, bias, ALU.add))
                steps.do(nc.vector.tensor_tensor(QK[u][:, :, :, 0:S], a, r, ALU.add))

            def keys_and_values(j, u):
                key_blocks(steps, u).then_inc(kb_ready, 1)
                ve.wait_ge(v_ready, j * 2 + u + 1)
                v, b = (x.rearrange("p (h o d) -> p h o d", h=HP, o=2) for x in (bank(u, 0)[:, 0:D], bv[:]))
                for im in range(2):
                    src = slice(SLOT * im, SLOT * im + SLOT)
                    for o in range(2):
                        ins = nc.vector.tensor_tensor(VB[u][SLOT * o:SLOT * o + SLOT, im, :, (HD + 1) * o:(HD + 1) * o + HD],
                                                      v[src, :, o, :], b[src, :, o, :], ALU.add)
                ins.then_inc(vb_ready, 1)

            def stream_vector(j, u):
                n = j * 2 + u + 1
                ve.wait_ge(projected, n)
                ve.wait_ge(bias_added, n)
                stream = tile_of(j * 2 + u)
                steps.do(nc.vector.tensor_tensor(stream, bank(u, 1)[:, 0:D], stream, ALU.add))
                statistics(steps, stream, u, var2_ready)
                ve.wait_ge(scattered[u], j * (16 * TOP0) + 16)
                nc.vector.tensor_scalar(row[u][:, D:D + 1], row[u][:, D:D + 1], float(2 * PAIR), None, ALU.add)
                normalise(ve, steps, row[u][:, 0:D], stream, u, dev2_ready, j * 2 + 1).then_inc(normed2, 1)

            def largest_logit(j, u):
                ve.wait_ge(routed, j * 2 + u + 1)
                ve.sem_inc(passed, 1)
                steps.do(nc.vector.max(r_top[u][:], bank(u, 1)[:, D:D + E0]))
                nc.vector.tensor_scalar(r_neg[u][:], r_top[u][:, 0:1], -1.0, None, ALU.mult).then_inc(neg_ready, 1)

            def choose(j, u):
                ve.wait_ge(rexp_ready, j * 2 + u + 1)
                steps.do(nc.vector.reciprocal(r_inv[u][:], r_sum[u][:]))
                steps.do(nc.vector.tensor_scalar(r_prob[u][:], r_exp[u][:], r_inv[u][:], None, ALU.mult))
                ve.sem_inc(passed, 1)
                steps.do(nc.vector.max(r_top[u][:], r_prob[u][:]))
                ve.sem_inc(passed, 1)
                steps.do(nc.vector.match_replace(r_left[u][:], r_top[u][:], r_prob[u][:], -1.0))
                nc.vector.tensor_scalar(r_mask[u][:], r_left[u][:], 0.0, None, ALU.is_lt).then_inc(mask_ready, 1)
                steps.mark(nc.vector.max_index(r_index[u][:], r_top[u][:], r_prob[u][:]))
                steps.do(nc.vector.tensor_reduce(r_sum[u][:], r_top[u][:], AX.X, ALU.add))
                steps.mark(nc.vector.tensor_copy(r_expert[u][:], r_index[u][:]))
                steps.do(nc.vector.reciprocal(r_inv[u][:], r_sum[u][:]))
                ve.wait_ge(mask_ready, j * 2 + u + 1)
                steps.mark(nc.vector.scalar_tensor_tensor(row[u][:, D + 1:ROW], r_mask[u][:], r_inv[u][:],
                                                          r_prob[u][:], ALU.mult, ALU.mult))
                steps.do(nc.vector.tensor_tensor(r_pick[u][:], spread(cols("iota"), TOP0), repeat(r_expert[u][:], E0),
                                                 ALU.is_equal))

            def find_slots(j, u):
                ve.wait_ge(counted, j * 2 + u + 1)
                nc.vector.tensor_tensor(taken[:], taken[:], r_mask[u][:], ALU.add).then_inc(taken_ready, 1)
                cnt = bank(u, 1)[:, D + E0:D + 2 * E0]
                steps.mark(nc.vector.tensor_scalar(r_over[u][:], cnt, cols("pad_far"), float(CAP), ALU.add, ALU.is_ge))
                steps.mark(nc.vector.tensor_tensor(r_slots[u][:], cnt, cols("slot_base"), ALU.add))
                steps.wait()
                steps.do(nc.vector.scalar_tensor_tensor(r_slots[u][:], r_over[u][:], FAR, r_slots[u][:],
                                                        ALU.mult, ALU.add))
                steps.do(nc.vector.tensor_tensor(r_pick[u][:], r_pick[u][:], spread(r_slots[u][:], TOP0), ALU.mult))
                steps.do(nc.vector.tensor_reduce(r_slot[u][:], r_pick[u][:], AX.X, ALU.add))
                nc.vector.tensor_copy(slot[u][:], r_slot[u][:]).then_inc(slots_ready, 1)

            def first_vector(j, u, more):
                (j1, u1), (j2, u2) = following(j, u)
                if more > 1:
                    embed(j2, u2)
                head_results(ve, steps, j * 2 + u + 1, u)
                if more > 1:
                    embedded_rows(j2, u2)
                if more > 0:
                    keys_and_values(j1, u1)
                stream_vector(j, u)
                if more > 0:
                    shift_tile(ve, steps, j1 * 2 + u1 + 1, u1, True)
                largest_logit(j, u)
                if more > 1:
                    rotate(j2, u2)
                choose(j, u)
                find_slots(j, u)

            for u in range(2):
                embed(FIRST, u)
            for u in range(2):
                embedded_rows(FIRST, u)
            nc.vector.tensor_copy(count_earlier[:], cols("earlier"))
            nc.vector.tensor_copy(count_valid[:], cols("valid"))
            for u in range(2):
                nc.vector.tensor_scalar(row[u][:, D:D + 1], cols("token"), float(PAIR * (u - 2)), None, ALU.add)
            ve.wait_ge(small_loaded, 16 * len(early))
            for m in range(4):
                steps.mark(nc.vector.tensor_scalar(rope_bias[:, m, :], cols("cos"), rope_b[:, m:m + 1], None, ALU.mult))
            steps.wait()
            for m in range(4):
                steps.mark(nc.vector.scalar_tensor_tensor(rope_bias[:, m, :], cols("sin"), rope_b[:, 4 + m:5 + m],
                                                          rope_bias[:, m, :], ALU.mult, ALU.add))
            steps.wait()
            rotate(FIRST, 0)
            keys_and_values(FIRST, 0)
            shift_tile(ve, steps, 1, 0, True)
            rotate(FIRST, 1)
            with ve.Fori(0, TILES // 2 - 2) as i:
                steps.begin(i, LOOP0_STEPS)
                for u in range(2):
                    first_vector(i, u, 3)
            steps.end(TILES // 2 - 2)
            for t in range(TILES - 4, TILES):
                first_vector(t // 2, t % 2, TILES - 1 - t)

            def slot_tokens(e, i, u):
                ve.wait_ge(rows_loaded[u], i * 16 + 16)
                ve.wait_ge(y_ready, e + 1)
                nc.vector.tensor_copy(row_id[u][:], xrows[u][:, :, D:D + 1].rearrange("p c o -> p (c o)"))
                nc.vector.tensor_copy(row_w[u][:], xrows[u][:, :, bass.ds(e + (D + 1), 1)].rearrange("p c o -> p (c o)")
                                      ).then_inc(meta_ready, 1)

            def hidden(e, u):
                ve.wait_ge(silu_ready, e + 1)
                nc.vector.tensor_tensor(hid_a[u][:], silu_a[u][:], bank(u, 1)[:, CAP:2 * CAP], ALU.mult)
                nc.vector.tensor_tensor(hid_b[u][P - F0B:P, :], silu_b[u][P - F0B:P, :],
                                        bank(u, 2)[P - F0B:P, 0:CAP], ALU.mult).then_inc(hid_ready, 1)

            def weighted(e, i, u):
                ve.wait_ge(meta_ready, e + 1)
                steps.do(nc.vector.tensor_scalar(dest_f[u][:], row_id[u][:], 0.0, cols("empty_row"),
                                                 ALU.is_equal, ALU.mult))
                ve.wait_ge(added[0], i * 32 + 16 * u + 16)
                ve.wait_ge(added[1], i * 32 + 16 * u + 16)
                nc.vector.tensor_tensor(dest[u][:], dest_f[u][:], row_id[u][:], ALU.add)
                ve.wait_ge(down_ready, e + 1)
                for c in range(CT):
                    ins = nc.vector.tensor_scalar(y_rows[u][:, c, :], bank(u, 3)[:, c * D:(c + 1) * D],
                                                  row_w[u][:, c:c + 1], None, ALU.mult)
                ins.then_inc(y_ready, 1)

            def low_rows(e, u):
                ve.wait_ge(xT_ready, e + 1)
                nc.vector.tensor_tensor(xT_low[u], bank(u, 0), xT_high[u].bitcast(F32), ALU.subtract).then_inc(x_split, 1)

            def low_weights(e, u):
                ve.wait_ge(gu_high_ready, e + 1)
                split_half(nc.vector, u, 0).then_inc(gu_low_vec, 1)

            def expert_vector(e, i, now, more):
                hidden(e, now)
                low_rows(e + 1, 1 - now)
                weighted(e - 1, i, 1 - now)
                slot_tokens(e + 1, i + 1, 1 - now)
                if more:
                    low_weights(e + 2, now)

            for u in range(2):
                low_weights(u, u)
            slot_tokens(0, 0, 0)
            low_rows(0, 0)
            hidden(0, 0)
            low_rows(1, 1)
            slot_tokens(1, 0, 1)
            low_weights(2, 0)
            with ve.Fori(0, E0 // 2 - 2) as i:
                steps.begin(i, 2)
                for e, now in ((i * 2 + 1, 1), (i * 2 + 2, 0)):
                    expert_vector(e, i, now, True)
            steps.end(E0 // 2 - 2)
            expert_vector(E0 - 3, E0 // 2 - 2, 1, True)
            expert_vector(E0 - 2, E0 // 2 - 2, 0, False)
            hidden(E0 - 1, 1)
            weighted(E0 - 2, E0 // 2 - 1, 0)
            weighted(E0 - 1, E0 // 2 - 1, 1)

            def new_statistics(j, u):
                ve.wait_ge(summed, j * 2 + u + 1)
                statistics(steps, tile_of(j * 2 + u), u, var_ready)

            def new_rows(j, u):
                if j is not FIRST:
                    ve.wait_ge(residual_ready, j * 2 + (u - 1))
                normalise(ve, steps, N[u][:], tile_of(j * 2 + u), u, dev_ready, j * 2 + (TILES + 1)).then_inc(normed, 1)

            def add_qkv_bias(j, u):
                ve.wait_ge(qk_ready, j * 2 + (u + TILES + 1))
                src = psum[0:QKV_ROWS, 4 * u:4 * u + 4, 0:CG * PAIR].rearrange("p b (c x) -> p b c x", c=CG)
                dst = positions[u][0:QKV_ROWS, 0:LONG].rearrange("p (x b c) -> p b c x", b=4, c=CG)
                bias = repeat(bqkv1[:].rearrange("p (b c) -> p b c", b=4), PAIR)
                nc.vector.tensor_tensor(dst, src, bias, ALU.add).then_inc(qkv_ready, 1)

            def probabilities(j, u):
                ve.wait_ge(exped1, j * 2 + u + 1)
                pr = PR[u][:, :, 0:S]
                steps.do(nc.vector.tensor_reduce(den[u][:], pr, AX.X, ALU.add))
                steps.do(nc.vector.reciprocal(rden[u][:], den[u][:]))
                nc.vector.tensor_tensor(pr, pr, repeat(rden[u][:], S), ALU.mult).then_inc(probs_ready, 1)

            def add_residual(j, u):
                n = j * 2 + u + 1
                ve.wait_ge(projected, n + TILES)
                ve.wait_ge(residual_ready, n)
                steps.do(nc.vector.tensor_tensor(Z[u][:], bank(u, 1)[:, 0:D], residual[u][:], ALU.add))
                statistics(steps, Z[u][:], u, var3_ready)

            def scale_rows(j, u):
                steps.do(normalise(ve, steps, Z[u][:], Z[u][:], u, dev3_ready, j * 2 + 1))
                steps.do(nc.vector.tensor_tensor(Z[u][:], Z[u][:], gamma[:], ALU.mult))

            def finish_stream(j, u):
                stream = tile_of(j * 2 + u)
                steps.do(nc.vector.tensor_tensor(stream, stream, Z[u][:], ALU.add))
                statistics(steps, stream, u, var2_ready)

            def attend_vector(j, u, more):
                (j1, u1), (j2, u2) = following(j, u)
                if more > 0:
                    add_qkv_bias(j1, u1)
                ve.wait_ge(attended1, j * 2 + u + 1)
                results_by_chunks(nc.vector.tensor_copy, u, 1).then_inc(high_ready, 1)
                if more > 1:
                    new_statistics(j2, u2)
                    new_rows(j2, u2)
                add_residual(j, u)
                if more > 0:
                    shift_tile(ve, steps, j1 * 2 + (u1 + TILES + 1), u1, False)
                scale_rows(j, u)
                if more > 0:
                    probabilities(j1, u1)
                finish_stream(j, u)
                normalise(ve, steps, N3[u], tile_of(j * 2 + u), u, dev2_ready, j * 2 + (TILES + 1)).then_inc(normed2, 1)

            for u in range(2):
                new_statistics(FIRST, u)
            for u in range(2):
                new_rows(FIRST, u)
            add_qkv_bias(FIRST, 0)
            shift_tile(ve, steps, TILES + 1, 0, False)
            probabilities(FIRST, 0)
            with ve.Fori(0, TILES // 2 - 1) as i:
                steps.begin(i, LOOP1_STEPS)
                for u in range(2):
                    attend_vector(i, u, 2)
            steps.end(TILES // 2 - 1)
            attend_vector(TILES // 2 - 1, 0, 1)
            attend_vector(TILES // 2 - 1, 1, 0)
            ve.wait_ge(sig_ready, 1)
            steps.do(nc.vector.tensor_tensor(choice[:], sig1[:], spread(corr[:], TILES), ALU.add))
            quads = choice[:].rearrange("p t (g a b) -> p (t g) a b", g=2, a=2)
            a, b = quads[:, :, :, 0], quads[:, :, :, 1]
            steps.mark(nc.vector.tensor_tensor(pair_hi[:], a, b, ALU.max))
            steps.mark(nc.vector.tensor_tensor(pair_lo[:], a, b, ALU.min))
            steps.wait()
            steps.mark(nc.vector.tensor_tensor(best[:], pair_hi[:, :, 0:1], pair_hi[:, :, 1:2], ALU.max))
            steps.mark(nc.vector.tensor_tensor(second_a[:], pair_hi[:, :, 0:1], pair_hi[:, :, 1:2], ALU.min))
            steps.mark(nc.vector.tensor_tensor(second_b[:], pair_lo[:, :, 0:1], pair_lo[:, :, 1:2], ALU.max))
            steps.wait()
            steps.do(nc.vector.tensor_tensor(second_a[:], second_a[:], second_b[:], ALU.max))
            steps.do(nc.vector.tensor_tensor(best[:], best[:], second_a[:], ALU.add))
            g = best[:].rearrange("p (t g) o -> p t (g o)", g=2)
            steps.mark(nc.vector.tensor_tensor(group_sel[:, :, 0:1], g[:, :, 0:1], g[:, :, 1:2], ALU.is_ge))
            steps.mark(nc.vector.tensor_tensor(group_sel[:, :, 1:2], g[:, :, 0:1], g[:, :, 1:2], ALU.is_lt))
            steps.wait()
            groups = choice[:].rearrange("p t (g a) -> p (t g) a", g=2)
            steps.do(nc.vector.tensor_tensor(groups, groups, repeat(group_sel[:].rearrange("p t g -> p (t g)"), 4),
                                             ALU.mult))
            steps.do(nc.vector.tensor_scalar(choice[:], choice[:], 0.0, None, ALU.add))
            for t in range(TILES):
                steps.mark(nc.vector.max(sorted1[:, t, :], choice[:, t, :]))
            steps.wait()
            for t in range(TILES):
                steps.mark(nc.vector.max_index(index1[:, t, :], sorted1[:, t, :], choice[:, t, :]))
            steps.wait()
            steps.do(nc.vector.tensor_copy(index1f[:], index1[:, :, 0:TOP1]))
            full = [P, TILES * TOP1, E1]
            flat = picks1[:].rearrange("p t k e -> p (t k) e")
            chosen = index1f[:].rearrange("p t k -> p (t k)")
            steps.do(nc.vector.tensor_tensor(flat, cols("iota")[:, 0:E1].unsqueeze(1).to_broadcast(full),
                                             repeat(chosen, E1), ALU.is_equal))
            steps.do(nc.vector.tensor_tensor(picked1[:], picks1[:], sig1[:].unsqueeze(2).to_broadcast([P, TILES, TOP1, E1]),
                                             ALU.mult))
            steps.do(nc.vector.tensor_reduce(weight1[:], picked1[:], AX.X, ALU.add))
            steps.do(nc.vector.tensor_reduce(total1[:], weight1[:], AX.X, ALU.add))
            steps.do(nc.vector.tensor_scalar(total1[:], total1[:], 1e-20, None, ALU.add))
            steps.do(nc.vector.reciprocal(total1[:], total1[:]))
            steps.do(nc.vector.tensor_tensor(weight1[:], weight1[:], repeat(total1[:], TOP1), ALU.mult))
            steps.do(nc.vector.tensor_tensor(flat, flat, repeat(weight1[:].rearrange("p t k -> p (t k)"), E1), ALU.mult))
            nc.vector.tensor_tensor(comb1[:].rearrange("p e t -> p t e"), picks1[:, :, 0, :], picks1[:, :, 1, :],
                                    ALU.add).then_inc(comb_ready, 1)

            def joined(h):
                return (x.rearrange("p (m q) -> p m q", q=S) for x in (silu1[h][:], psum[:, 2 * h + 1, 0:HALF]))

            def hidden_parts(n, h):
                hidden, up = joined(h)
                nc.vector.tensor_tensor(hidden, hidden, up, ALU.mult).then_inc(product1_ready, 1)
                ve.wait_ge(high1_ready, n + 1)
                nc.vector.tensor_tensor(hid1_low[h][:].rearrange("p t i q -> p (t i) q")[:, :, 0:S], hidden,
                                        hid1_high[h][:].rearrange("p t i q -> p (t i) q")[:, :, 0:S].bitcast(F32),
                                        ALU.subtract).then_inc(hid1_ready, 1)

            def shared_hidden(h):
                ve.wait_ge(silu1_ready, h + 1)
                hidden_parts(h, h)

            shared_hidden(0)
            ve.wait_ge(comb_turned, 1)
            nc.vector.tensor_copy(comb_T[:], psum[0:E1 * TILES, 0, 0:P]).then_inc(comb_copied, 1)
            shared_hidden(1)
            with ve.Fori(0, E1 // 2) as i:
                steps.begin(i, 4)
                ve.wait_ge(comb_loaded, i * 16 + 16)
                for j in range(2):
                    for h in range(2):
                        n = i * 4 + (2 + 2 * j + h)
                        ve.wait_ge(silu1_ready, n + 1)
                        w = comb_b[:, bass.ds(i * (2 * TOKENS) + (j * TOKENS + h * HALF), HALF)]
                        steps.do(nc.vector.tensor_tensor(silu1[h][:], silu1[h][:], w, ALU.mult))
                        hidden_parts(n, h)
            steps.end(E1 // 2)
            ve.wait_ge(down1_done, 2 * (E1 + 1))
            for b in range(TILES // 2):
                pair = H[:, 2 * b:2 * b + 2, :].rearrange("p t f -> p (t f)")
                nc.vector.tensor_tensor(pair, psum[:, 4 + b, :], pair, ALU.add).then_inc(final_ready, 1)

        @block.scalar
        def _(act):
            nt = [x[:].rearrange("p k q -> p (k q)") for x in NT]
            cxt = [x[:].rearrange("p k q -> p (k q)") for x in CXT]
            act.wait_ge(vec_setup, 1)
            act.wait_ge(first_loaded, 16 * len(first))

            def root(n, u, var, ready):
                act.wait_ge(var, n)
                nc.scalar.activation(dev[u][:], moments[u][:, 1:2], ACT.Sqrt, bias=cols("eps")).then_inc(ready, 1)

            def copy_turned(n, dst, src, psum_ready, ready):
                act.wait_ge(psum_ready, n)
                nc.scalar.copy(dst, src[:, 0:D]).then_inc(ready, 1)

            def copy_probs(n, u):
                act.wait_ge(prt_psum, n)
                nc.scalar.copy(PRT[u][:].rearrange("p (b h) q -> p b (h q)", b=2), scores(u)).then_inc(prt_ready, 1)

            def exponentials(n, u, ready):
                act.wait_ge(shifted, n)
                nc.scalar.activation(PR[u][:, :, 0:S], SM[u][:], ACT.Exp, scale=SCALE).then_inc(ready, 1)

            def first_scalar(j, u, more):
                (j1, u1), (j2, u2) = following(j, u)
                n = j * 2 + u + 1
                copy_probs(n, u)
                if more > 1:
                    root(j2 * 2 + u2 + 1, u2, var_ready, dev_ready)
                copy_turned(n, cxt[u], bank(u, 0), cx_transposed, cxt_ready)
                if more > 1:
                    copy_turned(j2 * 2 + u2 + 1, nt[u2], bank(u2, 0)[:, D:2 * D], transposed, NT_ready)
                root(n, u, var2_ready, dev2_ready)
                copy_turned(n, cxt[u], bank(u, 1), transposed2, NT2_ready)
                if more > 0:
                    exponentials(j1 * 2 + u1 + 1, u1, exped)
                act.wait_ge(neg_ready, n)
                nc.scalar.activation(r_exp[u][:], bank(u, 1)[:, D:D + E0], ACT.Exp, bias=r_neg[u][:],
                                     accum_out=r_sum[u][:]).then_inc(rexp_ready, 1)

            for u in range(2):
                root(u + 1, u, var_ready, dev_ready)
            for u in range(2):
                copy_turned(u + 1, nt[u], bank(u, 0)[:, D:2 * D], transposed, NT_ready)
            exponentials(1, 0, exped)
            with act.Fori(0, TILES // 2 - 2) as i:
                nc.scalar.activation(table_of[:], cols("eps"), ACT.Sqrt)
                for u in range(2):
                    first_scalar(i, u, 3)
            for t in range(TILES - 4, TILES):
                first_scalar(t // 2, t % 2, TILES - 1 - t)
            nc.scalar.activation(table_of[:], cols("eps"), ACT.Silu)

            def high_weights(e, i, u):
                act.wait_ge(gu_loaded[u], i * 16 + 16)
                nc.scalar.copy(gu_high[u][:], gu_w[u][:].rearrange("p k n -> p (k n)")).then_inc(gu_high_ready, 1)

            def high_rows(e, u):
                act.wait_ge(rows_transposed, e + 1)
                nc.scalar.copy(xT_high[u], bank(u, 0)).then_inc(xT_ready, 1)

            def expert_silu(e, u):
                act.wait_ge(gu_ready, e + 1)
                nc.scalar.activation(silu_a[u][:], bank(u, 1)[:, 0:CAP], ACT.Silu)
                nc.scalar.activation(silu_b[u][P - F0B:P, :], bank(u, 2)[0:F0B, 0:CAP],
                                     ACT.Silu).then_inc(silu_ready, 1)

            for u in range(2):
                high_weights(u, 0, u)
            high_rows(0, 0)
            with act.Fori(0, E0 // 2 - 1) as i:
                for u in range(2):
                    e = i * 2 + u
                    expert_silu(e, u)
                    high_rows(e + 1, 1 - u)
                    high_weights(e + 2, i + 1, u)
            expert_silu(E0 - 2, 0)
            high_rows(E0 - 1, 1)
            expert_silu(E0 - 1, 1)

            def keys(j, u):
                act.wait_ge(qkv_ready, j * 2 + u + 1)
                nc.scalar.copy(KP1[u][0:HD, :], positions[u][32:32 + HD, 0:LONG]).then_inc(keys_ready, 1)

            def values(j, u):
                act.wait_ge(values_turned, j * 2 + u + 1)
                v = bank(u, 0)[:, 0:D].rearrange("p (i h d) -> p i h d", i=2, h=HP)
                for o in range(2):
                    lo, hi = SLOT * o, SLOT * o + SLOT
                    ins = nc.scalar.copy(VB[u][lo:hi, :, :, (HD + 1) * o:(HD + 1) * o + HD], v[lo:hi])
                ins.then_inc(values_ready, 1)

            def attend_scalar(j, u, more):
                (j1, u1), (j2, u2) = following(j, u)
                n = j * 2 + u + 1
                if more > 0:
                    keys(j1, u1)
                act.wait_ge(attended1, n)
                results_by_chunks(nc.scalar.copy, u, 0).then_inc(low_ready, 1)
                if more > 1:
                    root(j2 * 2 + (u2 + TILES + 1), u2, var_ready, dev_ready)
                if more > 1:
                    copy_turned(j2 * 2 + (u2 + TILES + 1), nt[u2], bank(u2, 0), transposed, NT_ready)
                root(n, u, var3_ready, dev3_ready)
                if more > 0:
                    exponentials(j1 * 2 + (u1 + TILES + 1), u1, exped1)
                    values(j1, u1)
                root(n + TILES, u, var2_ready, dev2_ready)
                if more > 0:
                    copy_probs(n + (TILES + 1), u1)
                other = bank(1 - u, 1)
                act.wait_ge(n3_split, n)
                copy_turned(n + TILES, cxt[u], other, transposed2, NT2_ready)
                rows = CXT[u][:].rearrange("p k (i q) -> p k i q", i=2)
                act.wait_ge(NT2_ready, n + TILES)
                for f in range(KD):
                    nc.scalar.copy(N3_high[:, f, bass.ds(j * (2 * PAIR) + PAIR * u, PAIR)].rearrange(
                        "p (i q) -> p i q", i=2), rows[:, f, :, 0:S])
                act.wait_ge(logits_ready, n)
                nc.scalar.copy(logits1[:, bass.ds(j * 2 + u, 1), :].rearrange("p o e -> p (o e)"),
                               other[:, D:D + E1]).then_inc(logits_copied, 1)

            for u in range(2):
                root(u + TILES + 1, u, var_ready, dev_ready)
            for u in range(2):
                copy_turned(u + TILES + 1, nt[u], bank(u, 0), transposed, NT_ready)
            act.sem_inc(logits_copied, 1)
            keys(FIRST, 0)
            exponentials(TILES + 1, 0, exped1)
            values(FIRST, 0)
            copy_probs(TILES + 1, 0)
            with act.Fori(0, TILES // 2 - 1) as i:
                nc.scalar.activation(table_of[:], cols("eps"), ACT.Sqrt)
                for u in range(2):
                    attend_scalar(i, u, 2)
            attend_scalar(TILES // 2 - 1, 0, 1)
            attend_scalar(TILES // 2 - 1, 1, 0)
            act.wait_ge(logits_copied, TILES + 1)
            nc.scalar.activation(sig1[:], logits1[:], ACT.Sigmoid).then_inc(sig_ready, 1)
            for b in range(4, 8):
                ins = nc.scalar.copy(psum[:, b, :], zeros[:, 0:psum.shape[2]])
            ins.then_inc(sums_cleared, 1)

            def hidden_high(n, h):
                act.wait_ge(product1_ready, n + 1)
                nc.scalar.copy(hid1_high[h][:].rearrange("p t i q -> p (t i) q")[:, :, 0:S],
                               silu1[h][:].rearrange("p (m q) -> p m q", q=S)).then_inc(high1_ready, 1)

            def gate_silu(n, h):
                act.wait_ge(gu1_ready, n + 1)
                nc.scalar.activation(silu1[h][:], psum[:, 2 * h, 0:HALF], ACT.Silu).then_inc(silu1_ready, 1)

            for h in range(2):
                gate_silu(h, h)
                hidden_high(h, h)
            with act.Fori(0, E1 // 2) as i:
                for j in range(2):
                    for h in range(2):
                        n = i * 4 + (2 + 2 * j + h)
                        act.wait_ge(hid1_ready, n - 1)
                        gate_silu(n, h)
                        act.wait_ge(down1_done, n - 1)
                        hidden_high(n, h)

        @block.gpsimd
        def _(pool):
            for u in range(2):
                nc.gpsimd.memset(sums[u][:], 0.0)
            nc.gpsimd.memset(zeros[:], 0.0).then_inc(pool_step, 1)
            pool.wait_ge(pool_step, 1)
            for x in hid1_high + hid1_low:
                ins = nc.gpsimd.tensor_copy(x[:].rearrange("p t i q -> p (t i q)"), zeros[:, 0:HT * P])
            ins.then_inc(pool_setup, 1)
            pool.wait_ge(small_loaded, 16 * len(early))
            span = zeros.shape[1]
            half = E0 * CAP // 2
            reps = half * ROW // P // span
            for u in range(2):
                dst = table[half * u:half * (u + 1), :].rearrange("(p r) x -> p (r x)", p=P)
                pool.dma_start(dst.rearrange("p (a b) -> p a b", b=span), spread(zeros[:], reps)).then_inc(scattered[u], 16)
            for c in range(CT):
                top_rows = ACC_ROWS // P * P
                pool.dma_start(acc[c][0:top_rows, :].rearrange("(p r) f -> p r f", p=P),
                               spread(zeros[:, 0:D], top_rows // P)).then_inc(added[c], 16)
                pool.dma_start(acc[c][top_rows:ACC_ROWS, :], zeros[0:ACC_ROWS - top_rows, 0:D]).then_inc(added[c], 16)
            for u in range(2):
                pool.wait_ge(scattered[u], 16)

            def add_bias(j, u):
                pool.wait_ge(normed, j * 2 + u + 1)
                nc.gpsimd.tensor_tensor(tile_of(j * 2 + u), tile_of(j * 2 + u), bo[:], ALU.add).then_inc(bias_added, 1)

            def scatter(j, u):
                pool.wait_ge(slots_ready, j * 2 + u + 1)
                pool.sem_inc(passed, 1)
                for c in range(TOP0):
                    pool.indirect_dma_start(table, bass.IndirectOffsetOnAxis(ap=slot[u][:, c:c + 1], axis=0),
                                            row[u][:], None, bounds_check=E0 * CAP - 1,
                                            oob_is_err=False).then_inc(scattered[u], 16)

            for u in range(2):
                add_bias(FIRST, u)
            with pool.Fori(0, TILES // 2 - 1) as i:
                for u in range(2):
                    add_bias(i + 1, u)
                    scatter(i, u)
            for u in range(2):
                scatter(TILES // 2 - 1, u)
            def low_weights(e, u):
                pool.wait_ge(gu_high_ready, e + 1)
                split_half(nc.gpsimd, u, 1).then_inc(gu_low_pool, 1)

            def add_results(e, i, u):
                pool.wait_ge(y_ready, e + 3)
                for c in range(CT):
                    pool.wait_ge(added[c], i * 32 + (16 * u + 32))
                    pool.sem_inc(passed, 1)
                    pool.indirect_dma_start(acc[c], bass.IndirectOffsetOnAxis(ap=dest[u][:, c:c + 1], axis=0),
                                            y_rows[u][:, c, :], None, bounds_check=ACC_ROWS - 1,
                                            compute_op=ALU.add, oob_is_err=True).then_inc(added[c], 16)

            for e in range(3):
                low_weights(e, e % 2)
            with pool.Fori(0, E0 // 2 - 2) as i:
                for u in range(2):
                    low_weights(i * 2 + u + 3, 1 - u)
                    add_results(i * 2 + u, i, u)
            low_weights(E0 - 1, 1)
            for e in range(E0 - 4, E0):
                add_results(e, e // 2, e % 2)
            pool.wait_ge(late_loaded, 16 * len(late))

            def add_sums(j, u):
                pool.wait_ge(sums_loaded[u], j * (32 * CT) + 32 * CT)
                t = j * 2 + u
                nc.gpsimd.tensor_tensor(sums[u][:, 0, :], sums[u][:, 0, :], sums[u][:, 1, :], ALU.add
                                        ).then_inc(pool_step, 1)
                pool.wait_ge(pool_step, t + 2)
                nc.gpsimd.tensor_tensor(tile_of(t), tile_of(t), sums[u][:, 0, :], ALU.add).then_inc(summed, 1)

            def add_residual(j, u):
                t = j * 2 + u
                pool.wait_ge(normed, t + (TILES + 1))
                pool.wait_ge(normed2, t + (TILES - 1))
                nc.gpsimd.tensor_tensor(residual[u][:], N[u][:], bo1[:], ALU.add)
                nc.gpsimd.tensor_tensor(tile_of(t), tile_of(t), beta[:], ALU.add).then_inc(residual_ready, 1)

            def split_rows(j, u):
                n = j * 2 + u + 1
                pool.wait_ge(logits_copied, n + 1)
                at = bass.ds(j * (2 * PAIR) + PAIR * u, PAIR)
                for f in range(KD):
                    ins = nc.gpsimd.tensor_tensor(N3_low[:, f, at].rearrange("p (i q) -> p i q", i=2),
                                                  CXT[u][:, f, :].rearrange("p (i q) -> p i q", i=2)[:, :, 0:S],
                                                  N3_high[:, f, at].rearrange("p (i q) -> p i q", i=2).bitcast(F32),
                                                  ALU.subtract)
                ins.then_inc(n3_split, 1)

            def split_part(n, u, lo, hi, step, done):
                high, low = (x[u][:, lo:hi] for x in (w1_high, w1_low))
                pool.sem_inc(passed, 1)
                nc.gpsimd.tensor_copy(high, w1[u][:, lo:hi]).then_inc(high_step, 1)
                pool.wait_ge(high_step, n * 2 + step)
                nc.gpsimd.tensor_tensor(low, w1[u][:, lo:hi], high.bitcast(F32), ALU.subtract).then_inc(done, 1)

            def split_weights(n, i, u, before):
                pool.wait_ge(w1_loaded[u], i * 16 + 16)
                if before:
                    pool.wait_ge(gu1_ready, n * 2 - 2)
                split_part(n, u, 0, KD * 2 * I1, 1, gate1_split)
                if before:
                    pool.wait_ge(down1_done, n * 2 - 2)
                split_part(n, u, KD * 2 * I1, NW, 2, down1_split)

            pool.sem_inc(n3_split, 2)
            for u in range(2):
                add_sums(FIRST, u)
            add_residual(FIRST, 0)
            with pool.Fori(0, TILES // 2 - 1) as i:
                for u in range(2):
                    (j1, u1), (j2, u2) = following(i, u)
                    add_sums(j2, u2)
                    add_residual(j1, u1)
                    split_rows(i, u)
            add_residual(TILES // 2 - 1, 1)
            for u in range(2):
                split_weights(u, 0, u, False)
            for u in range(2):
                split_rows(TILES // 2 - 1, u)
            with pool.Fori(0, (E1 - 2) // 2) as i:
                for u in range(2):
                    split_weights(i * 2 + u + 2, i + 1, u, True)
            split_weights(E1, E1 // 2, 0, True)

        def product(dst, terms):
            for n, (a, b) in enumerate(terms):
                mm = nc.tensor.matmul(dst, a, b, start=(n == 0), stop=(n == len(terms) - 1))
            return mm

        def three(high, low, x_high, x_low):
            return [(high, x_high), (high, x_low), (low, x_high)]

        def turn_tile(pe, n, u, src, dst, ready, done):
            pe.wait_ge(ready, n)
            for g in range(KD):
                mm = nc.tensor.transpose(dst[:, g * P:(g + 1) * P], src[:, g * P:(g + 1) * P], cols("ident"))
            mm.then_inc(done, 1)

        def turn_probs(pe, n, u, ready):
            pe.wait_ge(ready, n)
            for hp in range(HP):
                mm = nc.tensor.transpose(scores(u)[:, hp // 4, (hp % 4) * P:(hp % 4 + 1) * P],
                                         PR[u][:, 2 * hp:2 * hp + 2, :].rearrange("p h q -> p (h q)"), cols("ident"))
            mm.then_inc(prt_psum, 1)

        @block.tensor
        def _(pe):
            pe.wait_ge(first_loaded, 16 * len(first))
            pe.wait_ge(vec_setup, 1)

            def embed(j, u):
                pe.wait_ge(patches_loaded[u], j * 16 + 16)
                if j is not FIRST:
                    pe.wait_ge(vb_ready, j * 2 + (u - 1))
                product(bank(u, 0)[:, 0:D], [(patches[u][:, kp, :], tok_w[:, kp, :]) for kp in range(KP)]
                        ).then_inc(embedded, 1)

            def queries_and_keys(j, u, half):
                pe.wait_ge(NT_ready, j * 2 + u + 1)
                tokens = [NT[u][:, f, :].rearrange("p (i q) -> p i q", i=2)[:, :, 0:S] for f in range(KD)]
                for m in range(4):
                    c = (4 * half + m) * P
                    mm = product(bank(u, 2 + half)[:, m * PAIR:(m + 1) * PAIR].rearrange("p (i q) -> p i q", i=2),
                                 [(wqk[:, f, c:c + P], tokens[f]) for f in range(KD)])
                if half == 1:
                    mm.then_inc(qk_ready, 1)

            def values(j, u):
                product(bank(u, 0)[:, 0:D], [(NT[u][:, f, :], wv[:, f, :]) for f in range(KD)]).then_inc(v_ready, 1)

            def score(j, u):
                pe.wait_ge(kb_ready, j * 2 + u + 1)
                for g in range(KD):
                    for im in range(2):
                        mm = product(scores(u)[SLOT * im:SLOT * im + SLOT, g, 0:HG * S],
                                     [(QK[u][:, g, im, :], KB[u][:, 2 * g + im, :, :].rearrange("p h q -> p (h q)"))])
                mm.then_inc(scored, 1)

            def first_tensor(j, u, more):
                (j1, u1), (j2, u2) = following(j, u)
                n = j * 2 + u + 1
                pe.wait_ge(prt_ready, n)
                pe.wait_ge(vb_ready, n)
                for hp in range(HP):
                    for im in range(2):
                        mm = product(bank(u, 1)[SLOT * im:SLOT * im + SLOT, hp * VW:(hp + 1) * VW],
                                     [(PRT[u][:, hp, SLOT * im:SLOT * im + SLOT], VB[u][:, im, hp, :])])
                mm.then_inc(attended, 1)
                turn_tile(pe, n, u, CX[u][:].rearrange("p h d -> p (h d)"), bank(u, 0), cx_ready, cx_transposed)
                pe.wait_ge(cxt_ready, n)
                if more > 1:
                    turn_tile(pe, j2 * 2 + u2 + 1, u2, N[u2], bank(u2, 0)[:, D:2 * D], normed, transposed)
                product(bank(u, 1)[:, 0:D], [(CXT[u][:, g, :], wo[:, g, :]) for g in range(KD)]).then_inc(projected, 1)
                if more > 0:
                    score(j1, u1)
                if more > 1:
                    queries_and_keys(j2, u2, 0)
                turn_tile(pe, n, u, row[u], bank(u, 1), normed2, transposed2)
                if more > 1:
                    queries_and_keys(j2, u2, 1)
                pe.wait_ge(NT2_ready, n)
                product(bank(u, 1)[:, D:D + E0], [(CXT[u][:, f, :], gate_w[:, f, :]) for f in range(KD)]
                        ).then_inc(routed, 1)
                if more > 1:
                    values(j2, u2)
                if more > 0:
                    turn_probs(pe, j1 * 2 + u1 + 1, u1, exped)
                if more > 2:
                    embed(*((j1 + 1, u1)))
                pe.wait_ge(mask_ready, n)
                pe.wait_ge(taken_ready, n)
                product(bank(u, 1)[:, D + E0:D + 2 * E0],
                        [(count_earlier[:], r_mask[u][:]), (count_valid[:], taken[:])]).then_inc(counted, 1)

            for u in range(2):
                embed(FIRST, u)
            turn_tile(pe, 1, 0, N[0], bank(0, 0)[:, D:2 * D], normed, transposed)
            turn_tile(pe, 2, 1, N[1], bank(1, 0)[:, D:2 * D], normed, transposed)
            pe.wait_ge(small_loaded, 16 * len(early))
            for u in range(2):
                for half in range(2):
                    queries_and_keys(FIRST, u, half)
                values(FIRST, u)
            score(FIRST, 0)
            turn_probs(pe, 1, 0, exped)
            embed(1, 0)
            with pe.Fori(0, TILES // 2 - 2) as i:
                for u in range(2):
                    first_tensor(i, u, 3)
            for t in range(TILES - 4, TILES):
                first_tensor(t // 2, t % 2, TILES - 1 - t)

            def turn_rows(i, u):
                pe.wait_ge(rows_loaded[u], i * 16 + 16)
                for f in range(KD):
                    for c in range(CT):
                        mm = nc.tensor.transpose(bank(u, 0)[:, f * CAP + c * P:f * CAP + (c + 1) * P],
                                                 xrows[u][:, c, f * P:(f + 1) * P], cols("ident"))
                mm.then_inc(rows_transposed, 1)

            def expert_gate_up(e, i, u):
                for split in (x_split, gu_low_vec, gu_low_pool):
                    pe.wait_ge(split, e + 1)
                for b, c, m in ((1, 0, 0), (1, CAP, 2 * P), (2, 0, P)):
                    terms = []
                    for f in range(KD):
                        ws, xs = slice(f * 2 * F0 + m, f * 2 * F0 + m + P), slice(f * CAP, (f + 1) * CAP)
                        terms += three(gu_high[u][:, ws], gu_low[u][:, ws], xT_high[u][:, xs], xT_low[u][:, xs])
                    mm = product(bank(u, b)[:, c:c + CAP], terms)
                mm.then_inc(gu_ready, 1)

            def expert_down(e, i, u):
                pe.wait_ge(dn_loaded[u], i * 32 + 32)
                pe.wait_ge(hid_ready, e + 1)
                pe.wait_ge(y_ready, e + 1)
                for c in range(CT):
                    mm = product(bank(u, 3)[:, c * D:(c + 1) * D],
                                 [(hid_a[u][:, c * P:(c + 1) * P], dn_w[u][:, 0, :]),
                                  (hid_b[u][P - F0B:P, c * P:(c + 1) * P], dn_w[u][P - F0B:P, 1, :])])
                mm.then_inc(down_ready, 1)

            turn_rows(0, 0)
            expert_gate_up(0, 0, 0)
            turn_rows(0, 1)
            with pe.Fori(0, E0 // 2 - 1) as i:
                for e, now, at in ((i * 2 + 1, 1, i), (i * 2 + 2, 0, i + 1)):
                    expert_gate_up(e, at, now)
                    turn_rows(i + 1, 1 - now)
                    expert_down(e - 1, i, 1 - now)
            expert_gate_up(E0 - 1, E0 // 2 - 1, 1)
            expert_down(E0 - 2, E0 // 2 - 1, 0)
            expert_down(E0 - 1, E0 // 2 - 1, 1)
            pe.wait_ge(late_loaded, 16 * len(late))
            def qkv_by_chunks(j, u, chunks):
                pe.wait_ge(NT_ready, j * 2 + (u + TILES + 1))
                tokens = [NT[u][:, f, :].rearrange("p (i q) -> p i q", i=2)[:, :, 0:S] for f in range(KD)]
                for c in chunks:
                    at = c % CG * PAIR
                    mm = product(bank(u, c // CG)[0:QKV_ROWS, at:at + PAIR].rearrange("p (i q) -> p i q", i=2),
                                 [(wqkv1[:, f, c, :], tokens[f]) for f in range(KD)])
                return mm

            def turn_values(j, u, im):
                pe.wait_ge(qkv_ready, j * 2 + u + 1)
                pe.sem_inc(passed, 1)
                for h in range(HEADS):
                    lo, at = SLOT * (h % 2), (im * HEADS + h) * S
                    mm = product(bank(u, 0)[lo:lo + SLOT, (im * HP + h // 2) * HD:(im * HP + h // 2 + 1) * HD],
                                 [(positions[u][SLOT:SLOT + HD, at:at + SLOT],
                                   cols("ident")[SLOT:SLOT + HD, SLOT:SLOT + HD])])
                if im == 1:
                    mm.then_inc(values_turned, 1)

            def score_long(j, u):
                pe.wait_ge(keys_ready, j * 2 + u + 1)
                pe.sem_inc(passed, 1)
                for im in range(2):
                    for h in range(HEADS):
                        at = (im * HEADS + h) * S
                        mm = product(scores(u)[SLOT * im:SLOT * im + SLOT, h // HG, h % HG * S:(h % HG + 1) * S],
                                     [(positions[u][0:HD, at:at + SLOT], KP1[u][0:HD, at:at + S])])
                mm.then_inc(scored, 1)

            def attend_tensor(j, u, more):
                (j1, u1), (j2, u2) = following(j, u)
                n = j * 2 + u + 1
                pe.wait_ge(prt_ready, n + TILES)
                pe.wait_ge(values_ready, n)
                pe.sem_inc(passed, 1)
                for g in reversed(range(KD)):
                    if g == 0:
                        pe.wait_ge(logits_copied, n)
                    for im in range(2):
                        for h in range(HG * g, HG * g + HG):
                            mm = product(bank(u, 2 * g + im)[0:HD, h % HG * S:(h % HG + 1) * S],
                                         [(VB[u][:, im, h // 2, (HD + 1) * (h % 2):(HD + 1) * (h % 2) + HD],
                                           PRT[u][:, h // 2, SLOT * im:SLOT * im + S])])
                mm.then_inc(attended1, 1)
                if more > 0:
                    turn_values(j1, u1, 0)
                pe.wait_ge(low_ready, n)
                pe.wait_ge(high_ready, n)
                product(bank(u, 1)[:, 0:D], [(CT1[u][:, c, :], wo1[:, c, :]) for c in range(CG)]).then_inc(projected, 1)
                if more > 1:
                    turn_tile(pe, j2 * 2 + (u2 + TILES + 1), u2, N[u2], bank(u2, 0), normed, transposed)
                if more > 0:
                    score_long(j1, u1)
                    turn_values(j1, u1, 1)
                if more > 1:
                    qkv_by_chunks(j2, u2, range(CG))
                    pe.wait_ge(var3_ready, n)
                    qkv_by_chunks(j2, u2, range(CG, 3 * CG))
                if more > 0:
                    turn_probs(pe, j1 * 2 + u1 + 1, u1, probs_ready)
                if more > 1:
                    qkv_by_chunks(j2, u2, range(3 * CG, CH)).then_inc(qk_ready, 1)
                other = bank(1 - u, 1)
                turn_tile(pe, n + TILES, u, N3[u], other, normed2, transposed2)
                pe.wait_ge(NT2_ready, n + TILES)
                product(other[:, D:D + E1], [(CXT[u][:, f, :], router_w[:, f, :]) for f in range(KD)]
                        ).then_inc(logits_ready, 1)

            for u in range(2):
                turn_tile(pe, u + TILES + 1, u, N[u], bank(u, 0), normed, transposed)
            qkv_by_chunks(FIRST, 0, range(CH)).then_inc(qk_ready, 1)
            turn_values(FIRST, 0, 0)
            score_long(FIRST, 0)
            turn_values(FIRST, 0, 1)
            qkv_by_chunks(FIRST, 1, range(3 * CG))
            turn_probs(pe, 1, 0, probs_ready)
            qkv_by_chunks(FIRST, 1, range(3 * CG, CH)).then_inc(qk_ready, 1)
            with pe.Fori(0, TILES // 2 - 1) as i:
                for u in range(2):
                    attend_tensor(i, u, 2)
            attend_tensor(TILES // 2 - 1, 0, 1)
            attend_tensor(TILES // 2 - 1, 1, 0)
            pe.wait_ge(pool_setup, 1)
            def gate_up(buf, h):
                cs = slice(h * HALF, (h + 1) * HALF)
                for m in range(2):
                    terms = []
                    for f in range(KD):
                        ws = slice(f * 2 * I1 + m * I1, f * 2 * I1 + (m + 1) * I1)
                        terms += three(w1_high[buf][:, ws], w1_low[buf][:, ws], N3_high[:, f, cs], N3_low[:, f, cs])
                    mm = product(psum[:, 2 * h + m, 0:HALF], terms)
                mm.then_inc(gu1_ready, 1)

            def down(buf, h):
                w_high, w_low = (x[buf][:, KD * 2 * I1:NW] for x in (w1_high, w1_low))
                for t in range(HT):
                    at = h * HT + t
                    x_high, x_low = (x[:, t, :, :].rearrange("p i q -> p (i q)") for x in (hid1_high[h], hid1_low[h]))
                    for a, b in three(x_high, x_low, w_high, w_low):
                        mm = nc.tensor.matmul(psum[:, 4 + at // 2, (at % 2) * D:(at % 2 + 1) * D], a, b,
                                              start=False, stop=True, skip_group_check=True)
                mm.then_inc(down1_done, 1)

            pe.wait_ge(down1_split, 1)
            pe.wait_ge(n3_split, TILES + 2)
            pe.wait_ge(logits_copied, TILES + 1)
            gate_up(0, 0)
            gate_up(0, 1)
            pe.wait_ge(hid1_ready, 1)
            pe.wait_ge(comb_ready, 1)
            nc.tensor.transpose(psum[0:E1 * TILES, 0, 0:P], comb1[:].rearrange("p e t -> p (e t)"), cols("ident")
                                ).then_inc(comb_turned, 1)
            pe.wait_ge(sums_cleared, 1)
            down(0, 0)
            pe.wait_ge(comb_copied, 1)
            with pe.Fori(0, E1 // 2) as i:
                for j, buf in ((0, 1), (1, 0)):
                    n = i * 4 + (2 + 2 * j)
                    pe.wait_ge(down1_split, i * 2 + (j + 2))
                    gate_up(buf, 0)
                    pe.wait_ge(hid1_ready, n)
                    down(1 - buf, 1)
                    gate_up(buf, 1)
                    pe.wait_ge(hid1_ready, n + 1)
                    down(buf, 0)
            pe.wait_ge(hid1_ready, 2 * (E1 + 1))
            down(0, 1)


_OUT = (IMAGES, S, D)


def _layout(a):
    def k_rows(w):
        return np.ascontiguousarray(w.reshape(w.shape[0] // P, P, -1).transpose(1, 0, 2))

    def by_chunks(q, k, v):
        w = np.zeros((q.shape[0], CH, QKV_ROWS), np.float32)
        for n, x in enumerate((q, k, v)):
            w[:, :, 32 * n:32 * n + HD] = x.reshape(-1, CH, HD)
        return w

    x = a["x"].reshape(TILES, 2, 3, 7, 16, 7, 16).transpose(0, 2, 4, 6, 1, 3, 5).reshape(TILES, KP, P, 2, S)
    patches = np.zeros((TILES, KP, P, 2, SLOT), np.float32)
    patches[..., :S] = x
    wqkv, bqkv = a["L0_attn_w_qkv"], a["L0_attn_b_qkv"]
    swap = np.arange(2 * D) ^ 1
    wqk = np.concatenate([wqkv[:2 * D], wqkv[:2 * D][swap]], axis=0).T
    rope_b = np.concatenate([bqkv[:2 * D], bqkv[:2 * D][swap]]).reshape(8, P).T
    order = np.concatenate([np.arange(P), np.arange(P, F0), np.arange(F0 + P, 2 * F0), np.arange(F0, F0 + P)])
    gu = a["L0_ffn_gate_up_proj"][:, order, :].transpose(0, 2, 1).reshape(E0, KD, P, 2 * F0).transpose(0, 2, 1, 3)
    wo1 = np.zeros((4, 32, CG, D), np.float32)
    wo1[:, :HD] = a["L1_attn_wo"].reshape(4, CG, HD, D).transpose(0, 2, 1, 3)
    gate = np.concatenate([a["L1_ffn_sw_gate"][None], a["L1_ffn_w_gate"]])
    up = np.concatenate([a["L1_ffn_sw_up"][None], a["L1_ffn_w_up"]])
    gu1 = np.concatenate([gate, up], axis=2).reshape(E1 + 1, KD, P, 2 * I1).transpose(0, 2, 1, 3)
    down1 = np.concatenate([a["L1_ffn_sw_down"][None], a["L1_ffn_w_down"]])
    return {
        "const": constants(),
        "patches": patches.transpose(0, 2, 1, 3, 4).reshape(TILES, P, KP, 2 * SLOT),
        "tok_w": k_rows(a["L0_tok_W"]), "tok_b": a["L0_tok_b"],
        "wqk": k_rows(wqk), "rope_b": rope_b,
        "wv": k_rows(wqkv[2 * D:].T), "bv": bqkv[2 * D:],
        "wo": k_rows(a["L0_attn_w_out"].T), "bo": a["L0_attn_b_out"],
        "gate_w": k_rows(a["L0_ffn_gate_weight"].T),
        "gu_w": gu, "dn_w": a["L0_ffn_down_proj"].transpose(0, 2, 1),
        "wqkv1": k_rows(by_chunks(a["L1_attn_wq"], a["L1_attn_wk"], a["L1_attn_wv"])).reshape(P, KD, CH, QKV_ROWS),
        "bqkv1": by_chunks(*(a[n][None] for n in ("L1_attn_bq", "L1_attn_bk", "L1_attn_bv")))[0].T,
        "wo1": wo1.reshape(P, CG, D), "bo1": a["L1_attn_bo"],
        "gamma": a["L1_attn_gamma"], "beta": a["L1_attn_beta"],
        "router_w": k_rows(a["L1_ffn_router_weight"].T), "corr": a["L1_ffn_correction_bias"],
        "w1": np.concatenate([gu1.reshape(E1 + 1, P, -1), down1], axis=2),
    }


def kernel(**inputs):
    import concourse.bacc as bacc
    from concourse.bass_utils import run_bass_kernel_spmd

    nc = bacc.Bacc("TRN2", target_bir_lowering=False, num_devices=1)
    laid = {n: np.ascontiguousarray(v) for n, v in _layout({n: np.asarray(v) for n, v in inputs.items()}).items()}
    arrays = {f"in_{n}": v for n, v in laid.items()}
    dram = {n: nc.dram_tensor(f"in_{n}", list(v.shape), F32, kind="ExternalInput").ap() for n, v in laid.items()}
    out = nc.dram_tensor("out_0", list(_OUT), F32, kind="ExternalOutput").ap()
    vit_tower(nc, dram, out)
    r = run_bass_kernel_spmd(nc, [arrays], core_ids=[0])
    return r.results[0]["out_0"]
```
